# Optimizing a Trainium2 kernel written in Bass

```python
import numpy as np
import jax
import jax.numpy as jnp

def _softmax(x, axis=-1):
    return jax.nn.softmax(x, axis=axis)

def _gelu(x):
    return jax.nn.gelu(x, approximate=True)

def _silu(x):
    return jax.nn.silu(x)

def _sigmoid(x):
    return jax.nn.sigmoid(x)

def _layernorm(x, axis=-1, eps=1e-05):
    m = jnp.mean(x, axis=axis, keepdims=True)
    v = jnp.var(x, axis=axis, keepdims=True)
    return (x - m) / jnp.sqrt(v + eps)

def _scatter_add(tgt, idx, src, axis=0):
    return tgt.at[idx].add(src)

def _segment_sum(src, seg, n):
    return jax.ops.segment_sum(src, seg, n)
kernel_name = 'mk_decoder_preln_d1_seqx_r8_bbc4b0'

def setup_inputs(seed: int=0):
    np.random.seed(seed)
    _w = jnp.asarray

    def _rec_inputs():
        import jax
        import jax.numpy as jnp
        _rk = jax.random.key(seed)
        x = 7.22e-05 + 1 * jax.random.normal(jax.random.fold_in(_rk, 1), (4, 256, 256), jnp.float32)
        _lenS = 256 - jax.random.randint(jax.random.fold_in(_rk, 7), (4,), 0, max(1, 256 // 4) + 1, jnp.int32)
        _lenS2 = 256 - jax.random.randint(jax.random.fold_in(_rk, 8), (4,), 0, max(1, 256 // 4) + 1, jnp.int32)
        _ctx_2048P = jax.random.normal(jax.random.fold_in(_rk, 11), (4, 16, 256), jnp.float32)
        _ctx_2048c = jax.random.dirichlet(jax.random.fold_in(_rk, 511), 0.3 * jnp.ones((16,), jnp.float32), (4, 256))
        _ctx_2048t = jnp.einsum('bsk,bkd->bsd', _ctx_2048c, _ctx_2048P)
        _ctx_2048t = _ctx_2048t * jax.lax.rsqrt(jnp.mean(jnp.square(_ctx_2048t)) + 1e-12) * 0.953939
        ctx_2048 = 4.13588e-05 + 0.999923 * (_ctx_2048t + 0.3 * jax.random.normal(jax.random.fold_in(_rk, 611), (4, 256, 256), jnp.float32))
        return (x, ctx_2048)
    x, ctx_2048 = _rec_inputs()

    def _L0_attn_setup():
        import jax, jax.numpy as jnp
        import numpy as np
        B, S, QD = (2, 512, 256)
        H, D = (32, 64)
        INNER = H * D
        key = jax.random.key(seed)
        ks = jax.random.split(key, 6)
        scale = 1.0 / np.sqrt(QD)
        return {'hidden_states': jax.random.normal(ks[0], (B, S, QD), dtype=jnp.float32), 'Wq': jax.random.normal(ks[1], (QD, INNER), dtype=jnp.float32) * scale, 'Wk': jax.random.normal(ks[2], (QD, INNER), dtype=jnp.float32) * scale, 'Wv': jax.random.normal(ks[3], (QD, INNER), dtype=jnp.float32) * scale, 'Wo': jax.random.normal(ks[4], (INNER, QD), dtype=jnp.float32) * (1.0 / np.sqrt(INNER)), 'bo': jax.random.normal(ks[5], (QD,), dtype=jnp.float32) * 0.01}
    _L0_attn_all = _L0_attn_setup()
    _L0_attn_in = {k: v for k, v in _L0_attn_all.items() if k in ('Wq', 'Wk', 'Wv', 'Wo', 'bo')}
    del _L0_attn_all

    def _L0_xattn_setup():
        import jax, jax.numpy as jnp
        import numpy as np
        N_HEAD = 8
        key = jax.random.key(seed)
        k1, k2, k3 = jax.random.split(key, 3)
        b, d, m = (4, 128, 256)
        c, n = (128, 256)
        q = jax.random.normal(k1, (b, d, m), dtype=jnp.float32)
        k = jax.random.normal(k2, (d // d * b, d, n), dtype=jnp.float32).reshape(b, d, n)
        v = jax.random.normal(k3, (b, c, n), dtype=jnp.float32)
        return {'q': q, 'k': k, 'v': v}
    _L0_xattn_all = _L0_xattn_setup()
    _L0_xattn_in = {k: v for k, v in _L0_xattn_all.items() if k in ()}
    del _L0_xattn_all

    def _L0_ffn_setup():
        import jax, jax.numpy as jnp
        import numpy as np
        TOP_K = 6
        N_GROUP = 8
        TOPK_GROUP = 3
        CAPACITY = 96
        RSF = 1.0
        key = jax.random.key(seed)
        ks = jax.random.split(key, 8)
        B, S, H = (1, 512, 256)
        E, M = (64, 176)
        MS = 352
        sc = 0.02
        return {'hidden_states': jax.random.normal(ks[0], (B, S, H), jnp.float32), 'gate_weight': jax.random.normal(ks[1], (E, H), jnp.float32) * sc, 'Wg': jax.random.normal(ks[2], (E, M, H), jnp.float32) * sc, 'Wu': jax.random.normal(ks[3], (E, M, H), jnp.float32) * sc, 'Wd': jax.random.normal(ks[4], (E, H, M), jnp.float32) * sc, 'Sg': jax.random.normal(ks[5], (MS, H), jnp.float32) * sc, 'Su': jax.random.normal(ks[6], (MS, H), jnp.float32) * sc, 'Sd': jax.random.normal(ks[7], (H, MS), jnp.float32) * sc}
    _L0_ffn_all = _L0_ffn_setup()
    _L0_ffn_in = {k: v for k, v in _L0_ffn_all.items() if k in ('gate_weight', 'Wg', 'Wu', 'Wd', 'Sg', 'Su', 'Sd')}
    del _L0_ffn_all
    return {'x': x, 'ctx_2048': ctx_2048, 'L0_attn_Wq': _L0_attn_in['Wq'], 'L0_attn_Wk': _L0_attn_in['Wk'], 'L0_attn_Wv': _L0_attn_in['Wv'], 'L0_attn_Wo': _L0_attn_in['Wo'], 'L0_attn_bo': _L0_attn_in['bo'], 'L0_ffn_gate_weight': _L0_ffn_in['gate_weight'], 'L0_ffn_Wg': _L0_ffn_in['Wg'], 'L0_ffn_Wu': _L0_ffn_in['Wu'], 'L0_ffn_Wd': _L0_ffn_in['Wd'], 'L0_ffn_Sg': _L0_ffn_in['Sg'], 'L0_ffn_Su': _L0_ffn_in['Su'], 'L0_ffn_Sd': _L0_ffn_in['Sd']}

def reference(x, ctx_2048, L0_attn_Wq, L0_attn_Wk, L0_attn_Wv, L0_attn_Wo, L0_attn_bo, L0_ffn_gate_weight, L0_ffn_Wg, L0_ffn_Wu, L0_ffn_Wd, L0_ffn_Sg, L0_ffn_Su, L0_ffn_Sd):
    import jax
    import jax.numpy as jnp

    def _L0_attn_ref(hidden_states, Wq, Wk, Wv, Wo, bo):
        import jax, jax.numpy as jnp
        import numpy as np
        B, S, QD = (2, 512, 256)
        H, D = (32, 64)
        INNER = H * D
        b, s, _ = hidden_states.shape

        def proj(W):
            return (hidden_states @ W).reshape(b, s, H, D).transpose(0, 2, 1, 3)
        q = jax.nn.relu(proj(Wq))
        k = jax.nn.relu(proj(Wk))
        v = proj(Wv)
        kv = jnp.einsum('bhsd,bhse->bhde', k, v)
        qkv = jnp.einsum('bhsd,bhde->bhse', q, kv)
        key_sum = k.sum(axis=2)
        normalizer = jnp.einsum('bhsd,bhd->bhs', q, key_sum)
        normalizer = jnp.clip(normalizer, 1e-06, None)[..., None]
        out = qkv / normalizer
        out = out.transpose(0, 2, 1, 3).reshape(b, s, INNER)
        return out @ Wo + bo

    def _L0_xattn_ref(q, k, v):
        import jax, jax.numpy as jnp
        import numpy as np
        N_HEAD = 8
        b, d, m = q.shape
        c = v.shape[1]
        h = N_HEAD
        qh = q.reshape(b * h, d // h, m)
        kh = k.reshape(b * h, d // h, -1)
        vh = v.reshape(b * h, c // h, -1)
        scale = 1.0 / jnp.sqrt(jnp.asarray(d // h, dtype=q.dtype))
        qk = jnp.einsum('bdm,bdn->bmn', qh, kh) * scale
        sm = jax.nn.softmax(qk, axis=-1)
        ret = jnp.einsum('bmn,bcn->bcm', sm, vh)
        return ret.reshape(b, c, m)

    def _L0_ffn_ref(hidden_states, gate_weight, Wg, Wu, Wd, Sg, Su, Sd):
        import jax, jax.numpy as jnp
        import numpy as np
        TOP_K = 6
        N_GROUP = 8
        TOPK_GROUP = 3
        CAPACITY = 96
        RSF = 1.0
        B, S, H = hidden_states.shape
        E, M, _ = Wg.shape
        K, NG, TG, C = (TOP_K, N_GROUP, TOPK_GROUP, CAPACITY)
        x = hidden_states.reshape(-1, H)
        T = x.shape[0]
        logits = x.astype(jnp.float32) @ gate_weight.astype(jnp.float32).T
        scores = jax.nn.softmax(logits, axis=-1)
        group_scores = scores.reshape(T, NG, E // NG).max(axis=-1)
        _, gidx = jax.lax.top_k(group_scores, TG)
        gmask = jnp.zeros((T, NG), scores.dtype).at[jnp.arange(T)[:, None], gidx].set(1.0)
        smask = jnp.repeat(gmask, E // NG, axis=1)
        tmp_scores = jnp.where(smask > 0, scores, 0.0)
        topk_w, topk_i = jax.lax.top_k(tmp_scores, K)
        topk_w = topk_w * RSF
        flat = topk_i.reshape(-1)
        oh = jax.nn.one_hot(flat, E, dtype=jnp.int32)
        pos = jnp.sum(jnp.cumsum(oh, axis=0) * oh, axis=-1) - 1
        slot = flat * C + jnp.minimum(pos, C - 1)
        tok = jnp.arange(T * K) // K
        buf = jnp.zeros((E * C, H), x.dtype).at[slot].set(x[tok]).reshape(E, C, H)
        g = jnp.einsum('ech,emh->ecm', buf, Wg)
        u = jnp.einsum('ech,emh->ecm', buf, Wu)
        out = jnp.einsum('ecm,ehm->ech', jax.nn.silu(g) * u, Wd).reshape(E * C, H)
        yk = out[slot].reshape(T, K, H)
        y = jnp.sum(yk * topk_w[..., None].astype(yk.dtype), axis=1)
        shared = jax.nn.silu(x @ Sg.T) * (x @ Su.T) @ Sd.T
        return (y + shared).reshape(B, S, H)
    x = x + _L0_attn_ref(_layernorm(x, axis=-1), L0_attn_Wq, L0_attn_Wk, L0_attn_Wv, L0_attn_Wo, L0_attn_bo)
    x = x + _L0_xattn_ref(_layernorm(x, axis=-1), ctx_2048, ctx_2048)
    x = x + _L0_ffn_ref(_layernorm(x, axis=-1), L0_ffn_gate_weight, L0_ffn_Wg, L0_ffn_Wu, L0_ffn_Wd, L0_ffn_Sg, L0_ffn_Su, L0_ffn_Sd)
    return x

_drawn_inputs = setup_inputs


def setup_inputs(seed=0):
    import zlib

    import numpy as np

    out = dict(_drawn_inputs(seed))
    spreads = {}
    factors = {'L0_ffn_gate_weight': 8.0,
     'L0_ffn_Wg': 8.0,
     'L0_ffn_Wu': 8.0,
     'L0_ffn_Wd': 8.0,
     'L0_ffn_Sg': 3.529,
     'L0_ffn_Su': 3.505,
     'L0_ffn_Sd': 3.505}
    for name, (base, spread) in spreads.items():
        noise = np.random.default_rng([zlib.crc32(name.encode()), seed]).standard_normal(out[name].shape)
        drawn = base * np.exp(spread * noise) if base else spread * noise
        out[name] = jnp.asarray(drawn.astype(out[name].dtype))
    for name, factor in factors.items():
        out[name] = (out[name] * factor).astype(out[name].dtype)
    return out
```

```python
from contextlib import ExitStack

import concourse.bass as bass
from concourse import mybir

ALU = mybir.AluOpType
ACT = mybir.ActivationFunctionType
AX = mybir.AxisListType
F32 = mybir.dt.float32
BF16 = mybir.dt.bfloat16
I32 = mybir.dt.int32
U32 = mybir.dt.uint32

P = 128
QUAD = 32
BANK = 512
EPS = 1e-5
FLOOR = 1e-6

B, S, D = 4, 256, 256
T = B * S
TILES = T // P
KT = D // P
INNER = 2048
HEAD = 64
GROUP = 512
GROUPS = INNER // GROUP
PAIRS = GROUP // P
TB = S // P
XH = 8
XD = D // XH
XSCALE = 1.0 / float(XD) ** 0.5
E = 64
NG = 8
TOPG = 3
TOPK = 6
CAP = 96
M = 176
MH = M // 2
MS = 352
MSP = MS // MH
RING = 4
PAD_E = E + RING
Y_ROWS = T * TOPK
VALS = 6


class Chain:

    def __init__(self, eng, sem):
        self.eng, self.sem, self.n, self.off = eng, sem, 0, None

    def link(self, ins):
        ins.then_inc(self.sem, 1)
        self.n += 1
        self.eng.wait_ge(self.sem, self.n if self.off is None else self.off + self.n)

    def enter(self, i, first, per):
        self.off, self.per = (i - first) * per, per

    def leave(self, turns):
        self.off = None
        self.n += (turns - 1) * self.per


def at_least(eng, sem, value):
    if not isinstance(value, int) or value > 0:
        eng.wait_ge(sem, value)


def one(t, i):
    if isinstance(i, int):
        return t[:, i, :]
    return t[:, bass.ds(i, 1), :].rearrange("p a n -> p (a n)")


def col(t, i):
    return t[:, i:i + 1] if isinstance(i, int) else t[:, bass.ds(i, 1)]


def decoder_layer(nc, x_in, ctx_in, wq_in, wk_in, wv_in, wo_in, bo_in, gate_in, wgu_in, wd_in, sgu_in, sd_in, out):
    ctx = ExitStack()
    with ctx:
        def sb(name, shape, dt=F32):
            return ctx.enter_context(nc.sbuf_tensor(name, shape, dt))

        def sem(name):
            return ctx.enter_context(nc.semaphore(name))

        def within(t, at, shape, partitions=P):
            names = "abcd"[:len(t.shape) - 1]
            flat = t[:, *[slice(None)] * len(names)].rearrange(f"p {' '.join(names)} -> p ({' '.join(names)})")
            size = 1
            for n in shape:
                size *= n
            part = flat[0:partitions, at:at + size]
            if len(shape) == 1:
                return part
            names = "abcd"[:len(shape)]
            return part.rearrange(f"p ({' '.join(names)}) -> p {' '.join(names)}", **dict(zip(names, shape)))

        h_rows = nc.dram_tensor("h_rows", (T, D), F32, kind="Internal").ap()
        y_rows = nc.dram_tensor("y_rows", (Y_ROWS + E, D), F32, kind="Internal").ap()

        ps = ctx.enter_context(nc.psum_tensor("ps", [P, 8, BANK], F32))

        ident = sb("ident", [P, P])
        ones_row = sb("ones_row", [1, P])
        ones_b = sb("ones_b", [P, P], BF16)
        before_b = sb("before_b", [P, P], BF16)
        iota_e = sb("iota_e", [P, E])
        iota_c = sb("iota_c", [P, CAP], BF16)
        zeros = sb("zeros", [P, TOPK * D // 2])
        slot_is_own = sb("slot_is_own", [CAP, 1])
        slot_is_last = sb("slot_is_last", [CAP, 1])
        dst_base = sb("dst_base", [CAP, PAD_E])
        eps_t = sb("eps_t", [P, 1])
        bo_row = sb("bo_row", [1, D])

        x_s = sb("x_s", [P, TILES, D])
        xn_s = sb("xn_s", [P, TILES, D])
        xnT = sb("xnT", [P, KT, T])
        stats = sb("stats", [P, TILES, 6])
        mv = sb("mv", [P, TILES, 2])
        std = sb("std", [P, TILES])
        rstd = sb("rstd", [P, TILES])

        wq_s = sb("wq_s", [P, KT, INNER])
        wk_s = sb("wk_s", [P, KT, INNER])
        wv_s = sb("wv_s", [P, KT, INNER])
        wo_s = sb("wo_s", [P, INNER // P, D])
        wq_g = sb("wq_g", [P, KT, GROUP])
        qT = sb("qT", [P, PAIRS, T])
        k_s = sb("k_s", [P, 2, TB, GROUP])
        v_s = sb("v_s", [P, 2, TB, PAIRS, P + 1])
        kv_s = sb("kv_s", [P, PAIRS, P])
        ks_s = sb("ks_s", [P, PAIRS, P])
        aT = sb("aT", [P, 2, PAIRS, S])

        nrm = sb("nrm", [P, S])

        ctx_s = sb("ctx_s", [P, B, KT * D])
        ctx_b = sb("ctx_b", [P, KT, D])
        q_b = within(qT, 0, [KT, D])
        vT_s = within(qT, KT * D, [KT, D])
        p_s = within(qT, 2 * KT * D, [RING, 2, D])
        pT_s = within(qT, 2 * KT * D + RING * 2 * D, [2, 2, D])
        mx = sb("mx", [P, RING, 2])
        nmx = sb("nmx", [P, RING, 2])
        psm = sb("psm", [P, RING, 2])
        prs = sb("prs", [P, RING, 2])

        gate_s = sb("gate_s", [P, KT, E])
        lg, sc, tmp, oh, rank1, mask, pos, ra = [within(wk_s, n * TILES * E, [TILES, E]) for n in range(8)]
        rb, w_te, w_over = [within(wq_s, n * TILES * E, [TILES, E]) for n in range(3)]
        mask_b = sb("mask_b", [P, TILES, E], BF16)
        cnt1 = sb("cnt1", [P, E])
        slot_of = sb("slot_of", [P, TILES, PAD_E])
        w_overT = sb("w_overT", [E, T])
        vals = sb("vals", [P, TILES, PAD_E, VALS], BF16)
        tmx = sb("tmx", [P, TILES])
        gsc = sb("gsc", [P, TILES, NG])
        g8 = sb("g8", [P, TILES, 8])
        gi8 = sb("gi8", [P, TILES, 8], U32)
        gif = sb("gif", [P, TILES, 8])
        gm = sb("gm", [P, TILES, NG])
        gt = sb("gt", [P, TILES, NG])
        v8 = sb("v8", [P, TILES, 8])
        i8 = sb("i8", [P, TILES, 8], U32)
        i8f = sb("i8f", [P, TILES, 8])

        sgu_s = sb("sgu_s", [P, KT, 2 * MS])
        sd_s = sb("sd_s", [MH, MSP, D])
        hT_j = sb("hT_j", [P, 2, KT, P])
        sh_s = within(wv_s, 0, [2, MS])
        sh_h = within(wv_s, 2 * MS, [2, MS])
        sh_T = within(wv_s, 4 * MS, [2, MSP, P], MH)

        wgu_s = sb("wgu_s", [P, RING, KT * 2 * M])
        wd_s = sb("wd_s", [MH, RING, 2 * D])
        ohs = within(wv_s, 4 * MS + 2 * MSP * P, [RING * TILES * CAP // 2]).bitcast(BF16).rearrange(
            "p (a b c) -> p a b c", a=RING, b=TILES)
        row_of = sb("row_of", [CAP, 1])
        dst_f = sb("dst_f", [CAP, PAD_E])
        src_now = sb("src_now", [CAP, RING], I32)
        dst_now = sb("dst_now", [CAP, RING], I32)
        w_sum = sb("w_sum", [CAP, 1])
        tab = sb("tab", [CAP, VALS])
        w_slot = sb("w_slot", [CAP, PAD_E])
        xe = within(k_s, 0, [RING, D], CAP)
        oe = within(k_s, RING * D, [RING, D], CAP)
        xeT = within(aT, 0, [2, KT, CAP])
        he_a = within(aT, 2 * KT * CAP, [2, M], CAP)
        he = within(aT, 2 * KT * CAP + 2 * M, [2, M], CAP)
        heT = within(aT, 2 * KT * CAP + 4 * M, [2, 2, CAP], MH)

        y_t = [within(wq_s, i * TOPK * D, [TOPK * D]) for i in range(2)]
        ysum = within(wq_s, 2 * TOPK * D, [2, D])
        over_s = within(wq_s, 2 * TOPK * D + 2 * D, [D], E)

        names = """x_loaded bo_loaded ctx_loaded gate_loaded sgu_loaded sd_loaded wq_loaded wk_loaded wv_loaded wo_loaded
            consts zeros_ready y_zeroed dve_step pool_step act_step
            var_ready std_ready xn_ready xT_made xT_moved bo_spread bo_added
            wq_staged projected proj_moved kv_made kv_laid heads_made heads_normed attn_made attn_added
            ctx_staged q_ready vT_made vT_moved s_made max_ready exp_done rcp_done p_normed t_made pT_moved av_made av_added
            h_stored logits_made lg_ready lg_exped mask_ready pos_made over_ready overT_made overT_moved
            hT_staged sh_gu_made sh_silu sh_mult shT_made shT_moved sh_made sh_added
            vals_ready oh_ready tab_made tab_moved xeT_made xeT_moved gu_made silu_done he_ready heT_made heT_moved
            oe_made oe_moved over_made out_ready out_stored over_loaded""".split()
        s = {n: sem(n) for n in names}
        wgu_loaded = [sem(f"wgu_loaded{i}") for i in range(RING)]
        wd_loaded = [sem(f"wd_loaded{i}") for i in range(RING)]
        gathered = [sem(f"gathered{i}") for i in range(RING)]
        scattered = [sem(f"scattered{i}") for i in range(RING)]
        y_loaded = [sem(f"y_loaded{i}") for i in range(2)]

        block = ctx.enter_context(nc.Block())
        TURNS = E // RING

        PJ = [0, 1, 2]
        KV = 3
        ON = [5, 6]
        AO = 7
        SB = [0, 1, 2, 3]
        TB_ = 4
        AV = [5, 6]
        VT = 7

        def projections():
            n = 0
            for what, b in (("q", 0), ("kv", 0), ("q", 1), ("kv", 1), ("kv", 2), ("kv", 3)):
                if what == "q":
                    rows = [("q", b, p) for p in range(PAIRS)]
                else:
                    rows = [("k", b, t) for t in range(TB)] + [("v", b, t) for t in range(TB)]
                for row in rows:
                    yield n, row
                    n += 1
        PROJ = list(projections())
        NPROJ = len(PROJ)
        V_DONE = {b: 1 + max(n for n, r in PROJ if r[0] == "v" and r[1] == b) for b in range(B)}
        Q_DONE = {h: 1 + max(n for n, r in PROJ if r[0] == "q" and r[1] == h) for h in range(2)}

        @block.sync
        def _(sp):
            for j in range(TILES):
                sp.dma_start(x_s[:, j, :], x_in[j * P:(j + 1) * P, :]).then_inc(s["x_loaded"], 16)
            sp.dma_start(bo_row[:, :], bo_in).then_inc(s["bo_loaded"], 16)
            for g in range(GROUPS):
                for name, dst, src in (("wq_loaded", wq_s, wq_in), ("wk_loaded", wk_s, wk_in), ("wv_loaded", wv_s, wv_in)):
                    at_least(sp, s[name], 16 * g)
                    sp.dma_start(dst[:, :, g * GROUP:(g + 1) * GROUP],
                                 src[:, g * GROUP:(g + 1) * GROUP].rearrange("(k p) n -> p k n", p=P)).then_inc(s[name], 16)
                at_least(sp, s["wo_loaded"], 16 * g)
                sp.dma_start(wo_s[:, g * PAIRS:(g + 1) * PAIRS, :],
                             wo_in[g * GROUP:(g + 1) * GROUP, :].rearrange("(k p) n -> p k n", p=P)).then_inc(s["wo_loaded"], 16)
            sp.dma_start(ctx_s[:, :, :].rearrange("p b (k n) -> p b k n", k=KT),
                         ctx_in.rearrange("b (k p) n -> p b k n", p=P)).then_inc(s["ctx_loaded"], 16)
            sp.dma_start(gate_s[:, :, :], gate_in).then_inc(s["gate_loaded"], 16)
            sp.dma_start(sgu_s[:, :, :], sgu_in).then_inc(s["sgu_loaded"], 16)
            sp.dma_start(sd_s[:, :, :], sd_in).then_inc(s["sd_loaded"], 16)
            sp.wait_ge(s["zeros_ready"], 1)
            for j in range(TILES):
                for i in range(2):
                    rows = P * TOPK // 2
                    sp.dma_start(y_rows[(2 * j + i) * rows:(2 * j + i + 1) * rows, :].rearrange("(p k) n -> p (k n)", p=P),
                                 zeros[:, :]).then_inc(s["y_zeroed"], 16)

            def load_expert(e, turn, i, before):
                if before:
                    sp.wait_ge(s["gu_made"], e - RING + 1)
                sp.dma_start(wgu_s[:, i, :], wgu_in[e] if isinstance(e, int) else
                             wgu_in[bass.ds(e, 1)].rearrange("a p n -> (a p) n")).then_inc(wgu_loaded[i], 16)
                if before:
                    sp.wait_ge(s["oe_made"], e - RING + 1)
                sp.dma_start(wd_s[:, i, :], wd_in[e] if isinstance(e, int) else
                             wd_in[bass.ds(e, 1)].rearrange("a p n -> (a p) n")).then_inc(wd_loaded[i], 16)

            for i in range(RING):
                load_expert(i, 0, i, False)
            sp.wait_ge(s["xn_ready"], 2)
            for j in range(TILES):
                sp.dma_start(h_rows[j * P:(j + 1) * P, :], xn_s[:, j, :]).then_inc(s["h_stored"], 16)
            with sp.Fori(1, TURNS) as r:
                for i in range(RING):
                    load_expert(r * RING + i, r, i, True)
            for i in range(RING):
                sp.wait_ge(scattered[i], 16 * TURNS)
            sp.dma_start(over_s, y_rows[Y_ROWS:Y_ROWS + E, :]).then_inc(s["over_loaded"], 16)
            for j in range(TILES):
                if j >= 2:
                    sp.wait_ge(s["out_ready"], j - 1)
                sp.dma_start(y_t[j % 2], y_rows[j * P * TOPK:(j + 1) * P * TOPK, :].rearrange(
                    "(p k) n -> p (k n)", k=TOPK)).then_inc(y_loaded[j % 2], 16)
                if j >= 1:
                    sp.wait_ge(s["out_ready"], j)
                    sp.dma_start(out[(j - 1) * P:j * P, :], x_s[:, j - 1, :]).then_inc(s["out_stored"], 16)
            sp.wait_ge(s["out_ready"], TILES)
            sp.dma_start(out[(TILES - 1) * P:T, :], x_s[:, TILES - 1, :]).then_inc(s["out_stored"], 16)
            sp.wait_ge(s["out_stored"], 16 * TILES)

        @block.gpsimd
        def _(pool):
            chain = Chain(pool, s["pool_step"])
            link = chain.link
            link(pool.memset(ident[:, :], 0.0))
            pool.affine_select(out=ident[:, :], in_=ident[:, :], compare_op=ALU.not_equal, fill=1.0, base=0,
                               pattern=[[-1, P]], channel_multiplier=1).then_inc(s["consts"], 1)
            pool.memset(ones_row[:, :], 1.0).then_inc(s["consts"], 1)
            pool.memset(eps_t[:, :], EPS).then_inc(s["consts"], 1)
            pool.memset(v_s[:, :, :, :, P:P + 1], 1.0).then_inc(s["consts"], 1)
            pool.memset(kv_s[:, :, :], 0.0).then_inc(s["consts"], 1)
            pool.memset(ks_s[:, :, :], 0.0).then_inc(s["consts"], 1)
            pool.memset(zeros[:, :], 0.0).then_inc(s["zeros_ready"], 1)

            def stage_wq(g):
                pool.wait_ge(s["wq_loaded"], g * 16 + 16)
                at_least(pool, s["projected"], (g - 1) * NPROJ + Q_DONE[1])
                src = wq_s[:, :, 0:GROUP] if isinstance(g, int) else wq_s[:, :, bass.ds(g * GROUP, GROUP)]
                pool.tensor_copy(wq_g[:, :, :], src).then_inc(s["wq_staged"], 1)

            stage_wq(0)
            link(pool.memset(ones_b[:, :], 1.0))
            pool.affine_select(out=before_b[:, :], in_=ones_b[:, :], compare_op=ALU.is_gt, fill=0.0, base=0,
                               pattern=[[1, P]], channel_multiplier=-1).then_inc(s["consts"], 1)
            pool.iota(iota_e[:, :], pattern=[[1, E]], base=0, channel_multiplier=0,
                      allow_small_or_imprecise_dtypes=True).then_inc(s["consts"], 1)
            pool.iota(iota_c[:, :], pattern=[[1, CAP]], base=0, channel_multiplier=0,
                      allow_small_or_imprecise_dtypes=True).then_inc(s["consts"], 1)
            link(pool.memset(slot_is_own[:, :], 1.0))
            pool.affine_select(out=slot_is_own[:, :], in_=slot_is_own[:, :], compare_op=ALU.not_equal, fill=0.0,
                               base=-(CAP - 1), pattern=[[0, 1]], channel_multiplier=1).then_inc(s["consts"], 1)
            link(pool.memset(slot_is_last[:, :], 1.0))
            pool.affine_select(out=slot_is_last[:, :], in_=slot_is_last[:, :], compare_op=ALU.is_equal, fill=0.0,
                               base=-(CAP - 1), pattern=[[0, 1]], channel_multiplier=1).then_inc(s["consts"], 1)
            link(pool.iota(dst_base[:, :], pattern=[[1, PAD_E]], base=Y_ROWS, channel_multiplier=0,
                           allow_small_or_imprecise_dtypes=True))
            pool.affine_select(out=dst_base[:, :], in_=dst_base[:, :], compare_op=ALU.is_equal, fill=-1.0,
                               base=-(CAP - 1), pattern=[[0, PAD_E]], channel_multiplier=1).then_inc(s["consts"], 1)
            link(pool.memset(vals[:, :, :, :], 0.0))
            pool.iota(vals[:, :, 0:E, 0], pattern=[[0, TILES], [0, E]], base=0, channel_multiplier=1,
                      allow_small_or_imprecise_dtypes=True).then_inc(s["consts"], 1)
            pool.iota(vals[:, :, 0:E, 1], pattern=[[P, TILES], [0, E]], base=0, channel_multiplier=0,
                      allow_small_or_imprecise_dtypes=True).then_inc(s["consts"], 1)
            pool.memset(slot_of[:, :, :], -1.0).then_inc(s["consts"], 1)

            with pool.Fori(1, GROUPS) as g:
                stage_wq(g)

            def cross(b):
                at_least(pool, s["s_made"], b * XH)
                at_least(pool, s["vT_made"], b)
                pool.wait_ge(s["ctx_loaded"], 16)
                pool.tensor_copy(ctx_b[:, :, :].rearrange("p k n -> p (k n)"), one(ctx_s, b)).then_inc(s["ctx_staged"], 1)
                for h in range(XH):
                    pool.wait_ge(s["rcp_done"], b * XH + h + 1)
                    i = h % RING
                    inverse = prs[:, i, :].rearrange("p (m a) -> p m a", a=1).broadcast_to([P, 2, D])
                    pool.tensor_tensor(p_s[:, i, :, :], p_s[:, i, :, :], inverse, ALU.mult).then_inc(s["p_normed"], 1)
            cross(0)
            with pool.Fori(1, B) as b:
                cross(b)

            def stage_tokens(j0):
                for i in range(2):
                    at_least(pool, s["sh_gu_made"], j0 + i - 1)
                    pool.wait_ge(s["xT_moved"], TILES)
                    src = (xnT[:, :, (j0 + i) * P:(j0 + i + 1) * P] if isinstance(j0, int)
                           else xnT[:, :, bass.ds((j0 + i) * P, P)])
                    pool.tensor_copy(hT_j[:, i, :, :], src).then_inc(s["hT_staged"], 1)
            stage_tokens(0)
            with pool.Fori(1, TILES // 2) as half:
                stage_tokens(half * 2)

            bound = pool.alloc_register()

            def gather(e, turn, i):
                pool.wait_ge(s["tab_moved"], e + 1)
                at_least(pool, s["xeT_made"], e - RING + 1)
                pool.wait_ge(s["h_stored"], 16 * TILES)
                pool.reg_add(bound, pool.zero_reg, T - 1)
                pool.indirect_dma_start(xe[:, i, :], None, h_rows, bass.IndirectOffsetOnAxis(ap=src_now[:, i:i + 1], axis=0),
                                        bounds_check=bound, oob_is_err=False).then_inc(gathered[i], 16)

            def scatter(e, i):
                pool.wait_ge(s["oe_moved"], e + 1)
                pool.wait_ge(s["y_zeroed"], 32 * TILES)
                pool.reg_add(bound, pool.zero_reg, Y_ROWS + E - 1)
                pool.indirect_dma_start(y_rows, bass.IndirectOffsetOnAxis(ap=dst_now[:, i:i + 1], axis=0), oe[:, i, :], None,
                                        bounds_check=bound, oob_is_err=False).then_inc(scattered[i], 16)

            for e in range(RING):
                gather(e, 0, e)

            def turn(r, last=False):
                for i in range(RING):
                    scatter(r * RING + i, i)
                    if not last:
                        gather(r * RING + i + RING, r + 1, i)
            turn(0)
            with pool.Fori(1, TURNS - 1) as r:
                turn(r)
            turn(TURNS - 1, True)

        @block.scalar
        def _(act):
            def root(n):
                act.wait_ge(s["var_ready"], n)
                nc.scalar.activation(std[:, :], mv[:, :, 1], ACT.Sqrt, bias=eps_t[:, 0:1]).then_inc(s["std_ready"], 1)

            def move_transposed(first):
                for c in range(TILES // 2):
                    act.wait_ge(s["xT_made"], first + c + 1)
                    nc.scalar.copy(xnT[:, :, 2 * c * P:(2 * c + 2) * P].rearrange("p k (i n) -> p k i n", i=2),
                                   ps[:, c, :].rearrange("p (i k n) -> p k i n", i=2, k=KT)).then_inc(s["xT_moved"], 1)

            act.wait_ge(s["consts"], 6)
            root(1)
            move_transposed(0)

            def attend(g):
                for n, (what, b, t) in PROJ:
                    act.wait_ge(s["projected"], g * NPROJ + n + 1)
                    src = ps[:, PJ[n % 3], :]
                    if what == "q":
                        if t == 0:
                            at_least(act, s["heads_made"], (g - 1) * B * PAIRS + (2 * b + 2) * PAIRS)
                        ins = nc.scalar.activation(qT[:, t, b * GROUP:(b + 1) * GROUP], src, ACT.Relu)
                    else:
                        if what == "k" and t == 0:
                            at_least(act, s["kv_made"], g * B + b - 1)
                        if what == "k":
                            ins = nc.scalar.activation(k_s[:, b % 2, t, :], src, ACT.Relu)
                        else:
                            ins = nc.scalar.copy(v_s[:, b % 2, t, :, 0:P], src.rearrange("p (a n) -> p a n", a=PAIRS))
                    ins.then_inc(s["proj_moved"], 1)
            attend(0)
            with act.Fori(1, GROUPS) as g:
                attend(g)

            root(2)

            def cross(b):
                act.wait_ge(s["vT_made"], b + 1)
                at_least(act, s["av_made"], b * XH)
                nc.scalar.copy(vT_s[:, :, :], ps[:, VT, :].rearrange("p (k n) -> p k n", k=KT)).then_inc(s["vT_moved"], 1)
                for h in range(XH):
                    act.wait_ge(s["max_ready"], b * XH + h + 1)
                    at_least(act, s["t_made"], b * XH + h - RING + 1)
                    for m in range(2):
                        ins = nc.scalar.activation(p_s[:, h % RING, m, :], ps[:, SB[h % 4], m * D:(m + 1) * D], ACT.Exp,
                                                   bias=nmx[:, h % RING, m:m + 1], scale=XSCALE,
                                                   accum_out=psm[:, h % RING, m:m + 1])
                    ins.then_inc(s["exp_done"], 1)
            cross(0)
            with act.Fori(1, B) as b:
                cross(b)

            root(3)
            move_transposed(TILES // 2)
            act.wait_ge(s["lg_ready"], 1)
            nc.scalar.activation(sc[:, :, :], lg[:, :, :], ACT.Exp).then_inc(s["lg_exped"], 1)

            def shared(j0):
                for i in range(2):
                    act.wait_ge(s["sh_gu_made"], j0 + i + 1)
                    at_least(act, s["sh_mult"], j0 + i - 1)
                    nc.scalar.activation(sh_s[:, i, :], ps[:, 0, 0:MS], ACT.Silu).then_inc(s["sh_silu"], 1)
                    act.wait_ge(s["shT_made"], j0 + i + 1)
                    at_least(act, s["sh_made"], j0 + i - 1)
                    nc.scalar.copy(sh_T[:, i, :, :], ps[0:MH, 2, :].rearrange("p (k n) -> p k n", k=MSP)).then_inc(s["shT_moved"], 1)
            shared(0)
            with act.Fori(1, TILES // 2) as half:
                shared(half * 2)
            act.wait_ge(s["overT_made"], 1)
            nc.scalar.copy(w_overT[:, :], ps[0:E, 6:8, :].rearrange("p a n -> p (a n)")).then_inc(s["overT_moved"], 1)

            def silu(e, i):
                act.wait_ge(s["gu_made"], e + 1)
                at_least(act, s["he_ready"], e - 1)
                nc.scalar.activation(he_a[:, i % 2, :], ps[0:CAP, i % 2, 0:M], ACT.Silu).then_inc(s["silu_done"], 1)

            def move_heT(e, i):
                act.wait_ge(s["heT_made"], e + 1)
                at_least(act, s["oe_made"], e - 1)
                nc.scalar.copy(heT[:, i % 2, :, :], ps[0:MH, 3, 0:2 * CAP].rearrange("p (k n) -> p k n", k=2)).then_inc(s["heT_moved"], 1)

            def move_oe(e, turn, i):
                act.wait_ge(s["oe_made"], e + 1)
                if not isinstance(turn, int) or turn > 0:
                    act.wait_ge(scattered[i], turn * 16)
                nc.scalar.copy(dst_now[:, i:i + 1], col(dst_f, e))
                nc.scalar.mul(oe[:, i, :], ps[0:CAP, 4 + i % 2, 0:D], col(w_slot, e)).then_inc(s["oe_moved"], 1)

            silu(0, 0)
            move_heT(0, 0)

            def turn(r, last=False):
                for i in range(RING):
                    e = r * RING + i
                    move_oe(e, r, i)
                    if not last or i < RING - 1:
                        silu(e + 1, i + 1)
                        move_heT(e + 1, i + 1)
            turn(0)
            with act.Fori(1, TURNS - 1) as r:
                turn(r)
            turn(TURNS - 1, True)

        @block.vector
        def _(dve):
            chain = Chain(dve, s["dve_step"])
            link = chain.link

            def flat(t):
                return t[:, :, :].rearrange("p a n -> p (a n)")

            def layer_stats(n, normalise):
                for j in range(TILES):
                    ins = nc.vector.bn_stats(stats[:, j, :], x_s[:, j, :])
                link(ins)
                for j in range(TILES):
                    ins = nc.vector.bn_aggr(mv[:, j, :], stats[:, j, :])
                ins.then_inc(s["var_ready"], 1)
                dve.wait_ge(s["var_ready"], n)
                dve.wait_ge(s["std_ready"], n)
                link(nc.vector.reciprocal(rstd[:, :], std[:, :]))
                if normalise:
                    for j in range(TILES):
                        ins = nc.vector.tensor_scalar(xn_s[:, j, :], x_s[:, j, :], mv[:, j, 0:1], rstd[:, j:j + 1],
                                                      ALU.subtract, ALU.mult)
                    ins.then_inc(s["xn_ready"], 1)

            dve.wait_ge(s["x_loaded"], 16 * TILES)
            layer_stats(1, True)
            dve.wait_ge(s["bo_spread"], 1)
            dve.wait_ge(s["xn_ready"], 1)
            nc.vector.tensor_tensor(x_s[:, :, :], x_s[:, :, :],
                                    ps[:, 7, 0:D].rearrange("p (a n) -> p a n", a=1).broadcast_to([P, TILES, D]),
                                    ALU.add).then_inc(s["bo_added"], 1)
            dve.wait_ge(s["bo_added"], 1)

            def lay_kv(g, b):
                dve.wait_ge(s["kv_made"], g * B + b + 1)
                at_least(dve, s["heads_made"], (g * B + b) * PAIRS)
                kv = ps[:, KV:KV + 2, :].rearrange("p a (c n) -> p (a c) n", c=2)
                for h in range(2):
                    r = slice(h * HEAD, (h + 1) * HEAD)
                    nc.vector.tensor_copy(kv_s[r, :, r], kv[r, :, r])
                    ins = nc.vector.tensor_copy(ks_s[r, :, r], kv[r, :, P:P + 1].broadcast_to([HEAD, PAIRS, HEAD]))
                ins.then_inc(s["kv_laid"], 1)

            def norm_heads(g, b):
                for p in range(PAIRS):
                    dve.wait_ge(s["heads_made"], (g * B + b) * PAIRS + p + 1)
                    if p == 0:
                        at_least(dve, s["attn_made"], g * B + b - 1)
                    on = ps[:, ON[p % 2], :]
                    at_least(dve, s["heads_normed"], (g * B + b) * PAIRS + p)
                    link(nc.vector.reciprocal(nrm[:, :], on[:, S:2 * S]))
                    nc.vector.scalar_tensor_tensor(out=aT[:, b % 2, p, :], in0=nrm[:, :], scalar=1.0 / FLOOR, in1=on[:, 0:S],
                                                   op0=ALU.min, op1=ALU.mult).then_inc(s["heads_normed"], 1)

            def add_attention(g, b):
                dve.wait_ge(s["attn_made"], g * B + b + 1)
                xs = x_s[:, 2 * b:2 * b + 2, :].rearrange("p a n -> p (a n)")
                at_least(dve, s["attn_added"], (g - 1) * B + b + 1)
                nc.vector.tensor_tensor(xs, xs, ps[:, AO, :], ALU.add).then_inc(s["attn_added"], 1)

            def attend(g):
                lay_kv(g, 0)
                for b in range(B):
                    norm_heads(g, b)
                    if b + 1 < B:
                        lay_kv(g, b + 1)
                    add_attention(g, b)
            before = chain.n
            attend(0)
            with dve.Fori(1, GROUPS) as g:
                chain.enter(g, 1, chain.n - before)
                attend(g)
            chain.leave(GROUPS - 1)

            dve.wait_ge(s["attn_added"], GROUPS * B)
            layer_stats(2, False)

            def add_cross(b, half):
                dve.wait_ge(s["av_made"], b * XH + 4 * half + 4)
                dve.wait_ge(s["q_ready"], b + 1)
                xs = one(x_s, b * 2 + half)
                nc.vector.tensor_tensor(xs, xs, ps[:, AV[half], 0:D], ALU.add).then_inc(s["av_added"], 1)

            def cross(b):
                at_least(dve, s["s_made"], b * XH)
                for half in range(2):
                    ins = nc.vector.tensor_scalar(q_b[:, half, :], one(x_s, b * 2 + half),
                                                  one(mv, b * 2 + half)[:, 0:1], col(rstd, b * 2 + half),
                                                  ALU.subtract, ALU.mult)
                ins.then_inc(s["q_ready"], 1)
                for h in range(XH + 3):
                    if h < XH:
                        dve.wait_ge(s["s_made"], b * XH + h + 1)
                        at_least(dve, s["max_ready"], b * XH + h - RING + 1)
                        link(nc.vector.tensor_reduce(mx[:, h % RING, :], ps[:, SB[h % 4], :].rearrange(
                            "p (a n) -> p a n", a=2), AX.X, ALU.max))
                        at_least(dve, s["exp_done"], b * XH + h - RING + 1)
                        nc.vector.tensor_scalar(nmx[:, h % RING, :], mx[:, h % RING, :], -XSCALE, None,
                                                ALU.mult).then_inc(s["max_ready"], 1)
                    if 1 <= h <= XH:
                        i = (h - 1) % RING
                        dve.wait_ge(s["exp_done"], b * XH + h)
                        at_least(dve, s["p_normed"], b * XH + h - RING)
                        nc.vector.reciprocal(prs[:, i, :], psm[:, i, :]).then_inc(s["rcp_done"], 1)
                    if 2 <= h <= XH + 1:
                        dve.wait_ge(s["t_made"], b * XH + h - 1)
                        at_least(dve, s["av_made"], b * XH + h - 3)
                        nc.vector.tensor_copy(pT_s[:, h % 2, :, :].rearrange("p a n -> p (a n)"),
                                              ps[:, TB_, :]).then_inc(s["pT_moved"], 1)
                    if h == 7:
                        add_cross(b, 0)
                add_cross(b, 1)
            before = chain.n
            cross(0)
            with dve.Fori(1, B) as b:
                chain.enter(b, 1, chain.n - before)
                cross(b)
            chain.leave(B - 1)

            dve.wait_ge(s["av_added"], 2 * B)
            layer_stats(3, True)

            dve.wait_ge(s["logits_made"], 1)
            lp = ps[:, 4, :].rearrange("p (j e) -> p j e", j=TILES)
            wide = [P, TILES, E]

            def spread(t):
                return t.rearrange("p (j a) -> p j a", a=1).broadcast_to(wide)

            link(nc.vector.tensor_reduce(tmx[:, :], lp, AX.X, ALU.max))
            nc.vector.tensor_tensor(lg[:, :, :], lp, spread(tmx[:, :]), ALU.subtract).then_inc(s["lg_ready"], 1)
            dve.wait_ge(s["lg_exped"], 1)
            link(nc.vector.tensor_reduce(tmx[:, :], sc[:, :, :], AX.X, ALU.add))
            link(nc.vector.reciprocal(tmx[:, :], tmx[:, :]))
            link(nc.vector.tensor_tensor(sc[:, :, :], sc[:, :, :], spread(tmx[:, :]), ALU.mult))
            link(nc.vector.tensor_reduce(flat(gsc), flat(sc).rearrange("p (c n) -> p c n", n=E // NG), AX.X, ALU.max))
            for j in range(TILES):
                ins = nc.vector.max(g8[:, j, :], gsc[:, j, :])
            link(ins)
            for j in range(TILES):
                ins = nc.vector.max_index(gi8[:, j, :], g8[:, j, :], gsc[:, j, :])
            link(ins)
            link(nc.vector.tensor_copy(gif[:, :, :], gi8[:, :, :]))
            groups = iota_e[:, 0:NG].rearrange("p (a n) -> p a n", a=1).broadcast_to([P, TILES, NG])
            dve.wait_ge(s["consts"], 15)
            for n in range(TOPG):
                chosen = gif[:, :, n:n + 1].broadcast_to([P, TILES, NG])
                link(nc.vector.tensor_tensor((gt if n else gm)[:, :, :], groups, chosen, ALU.is_equal))
                if n:
                    link(nc.vector.tensor_tensor(gm[:, :, :], gm[:, :, :], gt[:, :, :], ALU.add))
            link(nc.vector.tensor_tensor(flat(tmp).rearrange("p (c n) -> p c n", n=E // NG),
                                         flat(sc).rearrange("p (c n) -> p c n", n=E // NG),
                                         flat(gm).rearrange("p (c a) -> p c a", a=1).broadcast_to([P, TILES * NG, E // NG]),
                                         ALU.mult))
            for j in range(TILES):
                ins = nc.vector.max(v8[:, j, :], tmp[:, j, :])
            link(ins)
            for j in range(TILES):
                ins = nc.vector.max_index(i8[:, j, :], v8[:, j, :], tmp[:, j, :])
            link(ins)
            link(nc.vector.tensor_copy(i8f[:, :, :], i8[:, :, :]))
            experts = iota_e[:, :].rearrange("p (a n) -> p a n", a=1).broadcast_to(wide)
            for n in range(TOPK):
                chosen = i8f[:, :, n:n + 1].broadcast_to(wide)
                if n == 0:
                    link(nc.vector.tensor_tensor(rank1[:, :, :], experts, chosen, ALU.is_equal))
                    continue
                link(nc.vector.tensor_tensor(oh[:, :, :], experts, chosen, ALU.is_equal))
                link(nc.vector.scalar_tensor_tensor(out=rank1[:, :, :], in0=oh[:, :, :], scalar=float(n + 1),
                                                    in1=rank1[:, :, :], op0=ALU.mult, op1=ALU.add))
            nc.vector.tensor_scalar(mask_b[:, :, :], rank1[:, :, :], 0.0, None, ALU.is_gt).then_inc(s["mask_ready"], 1)
            link(nc.vector.tensor_scalar(mask[:, :, :], rank1[:, :, :], 0.0, None, ALU.is_gt))
            link(nc.vector.tensor_tensor(w_te[:, :, :], tmp[:, :, :], mask[:, :, :], ALU.mult))
            nc.vector.tensor_copy(vals[:, :, 0:E, 2], rank1[:, :, :])
            link(nc.vector.tensor_copy(vals[:, :, 0:E, 3], w_te[:, :, :]))
            link(nc.vector.tensor_tensor(ra[:, :, :], w_te[:, :, :], vals[:, :, 0:E, 3], ALU.subtract))
            link(nc.vector.tensor_copy(vals[:, :, 0:E, 4], ra[:, :, :]))
            link(nc.vector.tensor_tensor(ra[:, :, :], ra[:, :, :], vals[:, :, 0:E, 4], ALU.subtract))
            nc.vector.tensor_copy(vals[:, :, 0:E, 5], ra[:, :, :]).then_inc(s["vals_ready"], 1)
            dve.wait_ge(s["pos_made"], 1)
            link(nc.vector.tensor_scalar(cnt1[:, :], ps[:, 6, 0:E], -1.0, None, ALU.add))
            link(nc.vector.tensor_copy(flat(pos), ps[:, 5, :]))
            last_one = cnt1[:, :].rearrange("p (a n) -> p a n", a=1).broadcast_to(wide)
            link(nc.vector.tensor_tensor(ra[:, :, :], pos[:, :, :], last_one, ALU.is_equal))
            link(nc.vector.scalar_tensor_tensor(out=rb[:, :, :], in0=pos[:, :, :], scalar=float(CAP - 1), in1=ra[:, :, :],
                                                op0=ALU.is_lt, op1=ALU.max))
            link(nc.vector.tensor_tensor(rb[:, :, :], rb[:, :, :], mask[:, :, :], ALU.mult))
            link(nc.vector.tensor_scalar(ra[:, :, :], pos[:, :, :], float(CAP - 1), 1.0, ALU.min, ALU.add))
            link(nc.vector.tensor_tensor(ra[:, :, :], ra[:, :, :], rb[:, :, :], ALU.mult))
            link(nc.vector.tensor_scalar(slot_of[:, :, 0:E], ra[:, :, :], -1.0, None, ALU.add))
            nc.vector.scalar_tensor_tensor(out=w_over[:, :, :], in0=pos[:, :, :], scalar=float(CAP - 1),
                                           in1=w_te[:, :, :], op0=ALU.is_ge, op1=ALU.mult).then_inc(s["over_ready"], 1)

            def one_hot(e, i):
                at_least(dve, s["tab_made"], e - RING + 1)
                slots = (slot_of[:, :, e:e + 1] if isinstance(e, int) else slot_of[:, :, bass.ds(e, 1)])
                nc.vector.tensor_tensor(ohs[:, i % RING, :, :], slots.broadcast_to([P, TILES, CAP]),
                                        iota_c[:, :].rearrange("p (a n) -> p a n", a=1).broadcast_to([P, TILES, CAP]),
                                        ALU.is_equal).then_inc(s["oh_ready"], 1)

            def tables(e, i):
                dve.wait_ge(s["tab_made"], e + 1)
                at_least(dve, s["xeT_made"], e - RING + 1)
                link(nc.vector.tensor_copy(tab[:, :], ps[0:CAP, 6, 0:VALS]))
                link(nc.vector.tensor_tensor(src_now[:, i:i + 1], tab[:, 0:1], tab[:, 1:2], ALU.add))
                link(nc.vector.tensor_reduce(w_sum[:, :], tab[:, 3:6], AX.X, ALU.add))
                nc.vector.tensor_scalar(col(w_slot, e), w_sum[:, :], slot_is_own[:, 0:1], slot_is_last[:, 0:1],
                                        ALU.mult, ALU.add)
                link(nc.vector.scalar_tensor_tensor(out=row_of[:, :], in0=src_now[:, i:i + 1], scalar=float(TOPK),
                                                    in1=tab[:, 2:3], op0=ALU.mult, op1=ALU.add))
                nc.vector.tensor_scalar(col(dst_f, e), row_of[:, :], slot_is_own[:, 0:1], col(dst_base, e),
                                        ALU.mult, ALU.add).then_inc(s["tab_moved"], 1)

            def move_xeT(e, i):
                dve.wait_ge(s["xeT_made"], e + 1)
                at_least(dve, s["gu_made"], e - 1)
                nc.vector.tensor_copy(xeT[:, i % 2, :, :].rearrange("p k n -> p (k n)"),
                                      ps[:, 2, 0:KT * CAP]).then_inc(s["xeT_moved"], 1)

            def mult(e, i):
                dve.wait_ge(s["silu_done"], e + 1)
                at_least(dve, s["heT_made"], e - 1)
                nc.vector.tensor_tensor(he[:, i % 2, :], he_a[:, i % 2, :], ps[0:CAP, i % 2, M:2 * M],
                                        ALU.mult).then_inc(s["he_ready"], 1)

            def shared(j0):
                for i in range(2):
                    dve.wait_ge(s["sh_silu"], j0 + i + 1)
                    at_least(dve, s["shT_made"], j0 + i - 1)
                    nc.vector.tensor_tensor(sh_h[:, i, :], sh_s[:, i, :], ps[:, 1, 0:MS], ALU.mult).then_inc(s["sh_mult"], 1)
                    dve.wait_ge(s["sh_made"], j0 + i + 1)
                    xs = one(x_s, j0 + i)
                    nc.vector.tensor_tensor(xs, xs, ps[:, 3, 0:D], ALU.add).then_inc(s["sh_added"], 1)
            shared(0)
            with dve.Fori(1, TILES // 2) as half:
                shared(half * 2)
            dve.wait_ge(s["dve_step"], chain.n)
            for e in range(RING):
                one_hot(e, e)
            for e in range(RING):
                tables(e, e)
            one_hot(RING, 0)
            move_xeT(0, 0)
            move_xeT(1, 1)
            mult(0, 0)

            def turn(r, last=False):
                for i in range(RING):
                    e = r * RING + i
                    if not last or i < RING - 1:
                        mult(e + 1, i + 1)
                    if not last:
                        one_hot(e + RING + 1, i + 1)
                    if not last or i < RING - 2:
                        move_xeT(e + 2, i)
                    if not last:
                        tables(e + RING, i)
            before = chain.n
            turn(0)
            with dve.Fori(1, TURNS - 1) as r:
                chain.enter(r, 1, chain.n - before)
                turn(r)
            chain.leave(TURNS - 2)
            turn(TURNS - 1, True)

            dve.wait_ge(s["sh_added"], TILES)
            for j in range(TILES):
                dve.wait_ge(y_loaded[j % 2], 16 * (j // 2 + 1))
                link(nc.vector.tensor_reduce(ysum[:, j % 2, :], y_t[j % 2].rearrange("p (k n) -> p n k", k=TOPK), AX.X, ALU.add))
                link(nc.vector.tensor_tensor(x_s[:, j, :], x_s[:, j, :], ysum[:, j % 2, :], ALU.add))
                dve.wait_ge(s["over_made"], j + 1)
                nc.vector.tensor_tensor(x_s[:, j, :], x_s[:, j, :], ps[:, j % 4, 0:D], ALU.add).then_inc(s["out_ready"], 1)

        @block.tensor
        def _(pe):
            def transpose_all(first, ready):
                pe.wait_ge(s["xn_ready"], ready)
                for c in range(TILES // 2):
                    for i in range(2):
                        for k in range(KT):
                            q = i * KT + k
                            ins = pe.transpose(ps[:, c, q * P:(q + 1) * P], xn_s[:, 2 * c + i, k * P:(k + 1) * P], ident[:, :])
                    ins.then_inc(s["xT_made"], 1)

            pe.wait_ge(s["consts"], 6)
            pe.wait_ge(s["bo_loaded"], 16)
            pe.matmul(ps[:, 7, 0:D], ones_row[:, :], bo_row[:, :], start=True, stop=True).then_inc(s["bo_spread"], 1)
            transpose_all(0, 1)
            pe.wait_ge(s["xT_moved"], TILES // 2)
            pe.wait_ge(s["bo_added"], 1)

            def attend(g):
                def project(n):
                    what, b, t = PROJ[n][1]
                    bank = ps[:, PJ[n % 3], :]
                    at_least(pe, s["proj_moved"], g * NPROJ + n - 2)
                    if n == 0:
                        pe.wait_ge(s["wq_staged"], g + 1)
                    if (what, b, t) == ("k", 0, 0):
                        pe.wait_ge(s["wk_loaded"], g * 16 + 16)
                        pe.wait_ge(s["wv_loaded"], g * 16 + 16)
                    for k in range(KT):
                        if what == "q":
                            lhsT, rhs = wq_g[:, k, t * P:(t + 1) * P], xnT[:, k, b * GROUP:(b + 1) * GROUP]
                        else:
                            w = wk_s if what == "k" else wv_s
                            lhsT = xnT[:, k, (TB * b + t) * P:(TB * b + t + 1) * P]
                            rhs = w[:, k, 0:GROUP] if isinstance(g, int) else w[:, k, bass.ds(g * GROUP, GROUP)]
                        ins = pe.matmul(bank, lhsT, rhs, start=(k == 0), stop=(k == KT - 1))
                    ins.then_inc(s["projected"], 1)

                def keys_values(b):
                    pe.wait_ge(s["proj_moved"], g * NPROJ + V_DONE[b])
                    at_least(pe, s["kv_laid"], g * B + b)
                    for p in range(PAIRS):
                        for t in range(TB):
                            ins = pe.matmul(ps[:, KV + p // 2, (p % 2) * 256:(p % 2) * 256 + P + 1],
                                            k_s[:, b % 2, t, p * P:(p + 1) * P], v_s[:, b % 2, t, p, :],
                                            start=(t == 0), stop=(t == TB - 1))
                    ins.then_inc(s["kv_made"], 1)

                def heads(b):
                    pe.wait_ge(s["kv_laid"], g * B + b + 1)
                    pe.wait_ge(s["proj_moved"], g * NPROJ + Q_DONE[b // 2])
                    for p in range(PAIRS):
                        n = (g * B + b) * PAIRS + p
                        at_least(pe, s["heads_normed"], n - 1)
                        q = qT[:, p, b * S:(b + 1) * S]
                        pe.matmul(ps[:, ON[p % 2], 0:S], kv_s[:, p, :], q, start=True, stop=True)
                        pe.matmul(ps[:, ON[p % 2], S:2 * S], ks_s[:, p, :], q, start=True, stop=True).then_inc(s["heads_made"], 1)

                def attention_out(b):
                    pe.wait_ge(s["heads_normed"], (g * B + b + 1) * PAIRS)
                    at_least(pe, s["attn_added"], g * B + b)
                    if b == 0:
                        pe.wait_ge(s["wo_loaded"], g * 16 + 16)
                    for t in range(TB):
                        for p in range(PAIRS):
                            ins = pe.matmul(ps[:, AO, t * D:(t + 1) * D], aT[:, b % 2, p, t * P:(t + 1) * P],
                                            one(wo_s, g * PAIRS + p), start=(p == 0), stop=(p == PAIRS - 1))
                    ins.then_inc(s["attn_made"], 1)

                for n, (what, b, t) in PROJ[:12]:
                    project(n)
                keys_values(0)
                for b in range(1, B):
                    for n, row in PROJ:
                        if row[0] != "q" and row[1] == b:
                            project(n)
                    heads(b - 1)
                    keys_values(b)
                    attention_out(b - 1)
                heads(B - 1)
                attention_out(B - 1)
            attend(0)
            with pe.Fori(1, GROUPS) as g:
                attend(g)
            pe.wait_ge(s["attn_added"], GROUPS * B)
            pe.wait_ge(s["proj_moved"], GROUPS * NPROJ)

            def cross(b):
                pe.wait_ge(s["ctx_staged"], b + 1)
                at_least(pe, s["vT_moved"], b)
                for n in range(2):
                    for t in range(KT):
                        q = n * KT + t
                        ins = pe.transpose(ps[:, VT, q * P:(q + 1) * P], ctx_b[:, t, n * P:(n + 1) * P], ident[:, :])
                ins.then_inc(s["vT_made"], 1)
                pe.wait_ge(s["q_ready"], b + 1)
                for h in range(XH + 3):
                    if h < XH:
                        r = slice(h % 4 * QUAD, h % 4 * QUAD + QUAD)
                        at_least(pe, s["exp_done"], b * XH + h - 3)
                        for m in range(2):
                            ins = pe.matmul(ps[:, SB[h % 4], m * D:(m + 1) * D], q_b[r, h // 4, m * P:(m + 1) * P],
                                            ctx_b[r, h // 4, :], start=True, stop=True)
                        ins.then_inc(s["s_made"], 1)
                    if 2 <= h <= XH + 1:
                        pe.wait_ge(s["p_normed"], b * XH + h - 1)
                        at_least(pe, s["pT_moved"], b * XH + h - 2)
                        for n in range(2):
                            for m in range(2):
                                q = n * 2 + m
                                ins = pe.transpose(ps[:, TB_, q * P:(q + 1) * P], p_s[:, (h - 2) % RING, m, n * P:(n + 1) * P],
                                                   ident[:, :])
                        ins.then_inc(s["t_made"], 1)
                    if h >= 3:
                        a = h - 3
                        pe.wait_ge(s["pT_moved"], b * XH + a + 1)
                        if a == 0:
                            pe.wait_ge(s["vT_moved"], b + 1)
                        if a % 4 == 0:
                            at_least(pe, s["av_added"], b * 2 + a // 4 - 1)
                        r = slice(a % 4 * QUAD, a % 4 * QUAD + QUAD)
                        for n in range(2):
                            ins = pe.matmul(ps[r, AV[a // 4], 0:D], vT_s[:, n, a * XD:(a + 1) * XD], pT_s[:, a % 2, n, :],
                                            start=(n == 0), stop=(n == 1))
                        ins.then_inc(s["av_made"], 1)
            cross(0)
            with pe.Fori(1, B) as b:
                cross(b)
            pe.wait_ge(s["av_added"], 2 * B)

            transpose_all(TILES // 2, 2)
            pe.wait_ge(s["xT_moved"], TILES)
            pe.wait_ge(s["gate_loaded"], 16)
            for j in range(TILES):
                for k in range(KT):
                    ins = pe.matmul(ps[:, 4, j * E:(j + 1) * E], xnT[:, k, j * P:(j + 1) * P], gate_s[:, k, :],
                                    start=(k == 0), stop=(k == KT - 1))
            ins.then_inc(s["logits_made"], 1)

            pe.wait_ge(s["mask_ready"], 1)
            pe.wait_ge(s["consts"], 15)
            for j in range(TILES):
                for i in range(j + 1):
                    pe.matmul(ps[:, 5, j * E:(j + 1) * E], (before_b if i == j else ones_b)[:, :], mask_b[:, i, :],
                              start=(i == 0), stop=(i == j))
            for i in range(TILES):
                ins = pe.matmul(ps[:, 6, 0:E], ones_b[:, :], mask_b[:, i, :], start=(i == 0), stop=(i == TILES - 1))
            ins.then_inc(s["pos_made"], 1)
            pe.wait_ge(s["over_ready"], 1)
            for j in range(TILES):
                ins = pe.transpose(ps[0:E, 6 + j // 4, (j % 4) * P:(j % 4 + 1) * P], w_over[:, j, :], ident[:, :])
            ins.then_inc(s["overT_made"], 1)

            pe.wait_ge(s["sgu_loaded"], 16)
            pe.wait_ge(s["sd_loaded"], 16)

            def shared(j0):
                for i in range(2):
                    pe.wait_ge(s["hT_staged"], j0 + i + 1)
                    at_least(pe, s["sh_mult"], j0 + i)
                    for half in range(2):
                        for k in range(KT):
                            ins = pe.matmul(ps[:, half, 0:MS], hT_j[:, i, k, :], sgu_s[:, k, half * MS:(half + 1) * MS],
                                            start=(k == 0), stop=(k == KT - 1))
                    ins.then_inc(s["sh_gu_made"], 1)
                    pe.wait_ge(s["sh_mult"], j0 + i + 1)
                    at_least(pe, s["shT_moved"], j0 + i)
                    for k in range(MSP):
                        ins = pe.transpose(ps[0:MH, 2, k * P:(k + 1) * P], sh_h[:, i, k * MH:(k + 1) * MH], ident[:, :])
                    ins.then_inc(s["shT_made"], 1)
                    pe.wait_ge(s["shT_moved"], j0 + i + 1)
                    at_least(pe, s["sh_added"], j0 + i)
                    for k in range(MSP):
                        ins = pe.matmul(ps[:, 3, 0:D], sh_T[:, i, k, :], sd_s[:, k, :], start=(k == 0), stop=(k == MSP - 1))
                    ins.then_inc(s["sh_made"], 1)
            shared(0)
            with pe.Fori(1, TILES // 2) as half:
                shared(half * 2)
            pe.wait_ge(s["sh_added"], TILES)
            pe.wait_ge(s["overT_moved"], 1)
            pe.wait_ge(s["vals_ready"], 1)

            def table(e, i):
                pe.wait_ge(s["oh_ready"], e + 1)
                at_least(pe, s["tab_moved"], e)
                for j in range(TILES):
                    v = vals[:, j, e, :] if isinstance(e, int) else vals[:, j, bass.ds(e, 1), :].rearrange("p a n -> p (a n)")
                    ins = pe.matmul(ps[0:CAP, 6, 0:VALS], ohs[:, i % RING, j, :], v, start=(j == 0), stop=(j == TILES - 1))
                ins.then_inc(s["tab_made"], 1)

            def transpose_tokens(e, turn, i):
                pe.wait_ge(gathered[i % RING], turn * 16 + 16)
                at_least(pe, s["xeT_moved"], e)
                for k in range(KT):
                    ins = pe.transpose(ps[:, 2, k * CAP:(k + 1) * CAP], xe[:, i % RING, k * P:(k + 1) * P], ident[0:CAP, 0:CAP])
                ins.then_inc(s["xeT_made"], 1)

            def gate_up(e, turn, i):
                pe.wait_ge(wgu_loaded[i % RING], turn * 16 + 16)
                pe.wait_ge(s["xeT_moved"], e + 1)
                at_least(pe, s["he_ready"], e - 1)
                for k in range(KT):
                    ins = pe.matmul(ps[0:CAP, i % 2, 0:2 * M], xeT[:, i % 2, k, :], wgu_s[:, i % RING, k * 2 * M:(k + 1) * 2 * M],
                                    start=(k == 0), stop=(k == KT - 1))
                ins.then_inc(s["gu_made"], 1)

            def transpose_hidden(e, i):
                pe.wait_ge(s["he_ready"], e + 1)
                at_least(pe, s["heT_moved"], e)
                for k in range(2):
                    ins = pe.transpose(ps[0:MH, 3, k * CAP:(k + 1) * CAP], he[:, i % 2, k * MH:(k + 1) * MH], ident[0:CAP, 0:CAP])
                ins.then_inc(s["heT_made"], 1)

            def down(e, turn, i):
                pe.wait_ge(wd_loaded[i % RING], turn * 16 + 16)
                pe.wait_ge(s["heT_moved"], e + 1)
                at_least(pe, s["oe_moved"], e - 1)
                for k in range(2):
                    ins = pe.matmul(ps[0:CAP, 4 + i % 2, 0:D], heT[:, i % 2, k, :], wd_s[:, i % RING, k * D:(k + 1) * D],
                                    start=(k == 0), stop=(k == 1))
                ins.then_inc(s["oe_made"], 1)

            for e in range(RING):
                table(e, e)
            transpose_tokens(0, 0, 0)
            transpose_tokens(1, 0, 1)
            gate_up(0, 0, 0)
            transpose_hidden(0, 0)

            def turn(r, last=False):
                for i in range(RING):
                    e = r * RING + i
                    down(e, r, i)
                    if not last or i < RING - 1:
                        gate_up(e + 1, r + (i + 1) // RING, i + 1)
                    if not last or i < RING - 2:
                        transpose_tokens(e + 2, r + (i + 2) // RING, i + 2)
                    if not last:
                        table(e + RING, i)
                    if not last or i < RING - 1:
                        transpose_hidden(e + 1, i + 1)
            turn(0)
            with pe.Fori(1, TURNS - 1) as r:
                turn(r)
            turn(TURNS - 1, True)

            pe.wait_ge(s["over_loaded"], 16)
            pe.wait_ge(s["oe_moved"], E)
            for j in range(TILES):
                at_least(pe, s["out_ready"], j - 3)
                pe.matmul(ps[:, j % 4, 0:D], w_overT[:, j * P:(j + 1) * P], over_s, start=True, stop=True).then_inc(s["over_made"], 1)


def kernel(x, ctx_2048, L0_attn_Wq, L0_attn_Wk, L0_attn_Wv, L0_attn_Wo, L0_attn_bo, L0_ffn_gate_weight,
           L0_ffn_Wg, L0_ffn_Wu, L0_ffn_Wd, L0_ffn_Sg, L0_ffn_Su, L0_ffn_Sd):
    import numpy as np
    import concourse.bacc as bacc
    from concourse.bass_utils import run_bass_kernel_spmd

    def by_rows(w):
        return np.ascontiguousarray(np.asarray(w).T.reshape(KT, P, -1).transpose(1, 0, 2))

    gu = np.concatenate([np.asarray(L0_ffn_Wg), np.asarray(L0_ffn_Wu)], axis=1)
    arrays = {
        "x": np.asarray(x).reshape(T, D),
        "ctx": np.asarray(ctx_2048),
        "wq": np.asarray(L0_attn_Wq),
        "wk": np.asarray(L0_attn_Wk),
        "wv": np.asarray(L0_attn_Wv),
        "wo": np.asarray(L0_attn_Wo),
        "bo": np.asarray(L0_attn_bo).reshape(1, D),
        "gate": by_rows(L0_ffn_gate_weight),
        "wgu": gu.reshape(E, 2 * M, KT, P).transpose(0, 3, 2, 1).reshape(E, P, KT * 2 * M),
        "wd": np.asarray(L0_ffn_Wd).transpose(0, 2, 1).reshape(E, 2, MH, D).transpose(0, 2, 1, 3).reshape(E, MH, 2 * D),
        "sgu": np.concatenate([by_rows(L0_ffn_Sg), by_rows(L0_ffn_Su)], axis=2),
        "sd": np.asarray(L0_ffn_Sd).T.reshape(MSP, MH, D).transpose(1, 0, 2),
    }
    arrays = {f"in_{k}": np.ascontiguousarray(v) for k, v in arrays.items()}
    nc = bacc.Bacc("TRN2", target_bir_lowering=False, num_devices=1)
    args = [nc.dram_tensor(k, v.shape, mybir.dt.from_np(v.dtype), kind="ExternalInput").ap() for k, v in arrays.items()]
    args.append(nc.dram_tensor("out", (T, D), F32, kind="ExternalOutput").ap())
    decoder_layer(nc, *args)
    r = run_bass_kernel_spmd(nc, [arrays], core_ids=[0])
    return r.results[0]["out"].reshape(B, S, D)
```

```python
from contextlib import ExitStack

import concourse.bass as bass
from concourse import mybir

ALU = mybir.AluOpType
ACT = mybir.ActivationFunctionType
AX = mybir.AxisListType
F32 = mybir.dt.float32
F32R = mybir.dt.float32r
BF16 = mybir.dt.bfloat16
I32 = mybir.dt.int32
U32 = mybir.dt.uint32

P = 128
QUAD = 32
ALL = slice(None)
BANK = 512
EPS = 1e-5
FLOOR = 1e-6

B, S, D = 4, 256, 256
T = B * S
TILES = T // P
KT = D // P
INNER = 2048
HEAD = 64
GROUP = 512
GROUPS = INNER // GROUP
PAIRS = GROUP // P
TB = S // P
XH = 8
XD = D // XH
XSCALE = 1.0 / float(XD) ** 0.5
E = 64
NG = 8
TOPG = 3
TOPK = 6
CAP = 96
M = 176
MH = M // 2
MHP = 96
MS = 352
MSP = MS // MH
RING = 8
PRING = 4
PAD_E = E + RING
Y_ROWS = T * TOPK
VALS = 6


class Chain:

    def __init__(self, eng, sem):
        self.eng, self.sem, self.n, self.off = eng, sem, 0, None

    def link(self, ins):
        ins.then_inc(self.sem, 1)
        self.n += 1
        self.eng.wait_ge(self.sem, self.n if self.off is None else self.off + self.n)

    def enter(self, i, first, per):
        self.off, self.per = (i - first) * per, per

    def leave(self, turns):
        self.off = None
        self.n += (turns - 1) * self.per


def at_least(eng, sem, value):
    if not isinstance(value, int) or value > 0:
        eng.wait_ge(sem, value)


def one(t, i):
    if isinstance(i, int):
        return t[:, i, :]
    return t[:, bass.ds(i, 1), :].rearrange("p a n -> p (a n)")


def col(t, i):
    return t[:, i:i + 1] if isinstance(i, int) else t[:, bass.ds(i, 1)]


def decoder_layer(nc, x_in, ctx_in, wq_in, wk_in, wv_in, wo_in, bo_in, gate_in, wgu_in, wd_in, sgu_in, sd_in, out):
    ctx = ExitStack()
    with ctx:
        def sb(name, shape, dt=F32):
            return ctx.enter_context(nc.sbuf_tensor(name, shape, dt))

        def sem(name):
            return ctx.enter_context(nc.semaphore(name))

        h_rows = nc.dram_tensor("h_rows", (T, D), F32, kind="Internal").ap()
        y_rows = nc.dram_tensor("y_rows", (Y_ROWS + E, D), F32, kind="Internal").ap()

        ps = ctx.enter_context(nc.psum_tensor("ps", [P, 8, BANK], F32))

        ident = sb("ident", [P, P])
        ones_row = sb("ones_row", [1, P])
        ones_b = sb("ones_b", [P, P], BF16)
        before_b = sb("before_b", [P, P], BF16)
        iota_e = sb("iota_e", [P, E])
        iota_c = sb("iota_c", [P, CAP], BF16)
        zeros = sb("zeros", [P, TOPK * D // 2])
        slot_is_own = sb("slot_is_own", [CAP, 1])
        slot_is_last = sb("slot_is_last", [CAP, 1])
        dst_base = sb("dst_base", [CAP, PAD_E])
        eps_t = sb("eps_t", [P, 1])
        bo_row = sb("bo_row", [1, D])

        x_s = sb("x_s", [P, TILES, D])
        xn_s = sb("xn_s", [P, TILES, D])
        stats = sb("stats", [P, TILES, 6])
        mv = sb("mv", [P, TILES, 2])
        std = sb("std", [P, TILES])
        rstd = sb("rstd", [P, TILES])

        ctx_s = sb("ctx_s", [P, B, KT * D])
        gate_s = sb("gate_s", [P, KT, E])
        sgu_s = sb("sgu_s", [P, KT, 2 * MS])
        sd_s = sb("sd_s", [MHP, MSP, D])
        wgu_s = sb("wgu_s", [P, RING, KT * 2 * M])
        wd_s = sb("wd_s", [MHP, RING, 2 * D])

        slot_of = sb("slot_of", [P, TILES, PAD_E], BF16)
        vals = sb("vals", [P, TILES, PAD_E, VALS], BF16)
        vals_now = sb("vals_now", [P, 2, TILES, CAP], BF16)
        sh_h = sb("sh_h", [P, 2, MSP, MHP])
        he = sb("he", [CAP, 2, 2, MHP])

        attention_memory = ExitStack()
        ctx.enter_context(attention_memory)

        def sa(name, shape, dt=F32):
            return attention_memory.enter_context(nc.sbuf_tensor(name, shape, dt))

        PART = KT * GROUP
        w_raw = sa("w_raw", [P, 4, PART])
        w_hi = sa("w_hi", [P, 4, PART], F32R)
        w_lo = sa("w_lo", [P, 4, PART], F32R)
        xT_hi = sa("xT_hi", [P, KT, T], F32R)
        xT_lo = sa("xT_lo", [P, KT, T], F32R)
        qT = sa("qT", [P, PAIRS, T])
        k_s = sa("k_s", [P, TB, GROUP])
        v_s = sa("v_s", [P, TB, 2 * PAIRS, HEAD + 1])
        kv_s = sa("kv_s", [P, PAIRS, 2, HEAD + 1])
        rn = sa("rn", [P, 2 * PAIRS])
        a_s = sa("a_s", [P, TB, 2 * PAIRS, HEAD])
        aT_hi = sa("aT_hi", [P, PAIRS, S], F32R)
        aT_lo = sa("aT_lo", [P, PAIRS, S], F32R)
        attention_memory.close()

        xnT = sb("xnT", [P, KT, T])

        ctx_b = sb("ctx_b", [P, KT, D])
        q_b = sb("q_b", [P, KT, D])
        vT_s = sb("vT_s", [P, KT, D])
        p_s = sb("p_s", [P, PRING, 2, D])
        pT_s = sb("pT_s", [P, 2, 2, D])
        mx = sb("mx", [P, PRING, 2])
        nmx = sb("nmx", [P, PRING, 2])
        psm = sb("psm", [P, PRING, 2])
        prs = sb("prs", [P, PRING, 2])

        lg, sc, tmp, oh, rank1, mask, pos, ra, rb, w_te, w_over = [
            sb(n, [P, TILES, E]) for n in "lg sc tmp oh rank1 mask pos ra rb w_te w_over".split()]
        mask_b = sb("mask_b", [P, TILES, E], BF16)
        cnt1 = sb("cnt1", [P, E])
        w_overT = sb("w_overT", [E, T])
        tmx = sb("tmx", [P, TILES])
        gsc = sb("gsc", [P, TILES, NG])
        g8 = sb("g8", [P, TILES, 8])
        gi8 = sb("gi8", [P, TILES, 8], U32)
        gif = sb("gif", [P, TILES, 8])
        gm = sb("gm", [P, TILES, NG])
        gt = sb("gt", [P, TILES, NG])
        v8 = sb("v8", [P, TILES, 8])
        i8 = sb("i8", [P, TILES, 8], U32)
        i8f = sb("i8f", [P, TILES, 8])

        hT_j = sb("hT_j", [P, 2, KT, P])
        sh_s = sb("sh_s", [P, 2, MS])
        sh_T = sb("sh_T", [MHP, 2, MSP, P])

        ohs = sb("ohs", [P, RING, TILES, CAP], BF16)
        row_of = sb("row_of", [CAP, 2])
        dst_f = sb("dst_f", [CAP, PAD_E])
        src_now = sb("src_now", [CAP, RING], I32)
        dst_now = sb("dst_now", [CAP, RING], I32)
        w_sum = sb("w_sum", [CAP, 2])
        tab = sb("tab", [CAP, 2, VALS])
        w_slot = sb("w_slot", [CAP, PAD_E])
        xe = sb("xe", [CAP, RING, D])
        oe = sb("oe", [CAP, RING, D])
        xeT = sb("xeT", [P, 2, KT, CAP])
        he_a = sb("he_a", [CAP, 2, M])
        heT = sb("heT", [MHP, 2, 2, CAP])

        y_t = [sb(f"y_t{i}", [P, TOPK * D]) for i in range(2)]
        ysum = sb("ysum", [P, 2, D])
        over_s = sb("over_s", [E, D])

        names = """bo_loaded ctx_loaded gate_loaded sgu_loaded sd_loaded
            consts zeros_ready y_zeroed dve_step pool_step act_step
            var_ready std_ready xn_ready xT_made xT_moved bo_spread bo_added
            w_hi_ready w_lo_ready xT_lo_ready projected proj_moved kv_made kv_laid heads_made heads_normed
            aT_made aT_hi_ready aT_lo_ready attn_made attn_added rn_ready pads_ready
            ctx_staged q_ready vT_made vT_moved s_made max_ready exp_done rcp_done p_normed t_made pT_moved av_made av_added
            h_stored logits_made lg_ready lg_exped mask_ready pos_made over_ready overT_made overT_moved
            hT_staged sh_gu_made sh_silu sh_mult shT_made shT_moved sh_made sh_added
            vals_ready oh_ready tab_made tab_moved xeT_made xeT_moved gu_made silu_done he_ready heT_made heT_moved
            oe_made oe_moved over_made out_ready out_stored over_loaded""".split()
        s = {n: sem(n) for n in names}
        wgu_loaded = [sem(f"wgu_loaded{i}") for i in range(RING)]
        wd_loaded = [sem(f"wd_loaded{i}") for i in range(RING)]
        gathered = [sem(f"gathered{i}") for i in range(RING)]
        scattered = [sem(f"scattered{i}") for i in range(RING)]
        y_loaded = [sem(f"y_loaded{i}") for i in range(2)]
        w_loaded = [sem(f"w_loaded{n}") for n in "qkvo"]
        x_loaded = [sem(f"x_loaded{j}") for j in range(TILES)]

        block = ctx.enter_context(nc.Block())
        TURNS = E // RING

        XT = 4
        PJ = [0, 1]
        KV = 2
        HO = 4
        AT = 6
        AO = 7
        SB = [0, 1, 2, 3]
        TB_ = 4
        AV = [5, 6]
        VT = 7
        TAB = [6, 7]

        PROJ = [("q", h, p) for h in range(2) for p in range(PAIRS)]
        PROJ += [(what, b, t) for b in range(B) for what in "kv" for t in range(TB)]
        NPROJ = len(PROJ)
        NQ = 2 * PAIRS
        WQ, WK, WV, WO = range(4)

        def w_split(g, part):
            return g * 4 + part + 1

        def part_free(eng, g, part):
            if part == WQ:
                at_least(eng, s["projected"], (g - 1) * NPROJ + NQ)
            elif part in (WK, WV):
                at_least(eng, s["projected"], g * NPROJ)
            else:
                at_least(eng, s["attn_made"], g * B * TB)

        @block.sync
        def _(sp):
            for j in range(TILES):
                sp.dma_start(x_s[:, j, :], x_in[j * P:(j + 1) * P, :]).then_inc(x_loaded[j], 16)
            sp.dma_start(bo_row[:, :], bo_in).then_inc(s["bo_loaded"], 16)
            def load_group(g):
                cols = slice(g * GROUP, (g + 1) * GROUP) if isinstance(g, int) else bass.ds(g * GROUP, GROUP)
                for part, src in enumerate((wq_in, wk_in, wv_in)):
                    at_least(sp, s["w_lo_ready"], w_split(g - 1, part))
                    sp.dma_start(w_raw[:, part, :].rearrange("p (k n) -> p k n", k=KT),
                                 src[:, cols].rearrange("(k p) n -> p k n", p=P)).then_inc(w_loaded[part], 16)
                at_least(sp, s["w_lo_ready"], w_split(g - 1, WO))
                sp.dma_start(w_raw[:, WO, :].rearrange("p (k n) -> p k n", k=PAIRS),
                             wo_in[cols, :].rearrange("(k p) n -> p k n", p=P)).then_inc(w_loaded[WO], 16)
            load_group(0)
            sp.dma_start(ctx_s[:, :, :].rearrange("p b (k n) -> p b k n", k=KT),
                         ctx_in.rearrange("b (k p) n -> p b k n", p=P)).then_inc(s["ctx_loaded"], 16)
            sp.dma_start(gate_s[:, :, :], gate_in).then_inc(s["gate_loaded"], 16)
            sp.dma_start(sgu_s[:, :, :], sgu_in).then_inc(s["sgu_loaded"], 16)
            load_group(1)
            sp.wait_ge(s["pads_ready"], 1)
            sp.dma_start(sd_s[0:MH, :, :], sd_in).then_inc(s["sd_loaded"], 16)
            sp.wait_ge(s["zeros_ready"], 1)
            for j in range(TILES):
                for i in range(2):
                    rows = P * TOPK // 2
                    sp.dma_start(y_rows[(2 * j + i) * rows:(2 * j + i + 1) * rows, :].rearrange("(p k) n -> p (k n)", p=P),
                                 zeros[:, :]).then_inc(s["y_zeroed"], 16)

            def load_expert(e, turn, i, before):
                if before:
                    sp.wait_ge(s["gu_made"], e - RING + 1)
                sp.dma_start(wgu_s[:, i, :], wgu_in[e] if isinstance(e, int) else
                             wgu_in[bass.ds(e, 1)].rearrange("a p n -> (a p) n")).then_inc(wgu_loaded[i], 16)
                if before:
                    sp.wait_ge(s["oe_made"], e - RING + 1)
                sp.dma_start(wd_s[0:MH, i, :], wd_in[e] if isinstance(e, int) else
                             wd_in[bass.ds(e, 1)].rearrange("a p n -> (a p) n")).then_inc(wd_loaded[i], 16)

            for i in range(RING):
                load_expert(i, 0, i, False)
            with sp.Fori(2, GROUPS) as g:
                load_group(g)
            sp.wait_ge(s["xn_ready"], 2 * TILES)
            for j in range(TILES):
                sp.dma_start(h_rows[j * P:(j + 1) * P, :], xn_s[:, j, :]).then_inc(s["h_stored"], 16)
            with sp.Fori(1, TURNS) as r:
                for i in range(RING):
                    load_expert(r * RING + i, r, i, True)
            for i in range(RING):
                sp.wait_ge(scattered[i], 16 * TURNS)
            sp.dma_start(over_s[:, :], y_rows[Y_ROWS:Y_ROWS + E, :]).then_inc(s["over_loaded"], 16)
            for j in range(TILES):
                if j >= 2:
                    sp.wait_ge(s["out_ready"], j - 1)
                sp.dma_start(y_t[j % 2][:, :], y_rows[j * P * TOPK:(j + 1) * P * TOPK, :].rearrange(
                    "(p k) n -> p (k n)", k=TOPK)).then_inc(y_loaded[j % 2], 16)
                if j >= 1:
                    sp.wait_ge(s["out_ready"], j)
                    sp.dma_start(out[(j - 1) * P:j * P, :], x_s[:, j - 1, :]).then_inc(s["out_stored"], 16)
            sp.wait_ge(s["out_ready"], TILES)
            sp.dma_start(out[(TILES - 1) * P:T, :], x_s[:, TILES - 1, :]).then_inc(s["out_stored"], 16)
            sp.wait_ge(s["out_stored"], 16 * TILES)

        @block.gpsimd
        def _(pool):
            chain = Chain(pool, s["pool_step"])
            link = chain.link
            link(pool.memset(ident[:, :], 0.0))
            pool.affine_select(out=ident[:, :], in_=ident[:, :], compare_op=ALU.not_equal, fill=1.0, base=0,
                               pattern=[[-1, P]], channel_multiplier=1).then_inc(s["consts"], 1)
            pool.memset(ones_row[:, :], 1.0).then_inc(s["consts"], 1)
            pool.memset(eps_t[:, :], EPS).then_inc(s["consts"], 1)
            pool.memset(v_s[:, :, :, HEAD:HEAD + 1], 1.0).then_inc(s["consts"], 1)
            pool.memset(kv_s[:, :, :, :], 0.0).then_inc(s["consts"], 1)

            def split(g, part):
                pool.wait_ge(s["w_hi_ready"], w_split(g, part))
                pool.tensor_tensor(w_lo[:, part, :], w_raw[:, part, :], w_hi[:, part, :].bitcast(F32),
                                   ALU.subtract).then_inc(s["w_lo_ready"], 1)

            for part in (WQ, WK, WV):
                split(0, part)
            pool.memset(sd_s[:, :, :], 0.0)
            pool.memset(wd_s[:, :, :], 0.0).then_inc(s["pads_ready"], 1)
            pool.memset(zeros[:, :], 0.0).then_inc(s["zeros_ready"], 1)
            split(0, WO)
            pool.memset(sh_h[:, :, :, :], 0.0).then_inc(s["consts"], 1)
            pool.memset(he[:, :, :, :], 0.0).then_inc(s["consts"], 1)
            pool.memset(vals_now[:, :, :, :], 0.0).then_inc(s["consts"], 1)
            link(pool.memset(ones_b[:, :], 1.0))
            pool.affine_select(out=before_b[:, :], in_=ones_b[:, :], compare_op=ALU.is_gt, fill=0.0, base=0,
                               pattern=[[1, P]], channel_multiplier=-1).then_inc(s["consts"], 1)
            pool.iota(iota_e[:, :], pattern=[[1, E]], base=0, channel_multiplier=0,
                      allow_small_or_imprecise_dtypes=True).then_inc(s["consts"], 1)
            pool.iota(iota_c[:, :], pattern=[[1, CAP]], base=0, channel_multiplier=0,
                      allow_small_or_imprecise_dtypes=True).then_inc(s["consts"], 1)
            link(pool.memset(slot_is_own[:, :], 1.0))
            pool.affine_select(out=slot_is_own[:, :], in_=slot_is_own[:, :], compare_op=ALU.not_equal, fill=0.0,
                               base=-(CAP - 1), pattern=[[0, 1]], channel_multiplier=1).then_inc(s["consts"], 1)
            link(pool.memset(slot_is_last[:, :], 1.0))
            pool.affine_select(out=slot_is_last[:, :], in_=slot_is_last[:, :], compare_op=ALU.is_equal, fill=0.0,
                               base=-(CAP - 1), pattern=[[0, 1]], channel_multiplier=1).then_inc(s["consts"], 1)
            link(pool.iota(dst_base[:, :], pattern=[[1, PAD_E]], base=Y_ROWS, channel_multiplier=0,
                           allow_small_or_imprecise_dtypes=True))
            pool.affine_select(out=dst_base[:, :], in_=dst_base[:, :], compare_op=ALU.is_equal, fill=-1.0,
                               base=-(CAP - 1), pattern=[[0, PAD_E]], channel_multiplier=1).then_inc(s["consts"], 1)
            link(pool.memset(vals[:, :, :, :], 0.0))
            pool.iota(vals[:, :, 0:E, 0], pattern=[[0, TILES], [0, E]], base=0, channel_multiplier=1,
                      allow_small_or_imprecise_dtypes=True).then_inc(s["consts"], 1)
            pool.iota(vals[:, :, 0:E, 1], pattern=[[P, TILES], [0, E]], base=0, channel_multiplier=0,
                      allow_small_or_imprecise_dtypes=True).then_inc(s["consts"], 1)
            pool.memset(slot_of[:, :, :], -1.0).then_inc(s["consts"], 1)

            with pool.Fori(1, GROUPS) as g:
                for part in range(4):
                    split(g, part)

            def cross(b):
                at_least(pool, s["s_made"], b * XH)
                at_least(pool, s["vT_made"], b)
                pool.wait_ge(s["ctx_loaded"], 16)
                pool.wait_ge(s["attn_added"], GROUPS * B)
                pool.tensor_copy(ctx_b[:, :, :].rearrange("p k n -> p (k n)"), one(ctx_s, b)).then_inc(s["ctx_staged"], 1)
                for h in range(XH):
                    pool.wait_ge(s["rcp_done"], b * XH + h + 1)
                    i = h % PRING
                    inverse = prs[:, i, :].rearrange("p (m a) -> p m a", a=1).broadcast_to([P, 2, D])
                    pool.tensor_tensor(p_s[:, i, :, :], p_s[:, i, :, :], inverse, ALU.mult).then_inc(s["p_normed"], 1)
            cross(0)
            with pool.Fori(1, B) as b:
                cross(b)

            def stage_tokens(j0):
                for i in range(2):
                    at_least(pool, s["sh_gu_made"], j0 + i - 1)
                    pool.wait_ge(s["xT_moved"], TILES)
                    src = (xnT[:, :, (j0 + i) * P:(j0 + i + 1) * P] if isinstance(j0, int)
                           else xnT[:, :, bass.ds((j0 + i) * P, P)])
                    pool.tensor_copy(hT_j[:, i, :, :], src).then_inc(s["hT_staged"], 1)
            stage_tokens(0)
            with pool.Fori(1, TILES // 2) as half:
                stage_tokens(half * 2)

            bound = pool.alloc_register()

            def gather(e, turn, i):
                pool.wait_ge(s["tab_moved"], turn * (RING // 2) + i // 2 + 1)
                at_least(pool, s["xeT_made"], e - RING + 1)
                pool.wait_ge(s["h_stored"], 16 * TILES)
                pool.reg_add(bound, pool.zero_reg, T - 1)
                pool.indirect_dma_start(xe[:, i, :], None, h_rows, bass.IndirectOffsetOnAxis(ap=src_now[:, i:i + 1], axis=0),
                                        bounds_check=bound, oob_is_err=False).then_inc(gathered[i], 16)

            def scatter(e, i):
                pool.wait_ge(s["oe_moved"], e + 1)
                pool.wait_ge(s["y_zeroed"], 32 * TILES)
                pool.reg_add(bound, pool.zero_reg, Y_ROWS + E - 1)
                pool.indirect_dma_start(y_rows, bass.IndirectOffsetOnAxis(ap=dst_now[:, i:i + 1], axis=0), oe[:, i, :], None,
                                        bounds_check=bound, oob_is_err=False).then_inc(scattered[i], 16)

            for e in range(RING):
                gather(e, 0, e)

            def turn(r, last=False):
                for i in range(RING):
                    scatter(r * RING + i, i)
                    if not last:
                        gather(r * RING + i + RING, r + 1, i)
            turn(0)
            with pool.Fori(1, TURNS - 1) as r:
                turn(r)
            turn(TURNS - 1, True)

        @block.scalar
        def _(act):
            def root(n):
                act.wait_ge(s["var_ready"], n)
                nc.scalar.activation(std[:, :], mv[:, :, 1], ACT.Sqrt, bias=eps_t[:, 0:1]).then_inc(s["std_ready"], 1)

            def move_transposed(rows, first, to):
                for c in rows:
                    act.wait_ge(s["xT_made"], first + c + 1)
                    nc.scalar.copy(to[:, :, 2 * c * P:(2 * c + 2) * P].rearrange("p k (i n) -> p k i n", i=2),
                                   ps[:, XT + c, :].rearrange("p (i k n) -> p k i n", i=2, k=KT)).then_inc(s["xT_moved"], 1)

            def split(g, part):
                act.wait_ge(w_loaded[part], g * 16 + 16)
                part_free(act, g, part)
                nc.scalar.copy(w_hi[:, part, :], w_raw[:, part, :]).then_inc(s["w_hi_ready"], 1)

            act.wait_ge(s["consts"], 5)
            root(1)
            split(0, WQ)
            move_transposed(range(TILES // 4), 0, xT_hi)

            def high_heads(N, t):
                act.wait_ge(s["aT_made"], N * TB + t + 1)
                at_least(act, s["attn_made"], (N - 1) * TB + t + 1)
                nc.scalar.copy(aT_hi[:, :, t * P:(t + 1) * P],
                               ps[:, AT, :].rearrange("p (a n) -> p a n", a=PAIRS)).then_inc(s["aT_hi_ready"], 1)

            def move_projection(g, n):
                what, b, t = PROJ[n]
                act.wait_ge(s["projected"], g * NPROJ + n + 1)
                src = ps[:, PJ[n % 2], :]
                if what == "q":
                    if t == 0:
                        at_least(act, s["heads_made"], ((g - 1) * B + 2 * b + 2) * TB)
                    ins = nc.scalar.activation(qT[:, t, b * GROUP:(b + 1) * GROUP], src, ACT.Relu)
                elif what == "k":
                    if t == 0:
                        at_least(act, s["kv_made"], g * B + b)
                    ins = nc.scalar.activation(k_s[:, t, :], src, ACT.Relu)
                else:
                    ins = nc.scalar.copy(v_s[:, t, :, 0:HEAD], src.rearrange("p (a n) -> p a n", a=2 * PAIRS))
                ins.then_inc(s["proj_moved"], 1)

            def attend(g, first=False, last=False):
                for n in range(NPROJ):
                    move_projection(g, n)
                    if first and n == 1:
                        move_transposed(range(TILES // 4, TILES // 2), 0, xT_hi)
                    if n in (2, 3) and not first:
                        high_heads(g * B - 1, n - 2)
                    for part, after in ((WK, 0), (WV, 1), (WO, NQ - 1)):
                        if n == after:
                            split(g, part)
                    if n >= NQ + 2 * TB and (n - NQ) % (2 * TB) >= TB:
                        high_heads(g * B + (n - NQ) // (2 * TB) - 1, (n - NQ) % TB)
                    if n == NQ + 4 * TB - 1 and not last:
                        split(g + 1, WQ)
            attend(0, first=True)
            with act.Fori(1, GROUPS - 1) as g:
                attend(g)
            attend(GROUPS - 1, last=True)
            for t in range(TB):
                high_heads(GROUPS * B - 1, t)

            root(2)

            def cross(b):
                act.wait_ge(s["vT_made"], b + 1)
                at_least(act, s["av_made"], b * XH)
                nc.scalar.copy(vT_s[:, :, :], ps[:, VT, :].rearrange("p (k n) -> p k n", k=KT)).then_inc(s["vT_moved"], 1)
                for h in range(XH):
                    act.wait_ge(s["max_ready"], b * XH + h + 1)
                    at_least(act, s["t_made"], b * XH + h - PRING + 1)
                    for m in range(2):
                        ins = nc.scalar.activation(p_s[:, h % PRING, m, :], ps[:, SB[h % 4], m * D:(m + 1) * D], ACT.Exp,
                                                   bias=nmx[:, h % PRING, m:m + 1], scale=XSCALE,
                                                   accum_out=psm[:, h % PRING, m:m + 1])
                    ins.then_inc(s["exp_done"], 1)
            cross(0)
            with act.Fori(1, B) as b:
                cross(b)

            root(3)
            move_transposed(range(TILES // 2), TILES // 2, xnT)
            act.wait_ge(s["lg_ready"], 1)
            nc.scalar.activation(sc[:, :, :], lg[:, :, :], ACT.Exp).then_inc(s["lg_exped"], 1)

            def shared(j0):
                for i in range(2):
                    act.wait_ge(s["sh_gu_made"], j0 + i + 1)
                    at_least(act, s["sh_mult"], j0 + i - 1)
                    nc.scalar.activation(sh_s[:, i, :], ps[:, 0, 0:MS], ACT.Silu).then_inc(s["sh_silu"], 1)
                    act.wait_ge(s["shT_made"], j0 + i + 1)
                    at_least(act, s["sh_made"], j0 + i - 1)
                    nc.scalar.copy(sh_T[:, i, :, :], ps[0:MHP, 2, :].rearrange("p (k n) -> p k n", k=MSP)).then_inc(s["shT_moved"], 1)
            shared(0)
            with act.Fori(1, TILES // 2) as half:
                shared(half * 2)
            act.wait_ge(s["overT_made"], 1)
            nc.scalar.copy(w_overT[:, :], ps[0:E, 6:8, :].rearrange("p a n -> p (a n)")).then_inc(s["overT_moved"], 1)

            def silu(e, i):
                act.wait_ge(s["gu_made"], e + 1)
                at_least(act, s["he_ready"], e - 1)
                nc.scalar.activation(he_a[:, i % 2, :], ps[0:CAP, i % 2, 0:M], ACT.Silu).then_inc(s["silu_done"], 1)

            def move_heT(e, i):
                act.wait_ge(s["heT_made"], e + 1)
                at_least(act, s["oe_made"], e - 1)
                nc.scalar.copy(heT[:, i % 2, :, :], ps[0:MHP, 3, 0:2 * CAP].rearrange("p (k n) -> p k n", k=2)).then_inc(s["heT_moved"], 1)

            def move_oe(e, turn, i):
                act.wait_ge(s["oe_made"], e + 1)
                if not isinstance(turn, int) or turn > 0:
                    act.wait_ge(scattered[i], turn * 16)
                nc.scalar.copy(dst_now[:, i:i + 1], col(dst_f, e))
                nc.scalar.mul(oe[:, i, :], ps[0:CAP, 4 + i % 2, 0:D], col(w_slot, e)).then_inc(s["oe_moved"], 1)

            silu(0, 0)
            silu(1, 1)
            move_heT(0, 0)

            def turn(r, last=False):
                for i in range(RING):
                    e = r * RING + i
                    if not last or i < RING - 2:
                        silu(e + 2, i)
                    if not last or i < RING - 1:
                        move_heT(e + 1, i + 1)
                    move_oe(e, r, i)
            turn(0)
            with act.Fori(1, TURNS - 1) as r:
                turn(r)
            turn(TURNS - 1, True)

        @block.vector
        def _(dve):
            chain = Chain(dve, s["dve_step"])
            link = chain.link

            def flat(t):
                return t[:, :, :].rearrange("p a n -> p (a n)")

            def layer_stats(n, normalise):
                for j in range(TILES):
                    if n == 1:
                        dve.wait_ge(x_loaded[j], 16)
                    ins = nc.vector.bn_stats(stats[:, j, :], x_s[:, j, :])
                link(ins)
                for j in range(TILES):
                    ins = nc.vector.bn_aggr(mv[:, j, :], stats[:, j, :])
                ins.then_inc(s["var_ready"], 1)
                dve.wait_ge(s["var_ready"], n)
                dve.wait_ge(s["std_ready"], n)
                link(nc.vector.reciprocal(rstd[:, :], std[:, :]))
                if normalise:
                    for j in range(TILES):
                        nc.vector.tensor_scalar(xn_s[:, j, :], x_s[:, j, :], mv[:, j, 0:1], rstd[:, j:j + 1],
                                                ALU.subtract, ALU.mult).then_inc(s["xn_ready"], 1)

            layer_stats(1, True)
            for c in range(TILES // 2):
                dve.wait_ge(s["xT_moved"], c + 1)
                cols = slice(2 * c * P, (2 * c + 2) * P)
                nc.vector.tensor_tensor(xT_lo[:, :, cols].rearrange("p k (i n) -> p k i n", i=2),
                                        ps[:, XT + c, :].rearrange("p (i k n) -> p k i n", i=2, k=KT),
                                        xT_hi[:, :, cols].bitcast(F32).rearrange("p k (i n) -> p k i n", i=2),
                                        ALU.subtract).then_inc(s["xT_lo_ready"], 1)
            dve.wait_ge(s["bo_spread"], 1)
            dve.wait_ge(s["xn_ready"], TILES)
            nc.vector.tensor_tensor(x_s[:, :, :], x_s[:, :, :],
                                    ps[:, KV + 1, 0:D].rearrange("p (a n) -> p a n", a=1).broadcast_to([P, TILES, D]),
                                    ALU.add).then_inc(s["bo_added"], 1)
            dve.wait_ge(s["bo_added"], 1)

            def lay_kv(N):
                dve.wait_ge(s["kv_made"], N + 1)
                at_least(dve, s["heads_made"], N * TB)
                kv = ps[:, KV:KV + 2, :].rearrange("p a (c n) -> p (a c) n", c=2)
                for h in range(2):
                    r = slice(h * HEAD, (h + 1) * HEAD)
                    ins = nc.vector.tensor_copy(kv_s[r, :, h, :], kv[r, :, h * (HEAD + 1):(h + 1) * (HEAD + 1)])
                ins.then_inc(s["kv_laid"], 1)

            def norm_heads(N, t):
                n = N * TB + t
                dve.wait_ge(s["heads_made"], n + 1)
                at_least(dve, s["heads_normed"], n)
                ho = ps[:, HO:HO + 2, 0:PAIRS * (HEAD + 1)].rearrange("p c (h n) -> p c h n", h=PAIRS)
                inverse = rn[:, :].rearrange("p (c h a) -> p c h a", c=2, a=1)
                nc.vector.reciprocal(inverse, ho[:, :, :, HEAD:HEAD + 1]).then_inc(s["rn_ready"], 1)
                dve.wait_ge(s["rn_ready"], n + 1)
                at_least(dve, s["aT_made"], n - TB + 1)
                for c in range(2):
                    ins = nc.vector.scalar_tensor_tensor(out=a_s[:, t, c * PAIRS:(c + 1) * PAIRS, :],
                                                         in0=inverse[:, c].broadcast_to([P, PAIRS, HEAD]), scalar=1.0 / FLOOR,
                                                         in1=ho[:, c, :, 0:HEAD], op0=ALU.min, op1=ALU.mult)
                ins.then_inc(s["heads_normed"], 1)

            def low_heads(N, t):
                dve.wait_ge(s["aT_hi_ready"], N * TB + t + 1)
                cols = slice(t * P, (t + 1) * P)
                nc.vector.tensor_tensor(aT_lo[:, :, cols], ps[:, AT, :].rearrange("p (a n) -> p a n", a=PAIRS),
                                        aT_hi[:, :, cols].bitcast(F32), ALU.subtract).then_inc(s["aT_lo_ready"], 1)

            def add_attention(N, b):
                dve.wait_ge(s["attn_made"], (N + 1) * TB)
                xs = x_s[:, 2 * b:2 * b + 2, :].rearrange("p a n -> p (a n)")
                at_least(dve, s["attn_added"], N)
                nc.vector.tensor_tensor(xs, xs, ps[:, AO, :], ALU.add).then_inc(s["attn_added"], 1)

            def finish(N, b, lay_next):
                for t in range(TB):
                    norm_heads(N, t)
                for t in range(TB):
                    low_heads(N, t)
                if lay_next:
                    lay_kv(N + 1)
                add_attention(N, b)

            def attend(g, first=False):
                if not first:
                    finish(g * B - 1, B - 1, False)
                lay_kv(g * B)
                for b in range(B - 1):
                    finish(g * B + b, b, True)
            attend(0, first=True)
            with dve.Fori(1, GROUPS) as g:
                attend(g)
            finish(GROUPS * B - 1, B - 1, False)

            dve.wait_ge(s["attn_added"], GROUPS * B)
            layer_stats(2, False)

            def add_cross(b, half):
                dve.wait_ge(s["av_made"], b * XH + 4 * half + 4)
                dve.wait_ge(s["q_ready"], b + 1)
                xs = one(x_s, b * 2 + half)
                nc.vector.tensor_tensor(xs, xs, ps[:, AV[half], 0:D], ALU.add).then_inc(s["av_added"], 1)

            def cross(b):
                at_least(dve, s["s_made"], b * XH)
                for half in range(2):
                    ins = nc.vector.tensor_scalar(q_b[:, half, :], one(x_s, b * 2 + half),
                                                  one(mv, b * 2 + half)[:, 0:1], col(rstd, b * 2 + half),
                                                  ALU.subtract, ALU.mult)
                ins.then_inc(s["q_ready"], 1)
                for h in range(XH + 3):
                    if h < XH:
                        dve.wait_ge(s["s_made"], b * XH + h + 1)
                        at_least(dve, s["max_ready"], b * XH + h - PRING + 1)
                        link(nc.vector.tensor_reduce(mx[:, h % PRING, :], ps[:, SB[h % 4], :].rearrange(
                            "p (a n) -> p a n", a=2), AX.X, ALU.max))
                        at_least(dve, s["exp_done"], b * XH + h - PRING + 1)
                        nc.vector.tensor_scalar(nmx[:, h % PRING, :], mx[:, h % PRING, :], -XSCALE, None,
                                                ALU.mult).then_inc(s["max_ready"], 1)
                    if 1 <= h <= XH:
                        i = (h - 1) % PRING
                        dve.wait_ge(s["exp_done"], b * XH + h)
                        at_least(dve, s["p_normed"], b * XH + h - PRING)
                        nc.vector.reciprocal(prs[:, i, :], psm[:, i, :]).then_inc(s["rcp_done"], 1)
                    if 2 <= h <= XH + 1:
                        dve.wait_ge(s["t_made"], b * XH + h - 1)
                        at_least(dve, s["av_made"], b * XH + h - 3)
                        nc.vector.tensor_copy(pT_s[:, h % 2, :, :].rearrange("p a n -> p (a n)"),
                                              ps[:, TB_, :]).then_inc(s["pT_moved"], 1)
                    if h == 7:
                        add_cross(b, 0)
                add_cross(b, 1)
            before = chain.n
            cross(0)
            with dve.Fori(1, B) as b:
                chain.enter(b, 1, chain.n - before)
                cross(b)
            chain.leave(B - 1)

            dve.wait_ge(s["av_added"], 2 * B)
            layer_stats(3, True)

            dve.wait_ge(s["logits_made"], 1)
            lp = ps[:, 4, :].rearrange("p (j e) -> p j e", j=TILES)
            wide = [P, TILES, E]

            def spread(t):
                return t.rearrange("p (j a) -> p j a", a=1).broadcast_to(wide)

            link(nc.vector.tensor_reduce(tmx[:, :], lp, AX.X, ALU.max))
            nc.vector.tensor_tensor(lg[:, :, :], lp, spread(tmx[:, :]), ALU.subtract).then_inc(s["lg_ready"], 1)
            dve.wait_ge(s["lg_exped"], 1)
            link(nc.vector.tensor_reduce(tmx[:, :], sc[:, :, :], AX.X, ALU.add))
            link(nc.vector.reciprocal(tmx[:, :], tmx[:, :]))
            link(nc.vector.tensor_tensor(sc[:, :, :], sc[:, :, :], spread(tmx[:, :]), ALU.mult))
            link(nc.vector.tensor_reduce(flat(gsc), flat(sc).rearrange("p (c n) -> p c n", n=E // NG), AX.X, ALU.max))
            for j in range(TILES):
                ins = nc.vector.max(g8[:, j, :], gsc[:, j, :])
            link(ins)
            for j in range(TILES):
                ins = nc.vector.max_index(gi8[:, j, :], g8[:, j, :], gsc[:, j, :])
            link(ins)
            link(nc.vector.tensor_copy(gif[:, :, :], gi8[:, :, :]))
            groups = iota_e[:, 0:NG].rearrange("p (a n) -> p a n", a=1).broadcast_to([P, TILES, NG])
            dve.wait_ge(s["consts"], 17)
            for n in range(TOPG):
                chosen = gif[:, :, n:n + 1].broadcast_to([P, TILES, NG])
                link(nc.vector.tensor_tensor((gt if n else gm)[:, :, :], groups, chosen, ALU.is_equal))
                if n:
                    link(nc.vector.tensor_tensor(gm[:, :, :], gm[:, :, :], gt[:, :, :], ALU.add))
            link(nc.vector.tensor_tensor(flat(tmp).rearrange("p (c n) -> p c n", n=E // NG),
                                         flat(sc).rearrange("p (c n) -> p c n", n=E // NG),
                                         flat(gm).rearrange("p (c a) -> p c a", a=1).broadcast_to([P, TILES * NG, E // NG]),
                                         ALU.mult))
            for j in range(TILES):
                ins = nc.vector.max(v8[:, j, :], tmp[:, j, :])
            link(ins)
            for j in range(TILES):
                ins = nc.vector.max_index(i8[:, j, :], v8[:, j, :], tmp[:, j, :])
            link(ins)
            link(nc.vector.tensor_copy(i8f[:, :, :], i8[:, :, :]))
            experts = iota_e[:, :].rearrange("p (a n) -> p a n", a=1).broadcast_to(wide)
            for n in range(TOPK):
                chosen = i8f[:, :, n:n + 1].broadcast_to(wide)
                if n == 0:
                    link(nc.vector.tensor_tensor(rank1[:, :, :], experts, chosen, ALU.is_equal))
                    continue
                link(nc.vector.tensor_tensor(oh[:, :, :], experts, chosen, ALU.is_equal))
                link(nc.vector.scalar_tensor_tensor(out=rank1[:, :, :], in0=oh[:, :, :], scalar=float(n + 1),
                                                    in1=rank1[:, :, :], op0=ALU.mult, op1=ALU.add))
            nc.vector.tensor_scalar(mask_b[:, :, :], rank1[:, :, :], 0.0, None, ALU.is_gt).then_inc(s["mask_ready"], 1)
            link(nc.vector.tensor_scalar(mask[:, :, :], rank1[:, :, :], 0.0, None, ALU.is_gt))
            link(nc.vector.tensor_tensor(w_te[:, :, :], tmp[:, :, :], mask[:, :, :], ALU.mult))
            nc.vector.tensor_copy(vals[:, :, 0:E, 2], rank1[:, :, :])
            link(nc.vector.tensor_copy(vals[:, :, 0:E, 3], w_te[:, :, :]))
            link(nc.vector.tensor_tensor(ra[:, :, :], w_te[:, :, :], vals[:, :, 0:E, 3], ALU.subtract))
            link(nc.vector.tensor_copy(vals[:, :, 0:E, 4], ra[:, :, :]))
            link(nc.vector.tensor_tensor(ra[:, :, :], ra[:, :, :], vals[:, :, 0:E, 4], ALU.subtract))
            nc.vector.tensor_copy(vals[:, :, 0:E, 5], ra[:, :, :]).then_inc(s["vals_ready"], 1)
            dve.wait_ge(s["pos_made"], 1)
            link(nc.vector.tensor_scalar(cnt1[:, :], ps[:, 6, 0:E], -1.0, None, ALU.add))
            link(nc.vector.tensor_copy(flat(pos), ps[:, 5, :]))
            last_one = cnt1[:, :].rearrange("p (a n) -> p a n", a=1).broadcast_to(wide)
            link(nc.vector.tensor_tensor(ra[:, :, :], pos[:, :, :], last_one, ALU.is_equal))
            link(nc.vector.scalar_tensor_tensor(out=rb[:, :, :], in0=pos[:, :, :], scalar=float(CAP - 1), in1=ra[:, :, :],
                                                op0=ALU.is_lt, op1=ALU.max))
            link(nc.vector.tensor_tensor(rb[:, :, :], rb[:, :, :], mask[:, :, :], ALU.mult))
            link(nc.vector.tensor_scalar(ra[:, :, :], pos[:, :, :], float(CAP - 1), 1.0, ALU.min, ALU.add))
            link(nc.vector.tensor_tensor(ra[:, :, :], ra[:, :, :], rb[:, :, :], ALU.mult))
            link(nc.vector.tensor_scalar(slot_of[:, :, 0:E], ra[:, :, :], -1.0, None, ALU.add))
            nc.vector.scalar_tensor_tensor(out=w_over[:, :, :], in0=pos[:, :, :], scalar=float(CAP - 1),
                                           in1=w_te[:, :, :], op0=ALU.is_ge, op1=ALU.mult).then_inc(s["over_ready"], 1)

            def one_hot(e, i):
                at_least(dve, s["tab_made"], e - 1)
                own = (vals[:, :, e:e + 1, :] if isinstance(e, int) else vals[:, :, bass.ds(e, 1), :])
                nc.vector.tensor_copy(vals_now[:, i % 2, :, 0:VALS], own.rearrange("p j a n -> p j (a n)"))
                slots = (slot_of[:, :, e:e + 1] if isinstance(e, int) else slot_of[:, :, bass.ds(e, 1)])
                nc.vector.tensor_tensor(ohs[:, i % RING, :, :], slots.broadcast_to([P, TILES, CAP]),
                                        iota_c[:, :].rearrange("p (a n) -> p a n", a=1).broadcast_to([P, TILES, CAP]),
                                        ALU.is_equal).then_inc(s["oh_ready"], 1)

            def tables(e, i):
                dve.wait_ge(s["tab_made"], e + 2)
                two = slice(e, e + 2) if isinstance(e, int) else bass.ds(e, 2)
                link(nc.vector.tensor_copy(tab[:, :, :], ps[0:CAP, TAB[i // 2 % 2], 0:2 * CAP].rearrange(
                    "p (a n) -> p a n", a=2)[:, :, 0:VALS]))
                link(nc.vector.tensor_tensor(src_now[:, i:i + 2], tab[:, :, 0], tab[:, :, 1], ALU.add))
                link(nc.vector.tensor_reduce(w_sum[:, :], tab[:, :, 3:6], AX.X, ALU.add))
                nc.vector.tensor_scalar(w_slot[:, two], w_sum[:, :], slot_is_own[:, 0:1], slot_is_last[:, 0:1],
                                        ALU.mult, ALU.add)
                link(nc.vector.scalar_tensor_tensor(out=row_of[:, :], in0=src_now[:, i:i + 2], scalar=float(TOPK),
                                                    in1=tab[:, :, 2], op0=ALU.mult, op1=ALU.add))
                nc.vector.scalar_tensor_tensor(out=dst_f[:, two], in0=row_of[:, :], scalar=slot_is_own[:, 0:1],
                                               in1=dst_base[:, two], op0=ALU.mult, op1=ALU.add).then_inc(s["tab_moved"], 1)

            def move_xeT(e, i, wait_used=False):
                dve.wait_ge(s["xeT_made"], e + 1)
                if wait_used:
                    at_least(dve, s["gu_made"], e - 1)
                nc.vector.tensor_copy(xeT[:, i % 2, :, :].rearrange("p k n -> p (k n)"),
                                      ps[:, 2, 0:KT * CAP]).then_inc(s["xeT_moved"], 1)

            def mult(e, i):
                dve.wait_ge(s["silu_done"], e + 1)
                at_least(dve, s["heT_made"], e - 1)
                nc.vector.tensor_tensor(he[:, i % 2, :, 0:MH], he_a[:, i % 2, :].rearrange("p (k n) -> p k n", k=2),
                                        ps[0:CAP, i % 2, M:2 * M].rearrange("p (k n) -> p k n", k=2),
                                        ALU.mult).then_inc(s["he_ready"], 1)

            def shared(j0):
                for i in range(2):
                    dve.wait_ge(s["sh_silu"], j0 + i + 1)
                    at_least(dve, s["shT_made"], j0 + i - 1)
                    nc.vector.tensor_tensor(sh_h[:, i, :, 0:MH], sh_s[:, i, :].rearrange("p (k n) -> p k n", k=MSP),
                                            ps[:, 1, 0:MS].rearrange("p (k n) -> p k n", k=MSP), ALU.mult).then_inc(s["sh_mult"], 1)
                    dve.wait_ge(s["sh_made"], j0 + i + 1)
                    xs = one(x_s, j0 + i)
                    nc.vector.tensor_tensor(xs, xs, ps[:, 3, 0:D], ALU.add).then_inc(s["sh_added"], 1)
            shared(0)
            with dve.Fori(1, TILES // 2) as half:
                shared(half * 2)
            dve.wait_ge(s["dve_step"], chain.n)

            def next_tables(first, end):
                for e in range(first, end, 2):
                    one_hot(e + 1, e + 1)
                    one_hot(e + 2, e + 2)
                    tables(e, e)
            one_hot(0, 0)
            next_tables(0, RING // 2)
            move_xeT(0, 0)
            move_xeT(1, 1)
            mult(0, 0)
            next_tables(RING // 2, RING // 2 + 2)
            move_xeT(2, 0, True)
            mult(1, 1)
            next_tables(RING // 2 + 2, RING)

            def turn(r, last=False):
                for i in range(RING):
                    e = r * RING + i
                    if not last or i < RING - 3:
                        move_xeT(e + 3, i + 3)
                    if not last or i < RING - 2:
                        mult(e + 2, i)
                    if not last:
                        if i % 2 == 1:
                            tables(e + RING - 1, i - 1)
                        one_hot(e + RING + 1, i + 1)
            before = chain.n
            turn(0)
            with dve.Fori(1, TURNS - 1) as r:
                chain.enter(r, 1, chain.n - before)
                turn(r)
            chain.leave(TURNS - 2)
            turn(TURNS - 1, True)

            dve.wait_ge(s["sh_added"], TILES)
            for j in range(TILES):
                dve.wait_ge(y_loaded[j % 2], 16 * (j // 2 + 1))
                link(nc.vector.tensor_reduce(ysum[:, j % 2, :], y_t[j % 2][:, :].rearrange("p (k n) -> p n k", k=TOPK), AX.X, ALU.add))
                link(nc.vector.tensor_tensor(x_s[:, j, :], x_s[:, j, :], ysum[:, j % 2, :], ALU.add))
                dve.wait_ge(s["over_made"], j + 1)
                nc.vector.tensor_tensor(x_s[:, j, :], x_s[:, j, :], ps[:, j % 4, 0:D], ALU.add).then_inc(s["out_ready"], 1)

        @block.tensor
        def _(pe):
            def transpose_rows(rows, ready):
                for c in rows:
                    pe.wait_ge(s["xn_ready"], ready + 2 * c + 2)
                    for i in range(2):
                        for k in range(KT):
                            q = i * KT + k
                            ins = pe.transpose(ps[:, XT + c, q * P:(q + 1) * P], xn_s[:, 2 * c + i, k * P:(k + 1) * P], ident[:, :])
                    ins.then_inc(s["xT_made"], 1)

            pe.wait_ge(s["consts"], 5)
            pe.wait_ge(s["bo_loaded"], 16)
            pe.matmul(ps[:, KV + 1, 0:D], ones_row[:, :], bo_row[:, :], start=True, stop=True).then_inc(s["bo_spread"], 1)
            transpose_rows(range(TILES // 4), 0)
            pe.wait_ge(s["xT_lo_ready"], TILES // 4)

            def exact(bank, pairs):
                n = 0
                for (l_hi, l_lo), (r_hi, r_lo) in pairs:
                    for lhsT, rhs in ((l_hi, r_hi), (l_hi, r_lo), (l_lo, r_hi)):
                        ins = pe.matmul(bank, lhsT, rhs, start=(n == 0), stop=(n == 3 * len(pairs) - 1))
                        n += 1
                return ins

            def parts(hi, lo, *at):
                return hi[at], lo[at]

            def project(g, n):
                what, b, t = PROJ[n]
                at_least(pe, s["proj_moved"], g * NPROJ + n - 1)
                for part, at in ((WQ, 0), (WK, NQ), (WV, NQ + TB)):
                    if n == at:
                        pe.wait_ge(s["w_lo_ready"], w_split(g, part))
                pairs = []
                for k in range(KT):
                    if what == "q":
                        lhsT = parts(w_hi, w_lo, ALL, WQ, slice(k * GROUP + t * P, k * GROUP + (t + 1) * P))
                        rhs = parts(xT_hi, xT_lo, ALL, k, slice(b * GROUP, (b + 1) * GROUP))
                    else:
                        lhsT = parts(xT_hi, xT_lo, ALL, k, slice((TB * b + t) * P, (TB * b + t + 1) * P))
                        rhs = parts(w_hi, w_lo, ALL, WK if what == "k" else WV, slice(k * GROUP, (k + 1) * GROUP))
                    pairs.append((lhsT, rhs))
                exact(ps[:, PJ[n % 2], :], pairs).then_inc(s["projected"], 1)

            def keys_values(g, b):
                pe.wait_ge(s["proj_moved"], g * NPROJ + NQ + (b + 1) * 2 * TB)
                at_least(pe, s["kv_laid"], g * B + b)
                for p in range(PAIRS):
                    for t in range(TB):
                        ins = pe.matmul(ps[:, KV + p // 2, (p % 2) * D:(p % 2) * D + 2 * (HEAD + 1)],
                                        k_s[:, t, p * P:(p + 1) * P], v_s[:, t, 2 * p:2 * p + 2, :].rearrange("p a n -> p (a n)"),
                                        start=(t == 0), stop=(t == TB - 1))
                ins.then_inc(s["kv_made"], 1)

            def heads(N, b, t):
                if t == 0:
                    pe.wait_ge(s["kv_laid"], N + 1)
                at_least(pe, s["heads_normed"], N * TB + t)
                for p in range(PAIRS):
                    w = 2 * (HEAD + 1)
                    ins = pe.matmul(ps[:, HO + p // 2, (p % 2) * w:(p % 2 + 1) * w], qT[:, p, (b * TB + t) * P:(b * TB + t + 1) * P],
                                    kv_s[:, p, :, :].rearrange("p a n -> p (a n)"), start=True, stop=True)
                ins.then_inc(s["heads_made"], 1)

            def transpose_heads(N, t):
                pe.wait_ge(s["heads_normed"], N * TB + t + 1)
                at_least(pe, s["aT_lo_ready"], N * TB + t)
                for p in range(PAIRS):
                    ins = pe.transpose(ps[:, AT, p * P:(p + 1) * P], a_s[:, t, 2 * p:2 * p + 2, :].rearrange("p a n -> p (a n)"),
                                       ident[:, :])
                ins.then_inc(s["aT_made"], 1)

            def attention_out(g, N, b, t):
                pe.wait_ge(s["aT_lo_ready"], N * TB + t + 1)
                if t == 0:
                    at_least(pe, s["attn_added"], N)
                    if b == 0:
                        pe.wait_ge(s["w_lo_ready"], w_split(g, WO))
                exact(ps[:, AO, t * D:(t + 1) * D],
                      [(parts(aT_hi, aT_lo, ALL, p, slice(t * P, (t + 1) * P)),
                        parts(w_hi, w_lo, ALL, WO, slice(p * D, (p + 1) * D))) for p in range(PAIRS)]).then_inc(s["attn_made"], 1)

            def attend(g, first=False):
                N, b = g * B - 1, B - 1
                for n in range(NQ):
                    if first and n == 2:
                        transpose_rows(range(TILES // 4, TILES // 2), 0)
                    if first and n == PAIRS:
                        pe.wait_ge(s["xT_lo_ready"], TILES // 2)
                    project(g, n)
                    if not first:
                        if n < TB:
                            heads(N, b, n)
                        elif n < 2 * TB:
                            transpose_heads(N, n - TB)
                        elif n < 3 * TB:
                            attention_out(g, N, b, n - 2 * TB)
                for n in range(NQ, NQ + 2 * TB):
                    project(g, n)
                if first:
                    pe.wait_ge(s["bo_added"], 1)
                keys_values(g, 0)
                for b in range(B - 1):
                    N = g * B + b
                    at = NQ + (b + 1) * 2 * TB
                    for t in range(TB):
                        project(g, at + t)
                        heads(N, b, t)
                    for t in range(TB):
                        project(g, at + TB + t)
                        transpose_heads(N, t)
                    attention_out(g, N, b, 0)
                    keys_values(g, b + 1)
                    attention_out(g, N, b, 1)
            attend(0, first=True)
            with pe.Fori(1, GROUPS) as g:
                attend(g)
            for t in range(TB):
                heads(GROUPS * B - 1, B - 1, t)
            for t in range(TB):
                transpose_heads(GROUPS * B - 1, t)
            for t in range(TB):
                attention_out(GROUPS - 1, GROUPS * B - 1, B - 1, t)
            pe.wait_ge(s["attn_added"], GROUPS * B)
            pe.wait_ge(s["proj_moved"], GROUPS * NPROJ)

            def cross(b):
                pe.wait_ge(s["ctx_staged"], b + 1)
                at_least(pe, s["vT_moved"], b)
                for n in range(2):
                    for t in range(KT):
                        q = n * KT + t
                        ins = pe.transpose(ps[:, VT, q * P:(q + 1) * P], ctx_b[:, t, n * P:(n + 1) * P], ident[:, :])
                ins.then_inc(s["vT_made"], 1)
                pe.wait_ge(s["q_ready"], b + 1)
                for h in range(XH + 3):
                    if h < XH:
                        r = slice(h % 4 * QUAD, h % 4 * QUAD + QUAD)
                        at_least(pe, s["exp_done"], b * XH + h - 3)
                        for m in range(2):
                            ins = pe.matmul(ps[:, SB[h % 4], m * D:(m + 1) * D], q_b[r, h // 4, m * P:(m + 1) * P],
                                            ctx_b[r, h // 4, :], start=True, stop=True)
                        ins.then_inc(s["s_made"], 1)
                    if 2 <= h <= XH + 1:
                        pe.wait_ge(s["p_normed"], b * XH + h - 1)
                        at_least(pe, s["pT_moved"], b * XH + h - 2)
                        for n in range(2):
                            for m in range(2):
                                q = n * 2 + m
                                ins = pe.transpose(ps[:, TB_, q * P:(q + 1) * P], p_s[:, (h - 2) % PRING, m, n * P:(n + 1) * P],
                                                   ident[:, :])
                        ins.then_inc(s["t_made"], 1)
                    if h >= 3:
                        a = h - 3
                        pe.wait_ge(s["pT_moved"], b * XH + a + 1)
                        if a == 0:
                            pe.wait_ge(s["vT_moved"], b + 1)
                        if a % 4 == 0:
                            at_least(pe, s["av_added"], b * 2 + a // 4 - 1)
                        r = slice(a % 4 * QUAD, a % 4 * QUAD + QUAD)
                        for n in range(2):
                            ins = pe.matmul(ps[r, AV[a // 4], 0:D], vT_s[:, n, a * XD:(a + 1) * XD], pT_s[:, a % 2, n, :],
                                            start=(n == 0), stop=(n == 1))
                        ins.then_inc(s["av_made"], 1)
            cross(0)
            with pe.Fori(1, B) as b:
                cross(b)
            pe.wait_ge(s["av_added"], 2 * B)

            transpose_rows(range(TILES // 2), TILES)
            pe.wait_ge(s["xT_moved"], TILES)
            pe.wait_ge(s["gate_loaded"], 16)
            for j in range(TILES):
                for k in range(KT):
                    ins = pe.matmul(ps[:, 4, j * E:(j + 1) * E], xnT[:, k, j * P:(j + 1) * P], gate_s[:, k, :],
                                    start=(k == 0), stop=(k == KT - 1))
            ins.then_inc(s["logits_made"], 1)

            pe.wait_ge(s["mask_ready"], 1)
            pe.wait_ge(s["consts"], 17)
            for j in range(TILES):
                for i in range(j + 1):
                    pe.matmul(ps[:, 5, j * E:(j + 1) * E], (before_b if i == j else ones_b)[:, :], mask_b[:, i, :],
                              start=(i == 0), stop=(i == j))
            for i in range(TILES):
                ins = pe.matmul(ps[:, 6, 0:E], ones_b[:, :], mask_b[:, i, :], start=(i == 0), stop=(i == TILES - 1))
            ins.then_inc(s["pos_made"], 1)
            pe.wait_ge(s["over_ready"], 1)
            for j in range(TILES):
                ins = pe.transpose(ps[0:E, 6 + j // 4, (j % 4) * P:(j % 4 + 1) * P], w_over[:, j, :], ident[:, :])
            ins.then_inc(s["overT_made"], 1)

            pe.wait_ge(s["sgu_loaded"], 16)
            pe.wait_ge(s["sd_loaded"], 16)

            def shared(j0):
                for i in range(2):
                    pe.wait_ge(s["hT_staged"], j0 + i + 1)
                    at_least(pe, s["sh_mult"], j0 + i)
                    for half in range(2):
                        for k in range(KT):
                            ins = pe.matmul(ps[:, half, 0:MS], hT_j[:, i, k, :], sgu_s[:, k, half * MS:(half + 1) * MS],
                                            start=(k == 0), stop=(k == KT - 1))
                    ins.then_inc(s["sh_gu_made"], 1)
                    pe.wait_ge(s["sh_mult"], j0 + i + 1)
                    at_least(pe, s["shT_moved"], j0 + i)
                    for k in range(MSP):
                        ins = pe.transpose(ps[0:MHP, 2, k * P:(k + 1) * P], sh_h[:, i, k, :], ident[:, :])
                    ins.then_inc(s["shT_made"], 1)
                    pe.wait_ge(s["shT_moved"], j0 + i + 1)
                    at_least(pe, s["sh_added"], j0 + i)
                    for k in range(MSP):
                        ins = pe.matmul(ps[:, 3, 0:D], sh_T[:, i, k, :], sd_s[:, k, :], start=(k == 0), stop=(k == MSP - 1))
                    ins.then_inc(s["sh_made"], 1)
            shared(0)
            with pe.Fori(1, TILES // 2) as half:
                shared(half * 2)
            pe.wait_ge(s["sh_added"], TILES)
            pe.wait_ge(s["overT_moved"], 1)
            pe.wait_ge(s["vals_ready"], 1)

            def table(e, i):
                pe.wait_ge(s["oh_ready"], e + 1)
                for j in range(TILES):
                    q = i % 2 * CAP
                    ins = pe.matmul(ps[0:CAP, TAB[i // 2 % 2], q:q + CAP], ohs[:, i % RING, j, :],
                                    vals_now[:, i % 2, j, :], start=(j == 0), stop=(j == TILES - 1))
                ins.then_inc(s["tab_made"], 1)

            def transpose_tokens(e, turn, i, first=False):
                pe.wait_ge(gathered[i % RING], turn * 16 + 16)
                if first:
                    at_least(pe, s["xeT_moved"], e)
                for k in range(KT):
                    ins = pe.transpose(ps[:, 2, k * CAP:(k + 1) * CAP], xe[:, i % RING, k * P:(k + 1) * P], ident[0:CAP, 0:CAP])
                    if k == KT - 1:
                        ins.then_inc(s["xeT_made"], 1)

            def gate_up(e, turn, i):
                pe.wait_ge(wgu_loaded[i % RING], turn * 16 + 16)
                pe.wait_ge(s["xeT_moved"], e + 1)
                for k in range(KT):
                    ins = pe.matmul(ps[0:CAP, i % 2, 0:2 * M], xeT[:, i % 2, k, :], wgu_s[:, i % RING, k * 2 * M:(k + 1) * 2 * M],
                                    start=(k == 0), stop=(k == KT - 1))
                    if k == KT - 1:
                        ins.then_inc(s["gu_made"], 1)

            def transpose_hidden(e, i):
                pe.wait_ge(s["he_ready"], e + 1)
                at_least(pe, s["heT_moved"], e)
                for k in range(2):
                    ins = pe.transpose(ps[0:MHP, 3, k * CAP:(k + 1) * CAP], he[:, i % 2, k, :], ident[0:CAP, 0:CAP])
                    if k == 1:
                        ins.then_inc(s["heT_made"], 1)

            def down(e, turn, i, last=False):
                pe.wait_ge(wd_loaded[i % RING], turn * 16 + 16)
                if last:
                    pe.wait_ge(s["heT_moved"], e + 1)
                at_least(pe, s["oe_moved"], e - 1)
                for k in range(2):
                    ins = pe.matmul(ps[0:CAP, 4 + i % 2, 0:D], heT[:, i % 2, k, :], wd_s[:, i % RING, k * D:(k + 1) * D],
                                    start=(k == 0), stop=(k == 1))
                    if k == 1:
                        ins.then_inc(s["oe_made"], 1)

            for e in range(RING // 2):
                table(e, e)
            transpose_tokens(0, 0, 0)
            transpose_tokens(1, 0, 1, True)
            gate_up(0, 0, 0)
            for e in range(RING // 2, RING // 2 + 2):
                table(e, e)
            transpose_tokens(2, 0, 2, True)
            gate_up(1, 0, 1)
            transpose_hidden(0, 0)
            for e in range(RING // 2 + 2, RING):
                table(e, e)

            def turn(r, last=False):
                for i in range(RING):
                    e = r * RING + i
                    if not last or i < RING - 2:
                        gate_up(e + 2, r + (i + 2) // RING, i + 2)
                    if not last or i < RING - 3:
                        transpose_tokens(e + 3, r + (i + 3) // RING, i + 3)
                    if not last or i < RING - 1:
                        transpose_hidden(e + 1, i + 1)
                    down(e, r, i, last and i == RING - 1)
                    if not last:
                        table(e + RING, i)
            turn(0)
            with pe.Fori(1, TURNS - 1) as r:
                turn(r)
            turn(TURNS - 1, True)

            pe.wait_ge(s["over_loaded"], 16)
            pe.wait_ge(s["oe_moved"], E)
            for j in range(TILES):
                at_least(pe, s["out_ready"], j - 3)
                pe.matmul(ps[:, j % 4, 0:D], w_overT[:, j * P:(j + 1) * P], over_s[:, :], start=True, stop=True).then_inc(s["over_made"], 1)


def kernel(x, ctx_2048, L0_attn_Wq, L0_attn_Wk, L0_attn_Wv, L0_attn_Wo, L0_attn_bo, L0_ffn_gate_weight,
           L0_ffn_Wg, L0_ffn_Wu, L0_ffn_Wd, L0_ffn_Sg, L0_ffn_Su, L0_ffn_Sd):
    import numpy as np
    import concourse.bacc as bacc
    from concourse.bass_utils import run_bass_kernel_spmd

    def by_rows(w):
        return np.ascontiguousarray(np.asarray(w).T.reshape(KT, P, -1).transpose(1, 0, 2))

    gu = np.concatenate([np.asarray(L0_ffn_Wg), np.asarray(L0_ffn_Wu)], axis=1)
    arrays = {
        "x": np.asarray(x).reshape(T, D),
        "ctx": np.asarray(ctx_2048),
        "wq": np.asarray(L0_attn_Wq),
        "wk": np.asarray(L0_attn_Wk),
        "wv": np.asarray(L0_attn_Wv),
        "wo": np.asarray(L0_attn_Wo),
        "bo": np.asarray(L0_attn_bo).reshape(1, D),
        "gate": by_rows(L0_ffn_gate_weight),
        "wgu": gu.reshape(E, 2 * M, KT, P).transpose(0, 3, 2, 1).reshape(E, P, KT * 2 * M),
        "wd": np.asarray(L0_ffn_Wd).transpose(0, 2, 1).reshape(E, 2, MH, D).transpose(0, 2, 1, 3).reshape(E, MH, 2 * D),
        "sgu": np.concatenate([by_rows(L0_ffn_Sg), by_rows(L0_ffn_Su)], axis=2),
        "sd": np.asarray(L0_ffn_Sd).T.reshape(MSP, MH, D).transpose(1, 0, 2),
    }
    arrays = {f"in_{k}": np.ascontiguousarray(v) for k, v in arrays.items()}
    nc = bacc.Bacc("TRN2", target_bir_lowering=False, num_devices=1)
    args = [nc.dram_tensor(k, v.shape, mybir.dt.from_np(v.dtype), kind="ExternalInput").ap() for k, v in arrays.items()]
    args.append(nc.dram_tensor("out", (T, D), F32, kind="ExternalOutput").ap())
    decoder_layer(nc, *args)
    r = run_bass_kernel_spmd(nc, [arrays], core_ids=[0])
    return r.results[0]["out"].reshape(B, S, D)
```

```python
from contextlib import ExitStack

import concourse.bass as bass
from concourse import mybir

ALU = mybir.AluOpType
ACT = mybir.ActivationFunctionType
AX = mybir.AxisListType
F32 = mybir.dt.float32
F32R = mybir.dt.float32r
BF16 = mybir.dt.bfloat16
I32 = mybir.dt.int32
U32 = mybir.dt.uint32

P = 128
QUAD = 32
ALL = slice(None)
BANK = 512
EPS = 1e-5
FLOOR = 1e-6

B, S, D = 4, 256, 256
T = B * S
TILES = T // P
KT = D // P
INNER = 2048
HEAD = 64
GROUP = 512
GROUPS = INNER // GROUP
PAIRS = GROUP // P
TB = S // P
XH = 8
XD = D // XH
XSCALE = 1.0 / float(XD) ** 0.5
E = 64
NG = 8
TOPG = 3
TOPK = 6
CAP = 96
M = 176
MH = M // 2
MHP = 96
MS = 352
MSP = MS // MH
RING = 8
PRING = 8
YRING = 4
PAD_E = E + RING
Y_ROWS = T * TOPK
VALS = 6


class Chain:

    def __init__(self, eng, sem):
        self.eng, self.sem, self.n, self.off = eng, sem, 0, None

    def link(self, ins):
        ins.then_inc(self.sem, 1)
        self.n += 1
        self.eng.wait_ge(self.sem, self.n if self.off is None else self.off + self.n)

    def enter(self, i, first, per):
        self.off, self.per = (i - first) * per, per

    def leave(self, turns):
        self.off = None
        self.n += (turns - 1) * self.per


def at_least(eng, sem, value):
    if not isinstance(value, int) or value > 0:
        eng.wait_ge(sem, value)


def one(t, i):
    if isinstance(i, int):
        return t[:, i, :]
    return t[:, bass.ds(i, 1), :].rearrange("p a n -> p (a n)")


def col(t, i):
    return t[:, i:i + 1] if isinstance(i, int) else t[:, bass.ds(i, 1)]


def decoder_layer(nc, x_in, ctx_in, wq_in, wk_in, wv_in, wo_in, bo_in, gate_in, wgu_in, wd_in, sgu_in, sd_in, out):
    ctx = ExitStack()
    with ctx:
        def sb(name, shape, dt=F32):
            return ctx.enter_context(nc.sbuf_tensor(name, shape, dt))

        def sem(name):
            return ctx.enter_context(nc.semaphore(name))

        ctx_rows = ctx_in.rearrange("b d n -> (b d) n")
        h_rows = nc.dram_tensor("h_rows", (T, D), F32, kind="Internal").ap()
        q_rows = nc.dram_tensor("q_rows", (T, D), F32, kind="Internal").ap()
        y_rows = nc.dram_tensor("y_rows", (Y_ROWS + E, D), F32, kind="Internal").ap()

        ps = ctx.enter_context(nc.psum_tensor("ps", [P, 8, BANK], F32))

        ident = sb("ident", [P, P])
        ones_row = sb("ones_row", [1, P])
        ones_b = sb("ones_b", [P, P], BF16)
        before_b = sb("before_b", [P, P], BF16)
        iota_e = sb("iota_e", [P, E])
        iota_c = sb("iota_c", [P, CAP], BF16)
        zeros = sb("zeros", [P, TOPK * D // 2])
        slot_is_own = sb("slot_is_own", [CAP, 1])
        slot_is_last = sb("slot_is_last", [CAP, 1])
        dst_base = sb("dst_base", [CAP, PAD_E])
        eps_t = sb("eps_t", [P, 1])
        bo_row = sb("bo_row", [1, D])

        x_s = sb("x_s", [P, TILES, D])
        xn_s = sb("xn_s", [P, TILES, D])
        stats = sb("stats", [P, TILES, 6])
        mv = sb("mv", [P, TILES, 2])
        std = sb("std", [P, TILES])
        rstd = sb("rstd", [P, TILES])

        ctx_b = sb("ctx_b", [P, KT, D])
        gate_s = sb("gate_s", [P, KT, E])
        sgu_s = sb("sgu_s", [P, KT, 2 * MS])
        sd_s = sb("sd_s", [MHP, MSP, D])
        wgu_s = sb("wgu_s", [P, RING, KT * 2 * M])
        wd_s = sb("wd_s", [MHP, RING, 2 * D])

        slot_of = sb("slot_of", [P, TILES, PAD_E], BF16)
        vals = sb("vals", [P, TILES, PAD_E, VALS], BF16)
        vals_now = sb("vals_now", [P, RING // 2, TILES, CAP], BF16)
        sh_h = sb("sh_h", [P, 2, MSP, MHP])
        he = sb("he", [CAP, 2, 2, MHP])

        attention_memory = ExitStack()
        ctx.enter_context(attention_memory)

        def in_attention(name, shape, dt=F32):
            return attention_memory.enter_context(nc.sbuf_tensor(name, shape, dt))

        PART = KT * GROUP
        w_raw = in_attention("w_raw", [P, 4, PART])
        w_hi = in_attention("w_hi", [P, 4, PART], F32R)
        w_lo = in_attention("w_lo", [P, 4, PART], F32R)
        xT_hi = in_attention("xT_hi", [P, KT, T], F32R)
        xT_lo = in_attention("xT_lo", [P, KT, T], F32R)
        qT = in_attention("qT", [P, PAIRS, T])
        k_s = in_attention("k_s", [P, TB, GROUP])
        v_s = in_attention("v_s", [P, TB, 2 * PAIRS, HEAD + 1])
        kv_s = in_attention("kv_s", [P, PAIRS, 2, HEAD + 1])
        rn = in_attention("rn", [P, 2 * PAIRS])
        a_s = in_attention("a_s", [P, TB, 2 * PAIRS, HEAD])
        aT_hi = in_attention("aT_hi", [P, PAIRS, S], F32R)
        aT_lo = in_attention("aT_lo", [P, PAIRS, S], F32R)
        attention_memory.close()

        cross_memory = ExitStack()
        ctx.enter_context(cross_memory)

        def in_cross(name, shape, dt=F32):
            return cross_memory.enter_context(nc.sbuf_tensor(name, shape, dt))

        q_raw = in_cross("q_raw", [3 * XD, 2, XH // 2, D])
        k_raw = in_cross("k_raw", [3 * XD, 2, XH // 2, D])
        q_st = in_cross("q_st", [3 * XD, 2, XH // 2, D], F32R)
        k_st = in_cross("k_st", [3 * XD, 2, XH // 2, D], F32R)
        vT_s = in_cross("vT_s", [P, KT, D])
        p_s = in_cross("p_s", [P, PRING, 2, D])
        pT_s = in_cross("pT_s", [P, 2, 2, D])
        mx = in_cross("mx", [P, PRING, 2])
        nmx = in_cross("nmx", [P, PRING, 2])
        psm = in_cross("psm", [P, PRING, 2])
        prs = in_cross("prs", [P, PRING, 2])
        cross_memory.close()

        xnT = sb("xnT", [P, KT, T])

        lg, sc, tmp, oh, rank1, mask, pos, ra, rb, w_te, w_over = [
            sb(n, [P, TILES, E]) for n in "lg sc tmp oh rank1 mask pos ra rb w_te w_over".split()]
        mask_b = sb("mask_b", [P, TILES, E], BF16)
        cnt1 = sb("cnt1", [P, E])
        w_overT = sb("w_overT", [E, T])
        tmx = sb("tmx", [P, TILES])
        gsc = sb("gsc", [P, TILES, NG])
        g8 = sb("g8", [P, TILES, 8])
        gi8 = sb("gi8", [P, TILES, 8], U32)
        gif = sb("gif", [P, TILES, 8])
        gm = sb("gm", [P, TILES, NG])
        gt = sb("gt", [P, TILES, NG])
        v8 = sb("v8", [P, TILES, 8])
        i8 = sb("i8", [P, TILES, 8], U32)
        i8f = sb("i8f", [P, TILES, 8])

        hT_j = sb("hT_j", [P, 2, KT, P])
        sh_s = sb("sh_s", [P, 2, MS])
        sh_u = sb("sh_u", [P, 2, MS])
        sh_y = sb("sh_y", [P, 2, D])
        sh_T = sb("sh_T", [MHP, 2, MSP, P])

        ohs = sb("ohs", [P, RING, TILES, CAP], BF16)
        row_of = sb("row_of", [CAP, 2])
        dst_f = sb("dst_f", [CAP, PAD_E])
        src_now = sb("src_now", [CAP, RING], I32)
        dst_now = sb("dst_now", [CAP, RING], I32)
        w_sum = sb("w_sum", [CAP, 2])
        tab = sb("tab", [CAP, 2, VALS])
        w_slot = sb("w_slot", [CAP, PAD_E])
        xe = sb("xe", [CAP, RING, D])
        oe = sb("oe", [CAP, RING, D])
        xeT = sb("xeT", [P, 2, KT, CAP])
        he_a = sb("he_a", [CAP, 2, M])
        heT = sb("heT", [MHP, 2, 2, CAP])

        y_t = [sb(f"y_t{i}", [P, TOPK * D]) for i in range(YRING)]
        ysum = sb("ysum", [P, 2, D])
        over_s = sb("over_s", [E, D])

        names = """bo_loaded ctx_loaded gate_loaded sgu_loaded sd_loaded
            consts zeros_ready y_zeroed dve_step pool_step
            var_ready std_ready xn_ready xT_made xT_moved bo_spread bo_added
            w_hi_ready w_lo_ready xT_lo_ready projected proj_moved kv_made kv_laid heads_made heads_normed
            aT_made aT_hi_ready aT_lo_ready attn_made attn_added rn_ready pads_ready
            k_hi_ready q_hi_ready k_lo_ready q_lo_ready vT_made vT_moved
            s_made max_ready exp_done rcp_done p_normed t_made pT_moved av_made av_added
            h_stored logits_made lg_ready lg_exped mask_ready pos_made over_ready overT_made overT_moved
            hT_staged sh_gu_made sh_silu sh_mult shT_made shT_moved sh_made sh_moved sh_added
            vals_ready oh_ready tab_made tab_moved xeT_made xeT_moved gu_made silu_done he_ready heT_made heT_moved
            oe_made oe_moved over_made out_ready out_stored over_loaded""".split()
        s = {n: sem(n) for n in names}
        wgu_loaded = [sem(f"wgu_loaded{i}") for i in range(RING)]
        wd_loaded = [sem(f"wd_loaded{i}") for i in range(RING)]
        gathered = [sem(f"gathered{i}") for i in range(RING)]
        scattered = [sem(f"scattered{i}") for i in range(RING)]
        y_loaded = [sem(f"y_loaded{i}") for i in range(YRING)]
        w_loaded = [sem(f"w_loaded{n}") for n in "qkvo"]
        q_stored = [sem(f"q_stored{b}") for b in range(B)]
        q_loaded = [sem(f"q_loaded{i}") for i in range(2)]
        k_loaded = [sem(f"k_loaded{i}") for i in range(2)]
        x_loaded = [sem(f"x_loaded{j}") for j in range(TILES)]

        block = ctx.enter_context(nc.Block())
        TURNS = E // RING

        XT = 4
        PJ = [0, 1]
        KV = 2
        HO = 4
        AT = 6
        AO = 7
        SB = [0, 1, 2, 3]
        PT = 4
        AV = [5, 6]
        VT = 7
        TAB = [6, 7]

        LAG = 3

        PROJ = [("q", h, p) for h in range(2) for p in range(PAIRS)]
        PROJ += [(what, b, t) for b in range(B) for what in "kv" for t in range(TB)]
        NPROJ = len(PROJ)
        NQ = 2 * PAIRS
        WQ, WK, WV, WO = range(4)

        def w_split(g, part):
            return g * 4 + part + 1

        def part_free(eng, g, part):
            if part == WQ:
                at_least(eng, s["projected"], (g - 1) * NPROJ + NQ)
            elif part in (WK, WV):
                at_least(eng, s["projected"], g * NPROJ)
            else:
                at_least(eng, s["attn_made"], g * B * TB)

        @block.sync
        def _(sp):
            def load_weights(g, part):
                cols = slice(g * GROUP, (g + 1) * GROUP) if isinstance(g, int) else bass.ds(g * GROUP, GROUP)
                at_least(sp, s["w_lo_ready"], w_split(g - 1, part))
                if part == WO:
                    src = wo_in[cols, :].rearrange("(k p) n -> p k n", p=P)
                else:
                    src = (wq_in, wk_in, wv_in)[part][:, cols].rearrange("(k p) n -> p k n", p=P)
                sp.dma_start(w_raw[:, part, :].rearrange("p (k n) -> p k n", k=PAIRS if part == WO else KT),
                             src).then_inc(w_loaded[part], 16)

            def load_group(g):
                for part in (WQ, WK, WV, WO):
                    load_weights(g, part)

            for j in range(TILES // 2):
                sp.dma_start(x_s[:, j, :], x_in[j * P:(j + 1) * P, :]).then_inc(x_loaded[j], 16)
            load_weights(0, WQ)
            for j in range(TILES // 2, TILES):
                sp.dma_start(x_s[:, j, :], x_in[j * P:(j + 1) * P, :]).then_inc(x_loaded[j], 16)
            sp.dma_start(bo_row[:, :], bo_in).then_inc(s["bo_loaded"], 16)
            for part in (WK, WV, WO):
                load_weights(0, part)

            def load_context(b):
                at_least(sp, s["vT_made"], b)
                rows = ctx_in[b] if isinstance(b, int) else ctx_in[bass.ds(b, 1)].rearrange("a d n -> (a d) n")
                sp.dma_start(ctx_b[:, :, :], rows.rearrange("(k p) n -> p k n", p=P)).then_inc(s["ctx_loaded"], 16)

            load_context(0)
            sp.dma_start(gate_s[:, :, :], gate_in).then_inc(s["gate_loaded"], 16)
            sp.dma_start(sgu_s[:, :, :], sgu_in).then_inc(s["sgu_loaded"], 16)
            load_group(1)
            sp.wait_ge(s["pads_ready"], 1)
            sp.dma_start(sd_s[0:MH, :, :], sd_in).then_inc(s["sd_loaded"], 16)
            sp.wait_ge(s["zeros_ready"], 1)
            for j in range(TILES):
                for i in range(2):
                    rows = P * TOPK // 2
                    sp.dma_start(y_rows[(2 * j + i) * rows:(2 * j + i + 1) * rows, :].rearrange("(p k) n -> p (k n)", p=P),
                                 zeros[:, :]).then_inc(s["y_zeroed"], 16)

            def load_expert(e, turn, i, before):
                if before:
                    sp.wait_ge(s["gu_made"], e - RING + 1)
                sp.dma_start(wgu_s[:, i, :], wgu_in[e] if isinstance(e, int) else
                             wgu_in[bass.ds(e, 1)].rearrange("a p n -> (a p) n")).then_inc(wgu_loaded[i], 16)
                if before:
                    sp.wait_ge(s["oe_made"], e - RING + 1)
                sp.dma_start(wd_s[0:MH, i, :], wd_in[e] if isinstance(e, int) else
                             wd_in[bass.ds(e, 1)].rearrange("a p n -> (a p) n")).then_inc(wd_loaded[i], 16)

            for i in range(RING):
                load_expert(i, 0, i, False)
            with sp.Fori(2, GROUPS) as g:
                load_group(g)

            def load_heads(raw, src, b, half, loaded):
                rows = slice(b * S, (b + 1) * S) if isinstance(b, int) else bass.ds(b * S, S)
                heads = src[rows, :].rearrange("(c h p) n -> p c h n", c=2, p=XD)
                for part in range(3):
                    sp.dma_start(raw[part * XD:(part + 1) * XD, half, :, :], heads[:, half, :, :]).then_inc(loaded[half], 16)

            for b in range(B):
                sp.wait_ge(s["xn_ready"], TILES + 2 * b + 2)
                sp.dma_start(q_rows[b * S:(b + 1) * S, :].rearrange("(a p) n -> p a n", p=P),
                             xn_s[:, 2 * b:2 * b + 2, :]).then_inc(q_stored[b], 16)
                if b == 0:
                    sp.wait_ge(s["attn_added"], GROUPS * B)
                    for half in range(2):
                        load_heads(k_raw, ctx_rows, 0, half, k_loaded)
                    sp.wait_ge(q_stored[0], 16)
                    for half in range(2):
                        load_heads(q_raw, q_rows, 0, half, q_loaded)
            for b in range(1, B):
                sp.wait_ge(q_stored[b], 16)
            with sp.Fori(1, B) as b:
                for half in range(2):
                    sp.wait_ge(s["k_lo_ready"], (b * 2 + half - 1) * 2)
                    load_heads(k_raw, ctx_rows, b, half, k_loaded)
                    sp.wait_ge(s["q_lo_ready"], (b * 2 + half - 1) * 2)
                    load_heads(q_raw, q_rows, b, half, q_loaded)
                    if half == 0:
                        load_context(b)
            sp.wait_ge(s["xn_ready"], 3 * TILES)
            for j in range(TILES):
                sp.dma_start(h_rows[j * P:(j + 1) * P, :], xn_s[:, j, :]).then_inc(s["h_stored"], 16)
            with sp.Fori(1, TURNS) as r:
                for i in range(RING):
                    load_expert(r * RING + i, r, i, True)
            for i in range(RING):
                sp.wait_ge(scattered[i], 16 * TURNS)
            sp.dma_start(over_s[:, :], y_rows[Y_ROWS:Y_ROWS + E, :]).then_inc(s["over_loaded"], 16)

            def load_rows(j):
                sp.dma_start(y_t[j % YRING][:, :], y_rows[j * P * TOPK:(j + 1) * P * TOPK, :].rearrange(
                    "(p k) n -> p (k n)", k=TOPK)).then_inc(y_loaded[j % YRING], 16)

            for j in range(YRING):
                load_rows(j)
            for j in range(TILES):
                sp.wait_ge(s["out_ready"], j + 1)
                sp.dma_start(out[j * P:(j + 1) * P, :], x_s[:, j, :]).then_inc(s["out_stored"], 16)
                if j + YRING < TILES:
                    load_rows(j + YRING)
            sp.wait_ge(s["out_stored"], 16 * TILES)

        @block.gpsimd
        def _(pool):
            chain = Chain(pool, s["pool_step"])
            link = chain.link
            link(pool.memset(ident[:, :], 0.0))
            pool.affine_select(out=ident[:, :], in_=ident[:, :], compare_op=ALU.not_equal, fill=1.0, base=0,
                               pattern=[[-1, P]], channel_multiplier=1).then_inc(s["consts"], 1)
            pool.memset(ones_row[:, :], 1.0).then_inc(s["consts"], 1)
            pool.memset(eps_t[:, :], EPS).then_inc(s["consts"], 1)
            pool.memset(v_s[:, :, :, HEAD:HEAD + 1], 1.0).then_inc(s["consts"], 1)
            pool.memset(kv_s[:, :, :, :], 0.0).then_inc(s["consts"], 1)

            def split(g, part):
                pool.wait_ge(s["w_hi_ready"], w_split(g, part))
                pool.tensor_tensor(w_lo[:, part, :], w_raw[:, part, :], w_hi[:, part, :].bitcast(F32),
                                   ALU.subtract).then_inc(s["w_lo_ready"], 1)

            for part in (WQ, WK, WV):
                split(0, part)
            pool.memset(sd_s[:, :, :], 0.0)
            pool.memset(wd_s[:, :, :], 0.0).then_inc(s["pads_ready"], 1)
            pool.memset(zeros[:, :], 0.0).then_inc(s["zeros_ready"], 1)
            split(0, WO)
            pool.memset(sh_h[:, :, :, :], 0.0).then_inc(s["consts"], 1)
            pool.memset(he[:, :, :, :], 0.0).then_inc(s["consts"], 1)
            pool.memset(vals_now[:, :, :, :], 0.0).then_inc(s["consts"], 1)
            link(pool.memset(ones_b[:, :], 1.0))
            pool.affine_select(out=before_b[:, :], in_=ones_b[:, :], compare_op=ALU.is_gt, fill=0.0, base=0,
                               pattern=[[1, P]], channel_multiplier=-1).then_inc(s["consts"], 1)
            pool.iota(iota_e[:, :], pattern=[[1, E]], base=0, channel_multiplier=0,
                      allow_small_or_imprecise_dtypes=True).then_inc(s["consts"], 1)
            pool.iota(iota_c[:, :], pattern=[[1, CAP]], base=0, channel_multiplier=0,
                      allow_small_or_imprecise_dtypes=True).then_inc(s["consts"], 1)
            link(pool.memset(slot_is_own[:, :], 1.0))
            pool.affine_select(out=slot_is_own[:, :], in_=slot_is_own[:, :], compare_op=ALU.not_equal, fill=0.0,
                               base=-(CAP - 1), pattern=[[0, 1]], channel_multiplier=1).then_inc(s["consts"], 1)
            link(pool.memset(slot_is_last[:, :], 1.0))
            pool.affine_select(out=slot_is_last[:, :], in_=slot_is_last[:, :], compare_op=ALU.is_equal, fill=0.0,
                               base=-(CAP - 1), pattern=[[0, 1]], channel_multiplier=1).then_inc(s["consts"], 1)
            link(pool.iota(dst_base[:, :], pattern=[[1, PAD_E]], base=Y_ROWS, channel_multiplier=0,
                           allow_small_or_imprecise_dtypes=True))
            pool.affine_select(out=dst_base[:, :], in_=dst_base[:, :], compare_op=ALU.is_equal, fill=-1.0,
                               base=-(CAP - 1), pattern=[[0, PAD_E]], channel_multiplier=1).then_inc(s["consts"], 1)
            link(pool.memset(vals[:, :, :, :], 0.0))
            pool.iota(vals[:, :, 0:E, 0], pattern=[[0, TILES], [0, E]], base=0, channel_multiplier=1,
                      allow_small_or_imprecise_dtypes=True).then_inc(s["consts"], 1)
            pool.iota(vals[:, :, 0:E, 1], pattern=[[P, TILES], [0, E]], base=0, channel_multiplier=0,
                      allow_small_or_imprecise_dtypes=True).then_inc(s["consts"], 1)
            pool.memset(slot_of[:, :, :], -1.0).then_inc(s["consts"], 1)

            with pool.Fori(1, GROUPS) as g:
                for part in range(4):
                    split(g, part)

            def low_keys(b, pair):
                pool.wait_ge(s["k_hi_ready"], b * 4 + pair + 1)
                half, heads = pair // 2, slice(pair % 2 * 2, pair % 2 * 2 + 2)
                pool.tensor_tensor(k_st[0:XD, half, heads, :], k_raw[0:XD, half, heads, :],
                                   k_st[0:XD, half, heads, :].bitcast(F32), ALU.subtract).then_inc(s["k_lo_ready"], 1)

            def cross(b, last=False):
                for h in range(XH):
                    pool.wait_ge(s["rcp_done"], b * XH + h + 1)
                    i = h % PRING
                    inverse = prs[:, i, :].rearrange("p (m a) -> p m a", a=1).broadcast_to([P, 2, D])
                    pool.tensor_tensor(p_s[:, i, :, :], p_s[:, i, :, :], inverse, ALU.mult).then_inc(s["p_normed"], 1)
                    if h == 0:
                        low_keys(b, 3)
                    elif h % 2 == 0 and not last:
                        low_keys(b + 1, h // 2 - 1)
            for pair in range(3):
                low_keys(0, pair)
            cross(0)
            with pool.Fori(1, B - 1) as b:
                cross(b)
            cross(B - 1, last=True)

            def stage_tokens(j, i):
                at_least(pool, s["sh_gu_made"], j - 1)
                src = xnT[:, :, j * P:(j + 1) * P] if isinstance(j, int) else xnT[:, :, bass.ds(j * P, P)]
                pool.tensor_copy(hT_j[:, i, :, :], src).then_inc(s["hT_staged"], 1)

            def add_shared(j, i):
                pool.wait_ge(s["sh_moved"], j + 1)
                xs = one(x_s, j)
                pool.tensor_tensor(xs, xs, sh_y[:, i, :], ALU.add).then_inc(s["sh_added"], 1)

            def shared_pair(pair, first=False, last=False):
                for i in range(2):
                    j = pair * 2 + i
                    if not first:
                        add_shared(j - 2, i)
                    pool.wait_ge(s["sh_silu"], j + 1)
                    at_least(pool, s["shT_made"], j - 1)
                    pool.tensor_tensor(sh_h[:, i, :, 0:MH], sh_s[:, i, :].rearrange("p (k n) -> p k n", k=MSP),
                                       sh_u[:, i, :].rearrange("p (k n) -> p k n", k=MSP), ALU.mult).then_inc(s["sh_mult"], 1)
                    if not last:
                        stage_tokens(j + 2, i)
            pool.wait_ge(s["xT_moved"], TILES)
            for j in range(2):
                stage_tokens(j, j)
            shared_pair(0, first=True)
            with pool.Fori(1, TILES // 2 - 1) as pair:
                shared_pair(pair)
            shared_pair(TILES // 2 - 1, last=True)
            bound = pool.alloc_register()

            def gather(e, turn, i):
                pool.wait_ge(s["tab_moved"], turn * (RING // 2) + i // 2 + 1)
                at_least(pool, s["xeT_made"], e - RING + 1)
                pool.wait_ge(s["h_stored"], 16 * TILES)
                pool.reg_add(bound, pool.zero_reg, T - 1)
                pool.indirect_dma_start(xe[:, i, :], None, h_rows, bass.IndirectOffsetOnAxis(ap=src_now[:, i:i + 1], axis=0),
                                        bounds_check=bound, oob_is_err=False).then_inc(gathered[i], 16)

            def scatter(e, i):
                pool.wait_ge(s["oe_moved"], e + 1)
                pool.wait_ge(s["y_zeroed"], 32 * TILES)
                pool.reg_add(bound, pool.zero_reg, Y_ROWS + E - 1)
                pool.indirect_dma_start(y_rows, bass.IndirectOffsetOnAxis(ap=dst_now[:, i:i + 1], axis=0), oe[:, i, :], None,
                                        bounds_check=bound, oob_is_err=False).then_inc(scattered[i], 16)

            add_shared(TILES - 2, 0)
            for e in range(RING // 2):
                gather(e, 0, e)
            add_shared(TILES - 1, 1)
            for e in range(RING // 2, RING):
                gather(e, 0, e)

            def turn(r, last=False):
                for i in range(RING):
                    scatter(r * RING + i, i)
                    if not last:
                        gather(r * RING + i + RING, r + 1, i)
            turn(0)
            with pool.Fori(1, TURNS - 1) as r:
                turn(r)
            turn(TURNS - 1, True)

        @block.scalar
        def _(act):
            def root(n, tiles):
                act.wait_ge(s["var_ready"], n)
                r = slice(tiles[0], tiles[-1] + 1)
                nc.scalar.activation(std[:, r], mv[:, r, 1], ACT.Sqrt, bias=eps_t[:, 0:1]).then_inc(s["std_ready"], 1)

            def move_transposed(rows, first, to):
                for c in rows:
                    act.wait_ge(s["xT_made"], first + c + 1)
                    nc.scalar.copy(to[:, :, 2 * c * P:(2 * c + 2) * P].rearrange("p k (i n) -> p k i n", i=2),
                                   ps[:, XT + c, :].rearrange("p (i k n) -> p k i n", i=2, k=KT)).then_inc(s["xT_moved"], 1)

            def split(g, part):
                act.wait_ge(w_loaded[part], g * 16 + 16)
                part_free(act, g, part)
                nc.scalar.copy(w_hi[:, part, :], w_raw[:, part, :]).then_inc(s["w_hi_ready"], 1)

            act.wait_ge(s["consts"], 5)
            root(1, range(TILES // 2))
            split(0, WQ)
            root(2, range(TILES // 2, TILES))
            move_transposed(range(TILES // 4), 0, xT_hi)

            def high_heads(N, t):
                act.wait_ge(s["aT_made"], N * TB + t + 1)
                at_least(act, s["attn_made"], (N - 1) * TB + t + 1)
                nc.scalar.copy(aT_hi[:, :, t * P:(t + 1) * P],
                               ps[:, AT, :].rearrange("p (a n) -> p a n", a=PAIRS)).then_inc(s["aT_hi_ready"], 1)

            def move_projection(g, n):
                what, b, t = PROJ[n]
                act.wait_ge(s["projected"], g * NPROJ + n + 1)
                src = ps[:, PJ[n % 2], :]
                if what == "q":
                    if t == 0:
                        at_least(act, s["heads_made"], ((g - 1) * B + 2 * b + 2) * TB)
                    ins = nc.scalar.activation(qT[:, t, b * GROUP:(b + 1) * GROUP], src, ACT.Relu)
                elif what == "k":
                    if t == 0:
                        at_least(act, s["kv_made"], g * B + b)
                    ins = nc.scalar.activation(k_s[:, t, :], src, ACT.Relu)
                else:
                    ins = nc.scalar.copy(v_s[:, t, :, 0:HEAD], src.rearrange("p (a n) -> p a n", a=2 * PAIRS))
                ins.then_inc(s["proj_moved"], 1)

            def attend(g, first=False, last=False):
                for n in range(NPROJ):
                    move_projection(g, n)
                    if first and n == 1:
                        move_transposed(range(TILES // 4, TILES // 2), 0, xT_hi)
                    if n in (2, 3) and not first:
                        high_heads(g * B - 1, n - 2)
                    for part, after in ((WK, 0), (WV, 1), (WO, NQ - 1)):
                        if n == after:
                            split(g, part)
                    if n >= NQ + 2 * TB and (n - NQ) % (2 * TB) >= TB:
                        high_heads(g * B + (n - NQ) // (2 * TB) - 1, (n - NQ) % TB)
                    if n == NQ + 4 * TB - 1 and not last:
                        split(g + 1, WQ)
            attend(0, first=True)
            with act.Fori(1, GROUPS - 1) as g:
                attend(g)
            attend(GROUPS - 1, last=True)
            for t in range(TB):
                high_heads(GROUPS * B - 1, t)

            root(3, range(TILES - TB))
            root(4, range(TILES - TB, TILES))

            def high_part(st, raw, loaded, ready, b, pair):
                half, heads = pair // 2, slice(pair % 2 * 2, pair % 2 * 2 + 2)
                act.wait_ge(loaded[half], b * 48 + 48)
                at_least(act, s["s_made"], (b - 1) * XH + pair * 2 + 2)
                nc.scalar.copy(st[:, half, heads, :], raw[:, half, heads, :]).then_inc(s[ready], 1)

            def high_keys(b, pair):
                high_part(k_st, k_raw, k_loaded, "k_hi_ready", b, pair)

            def high_queries(b, pair):
                high_part(q_st, q_raw, q_loaded, "q_hi_ready", b, pair)

            def move_pT(n, h):
                act.wait_ge(s["t_made"], n + 1)
                at_least(act, s["av_made"], n - 1)
                nc.scalar.copy(pT_s[:, h % 2, :, :].rearrange("p a n -> p (a n)"), ps[:, PT, :]).then_inc(s["pT_moved"], 1)

            def cross(b, first=False, last=False):
                for h in range(XH):
                    n = b * XH + h
                    if (h - LAG) % 2 == 0 and (h >= LAG or not first):
                        move_pT(n - LAG, h - LAG)
                    act.wait_ge(s["max_ready"], n + 1)
                    at_least(act, s["t_made"], n - PRING + 1)
                    for m in range(2):
                        ins = nc.scalar.activation(p_s[:, h % PRING, m, :], ps[:, SB[h % 4], m * D:(m + 1) * D], ACT.Exp,
                                                   bias=nmx[:, h % PRING, m:m + 1], scale=XSCALE,
                                                   accum_out=psm[:, h % PRING, m:m + 1])
                    ins.then_inc(s["exp_done"], 1)
                    if h == 0:
                        high_queries(b, 3)
                    elif h % 2 == 1 and not last:
                        high_keys(b + 1, h // 2)
                    elif not last:
                        high_queries(b + 1, h // 2 - 1)
                    if h == LAG:
                        act.wait_ge(s["vT_made"], b + 1)
                        at_least(act, s["av_made"], b * XH)
                        nc.scalar.copy(vT_s[:, :, :], ps[:, VT, :].rearrange("p (k n) -> p k n", k=KT)).then_inc(s["vT_moved"], 1)
            act.wait_ge(s["attn_added"], GROUPS * B)
            for pair in range(4):
                high_keys(0, pair)
            for pair in range(3):
                high_queries(0, pair)
            cross(0, first=True)
            with act.Fori(1, B - 1) as b:
                cross(b)
            cross(B - 1, last=True)
            for h in range(XH - LAG, XH):
                if h % 2 == 0:
                    move_pT((B - 1) * XH + h, h)

            root(5, range(TILES - TB))
            root(6, range(TILES - TB, TILES))
            move_transposed(range(TILES // 2), TILES // 2, xnT)
            act.wait_ge(s["lg_ready"], 1)
            nc.scalar.activation(sc[:, :, :], lg[:, :, :], ACT.Exp).then_inc(s["lg_exped"], 1)

            def move_hidden(j, i):
                act.wait_ge(s["shT_made"], j + 1)
                nc.scalar.copy(sh_T[:, i, :, :], ps[0:MHP, 2, :].rearrange("p (k n) -> p k n", k=MSP)).then_inc(s["shT_moved"], 1)

            def move_shared(j, i):
                act.wait_ge(s["sh_made"], j + 1)
                nc.scalar.copy(sh_y[:, i, :], ps[:, 3, 0:D]).then_inc(s["sh_moved"], 1)

            def shared_pair(pair, first=False):
                for i in range(2):
                    j = pair * 2 + i
                    act.wait_ge(s["sh_gu_made"], j + 1)
                    at_least(act, s["sh_mult"], j - 1)
                    nc.scalar.activation(sh_s[:, i, :], ps[:, 0, 0:MS], ACT.Silu)
                    nc.scalar.copy(sh_u[:, i, :], ps[:, 1, 0:MS]).then_inc(s["sh_silu"], 1)
                    if not first:
                        move_shared(j - 2, i)
                    if i == 1 or not first:
                        move_hidden(j - 1, (i + 1) % 2)
            shared_pair(0, first=True)
            with act.Fori(1, TILES // 2 - 1) as pair:
                shared_pair(pair)
            shared_pair(TILES // 2 - 1)
            act.wait_ge(s["overT_made"], 1)
            nc.scalar.copy(w_overT[:, :], ps[0:E, 6:8, :].rearrange("p a n -> p (a n)")).then_inc(s["overT_moved"], 1)
            move_shared(TILES - 2, 0)
            move_hidden(TILES - 1, 1)
            move_shared(TILES - 1, 1)

            def silu(e, i):
                act.wait_ge(s["gu_made"], e + 1)
                at_least(act, s["he_ready"], e - 1)
                nc.scalar.activation(he_a[:, i % 2, :], ps[0:CAP, i % 2, 0:M], ACT.Silu).then_inc(s["silu_done"], 1)

            def move_heT(e, i):
                act.wait_ge(s["heT_made"], e + 1)
                at_least(act, s["oe_made"], e - 1)
                nc.scalar.copy(heT[:, i % 2, :, :], ps[0:MHP, 3, 0:2 * CAP].rearrange("p (k n) -> p k n", k=2)).then_inc(s["heT_moved"], 1)

            def move_oe(e, turn, i):
                act.wait_ge(s["oe_made"], e + 1)
                if not isinstance(turn, int) or turn > 0:
                    act.wait_ge(scattered[i], turn * 16)
                nc.scalar.copy(dst_now[:, i:i + 1], col(dst_f, e))
                nc.scalar.mul(oe[:, i, :], ps[0:CAP, 4 + i % 2, 0:D], col(w_slot, e)).then_inc(s["oe_moved"], 1)

            silu(0, 0)
            silu(1, 1)
            move_heT(0, 0)

            def turn(r, last=False):
                for i in range(RING):
                    e = r * RING + i
                    if not last or i < RING - 2:
                        silu(e + 2, i)
                    if not last or i < RING - 1:
                        move_heT(e + 1, i + 1)
                    move_oe(e, r, i)
            turn(0)
            with act.Fori(1, TURNS - 1) as r:
                turn(r)
            turn(TURNS - 1, True)

        @block.vector
        def _(dve):
            chain = Chain(dve, s["dve_step"])
            link = chain.link

            def flat(t):
                return t[:, :, :].rearrange("p a n -> p (a n)")

            def row_stats(tiles, loading=False):
                for j in tiles:
                    if loading:
                        dve.wait_ge(x_loaded[j], 16)
                    ins = nc.vector.bn_stats(stats[:, j, :], x_s[:, j, :])
                link(ins)
                for j in tiles:
                    ins = nc.vector.bn_aggr(mv[:, j, :], stats[:, j, :])
                ins.then_inc(s["var_ready"], 1)

            def invert_deviations(n, tiles):
                dve.wait_ge(s["var_ready"], n)
                dve.wait_ge(s["std_ready"], n)
                r = slice(tiles[0], tiles[-1] + 1)
                link(nc.vector.reciprocal(rstd[:, r], std[:, r]))

            def normalise(tiles):
                for j in tiles:
                    nc.vector.tensor_scalar(xn_s[:, j, :], x_s[:, j, :], mv[:, j, 0:1], rstd[:, j:j + 1],
                                            ALU.subtract, ALU.mult).then_inc(s["xn_ready"], 1)

            halves = range(TILES // 2), range(TILES // 2, TILES)
            for tiles in halves:
                row_stats(tiles, loading=True)
            for n, tiles in enumerate(halves):
                invert_deviations(n + 1, tiles)
                normalise(tiles)
            for c in range(TILES // 2):
                dve.wait_ge(s["xT_moved"], c + 1)
                cols = slice(2 * c * P, (2 * c + 2) * P)
                nc.vector.tensor_tensor(xT_lo[:, :, cols].rearrange("p k (i n) -> p k i n", i=2),
                                        ps[:, XT + c, :].rearrange("p (i k n) -> p k i n", i=2, k=KT),
                                        xT_hi[:, :, cols].bitcast(F32).rearrange("p k (i n) -> p k i n", i=2),
                                        ALU.subtract).then_inc(s["xT_lo_ready"], 1)
            dve.wait_ge(s["bo_spread"], 1)
            dve.wait_ge(s["xn_ready"], TILES)
            nc.vector.tensor_tensor(x_s[:, :, :], x_s[:, :, :],
                                    ps[:, KV + 1, 0:D].rearrange("p (a n) -> p a n", a=1).broadcast_to([P, TILES, D]),
                                    ALU.add).then_inc(s["bo_added"], 1)
            dve.wait_ge(s["bo_added"], 1)

            def lay_kv(N):
                dve.wait_ge(s["kv_made"], N + 1)
                at_least(dve, s["heads_made"], N * TB)
                kv = ps[:, KV:KV + 2, :].rearrange("p a (c n) -> p (a c) n", c=2)
                for h in range(2):
                    r = slice(h * HEAD, (h + 1) * HEAD)
                    ins = nc.vector.tensor_copy(kv_s[r, :, h, :], kv[r, :, h * (HEAD + 1):(h + 1) * (HEAD + 1)])
                ins.then_inc(s["kv_laid"], 1)

            def norm_heads(N, t):
                n = N * TB + t
                dve.wait_ge(s["heads_made"], n + 1)
                at_least(dve, s["heads_normed"], n)
                ho = ps[:, HO:HO + 2, 0:PAIRS * (HEAD + 1)].rearrange("p c (h n) -> p c h n", h=PAIRS)
                inverse = rn[:, :].rearrange("p (c h a) -> p c h a", c=2, a=1)
                nc.vector.reciprocal(inverse, ho[:, :, :, HEAD:HEAD + 1]).then_inc(s["rn_ready"], 1)
                dve.wait_ge(s["rn_ready"], n + 1)
                at_least(dve, s["aT_made"], n - TB + 1)
                for c in range(2):
                    ins = nc.vector.scalar_tensor_tensor(out=a_s[:, t, c * PAIRS:(c + 1) * PAIRS, :],
                                                         in0=inverse[:, c].broadcast_to([P, PAIRS, HEAD]), scalar=1.0 / FLOOR,
                                                         in1=ho[:, c, :, 0:HEAD], op0=ALU.min, op1=ALU.mult)
                ins.then_inc(s["heads_normed"], 1)

            def low_heads(N, t):
                dve.wait_ge(s["aT_hi_ready"], N * TB + t + 1)
                cols = slice(t * P, (t + 1) * P)
                nc.vector.tensor_tensor(aT_lo[:, :, cols], ps[:, AT, :].rearrange("p (a n) -> p a n", a=PAIRS),
                                        aT_hi[:, :, cols].bitcast(F32), ALU.subtract).then_inc(s["aT_lo_ready"], 1)

            def add_attention(N, b):
                dve.wait_ge(s["attn_made"], (N + 1) * TB)
                xs = x_s[:, 2 * b:2 * b + 2, :].rearrange("p a n -> p (a n)")
                at_least(dve, s["attn_added"], N)
                nc.vector.tensor_tensor(xs, xs, ps[:, AO, :], ALU.add).then_inc(s["attn_added"], 1)

            def finish(N, b, lay_next):
                for t in range(TB):
                    norm_heads(N, t)
                for t in range(TB):
                    low_heads(N, t)
                if lay_next:
                    lay_kv(N + 1)
                add_attention(N, b)

            def attend(g, first=False):
                if not first:
                    finish(g * B - 1, B - 1, False)
                lay_kv(g * B)
                for b in range(B - 1):
                    finish(g * B + b, b, True)
            attend(0, first=True)
            with dve.Fori(1, GROUPS) as g:
                attend(g)
            done, rest = range(TILES - TB), range(TILES - TB, TILES)
            for t in range(TB):
                norm_heads(GROUPS * B - 1, t)
            for t in range(TB):
                low_heads(GROUPS * B - 1, t)
            dve.wait_ge(s["attn_added"], GROUPS * B - 1)
            row_stats(done)
            invert_deviations(3, done)
            normalise(done[0:TB])
            add_attention(GROUPS * B - 1, B - 1)
            dve.wait_ge(s["attn_added"], GROUPS * B)
            row_stats(rest)
            normalise(done[TB:])
            invert_deviations(4, rest)
            normalise(rest)

            def add_cross(b, half):
                dve.wait_ge(s["av_made"], b * XH + 4 * half + 4)
                xs = one(x_s, b * 2 + half)
                nc.vector.tensor_tensor(xs, xs, ps[:, AV[half], 0:D], ALU.add).then_inc(s["av_added"], 1)

            def low_queries(b, pair):
                dve.wait_ge(s["q_hi_ready"], b * 4 + pair + 1)
                r, half, heads = slice(2 * XD, 3 * XD), pair // 2, slice(pair % 2 * 2, pair % 2 * 2 + 2)
                nc.vector.tensor_tensor(q_st[r, half, heads, :], q_raw[r, half, heads, :],
                                        q_st[r, half, heads, :].bitcast(F32), ALU.subtract).then_inc(s["q_lo_ready"], 1)

            def invert_sums(n, h):
                dve.wait_ge(s["exp_done"], n + 1)
                nc.vector.reciprocal(prs[:, h % PRING, :], psm[:, h % PRING, :]).then_inc(s["rcp_done"], 1)

            def move_pT(n, h):
                dve.wait_ge(s["t_made"], n + 1)
                at_least(dve, s["av_made"], n - 1)
                nc.vector.tensor_copy(pT_s[:, h % 2, :, :].rearrange("p a n -> p (a n)"), ps[:, PT, :]).then_inc(s["pT_moved"], 1)

            def cross(b, first=False, last=False):
                for h in range(XH):
                    n = b * XH + h
                    dve.wait_ge(s["s_made"], n + 1)
                    at_least(dve, s["max_ready"], n - PRING + 1)
                    link(nc.vector.tensor_reduce(mx[:, h % PRING, :], ps[:, SB[h % 4], :].rearrange(
                        "p (a n) -> p a n", a=2), AX.X, ALU.max))
                    at_least(dve, s["exp_done"], n - PRING + 1)
                    nc.vector.tensor_scalar(nmx[:, h % PRING, :], mx[:, h % PRING, :], -XSCALE, None,
                                            ALU.mult).then_inc(s["max_ready"], 1)
                    if (h - LAG) % 2 == 1 and (h >= LAG or not first):
                        move_pT(n - LAG, h - LAG)
                    if h in (2, 6) and not first:
                        add_cross(b - 1, h // 4)
                    if h >= 1 or not first:
                        invert_sums(n - 1, h - 1)
                    if h == 1:
                        low_queries(b, 3)
                    elif h % 2 == 1 and not last:
                        low_queries(b + 1, h // 2 - 1)
            before = chain.n
            for pair in range(3):
                low_queries(0, pair)
            cross(0, first=True)
            with dve.Fori(1, B - 1) as b:
                chain.enter(b, 1, chain.n - before)
                cross(b)
            chain.leave(B - 2)
            cross(B - 1, last=True)
            invert_sums(B * XH - 1, XH - 1)
            done, rest = range(TILES - TB), range(TILES - TB, TILES)
            dve.wait_ge(s["av_added"], 2 * (B - 1))
            row_stats(done)
            for h in range(XH - LAG, XH):
                if h % 2 == 1:
                    move_pT((B - 1) * XH + h, h)
            for b in range(B):
                dve.wait_ge(q_stored[b], 16)
            for half in range(2):
                add_cross(B - 1, half)
            dve.wait_ge(s["av_added"], 2 * B)
            row_stats(rest)
            invert_deviations(5, done)
            normalise(done)
            invert_deviations(6, rest)
            normalise(rest)

            dve.wait_ge(s["logits_made"], 1)
            lp = ps[:, 4, :].rearrange("p (j e) -> p j e", j=TILES)
            wide = [P, TILES, E]

            def spread(t):
                return t.rearrange("p (j a) -> p j a", a=1).broadcast_to(wide)

            link(nc.vector.tensor_reduce(tmx[:, :], lp, AX.X, ALU.max))
            nc.vector.tensor_tensor(lg[:, :, :], lp, spread(tmx[:, :]), ALU.subtract).then_inc(s["lg_ready"], 1)
            dve.wait_ge(s["lg_exped"], 1)
            link(nc.vector.tensor_reduce(tmx[:, :], sc[:, :, :], AX.X, ALU.add))
            link(nc.vector.reciprocal(tmx[:, :], tmx[:, :]))
            link(nc.vector.tensor_tensor(sc[:, :, :], sc[:, :, :], spread(tmx[:, :]), ALU.mult))
            link(nc.vector.tensor_reduce(flat(gsc), flat(sc).rearrange("p (c n) -> p c n", n=E // NG), AX.X, ALU.max))
            for j in range(TILES):
                ins = nc.vector.max(g8[:, j, :], gsc[:, j, :])
            link(ins)
            for j in range(TILES):
                ins = nc.vector.max_index(gi8[:, j, :], g8[:, j, :], gsc[:, j, :])
            link(ins)
            link(nc.vector.tensor_copy(gif[:, :, :], gi8[:, :, :]))
            groups = iota_e[:, 0:NG].rearrange("p (a n) -> p a n", a=1).broadcast_to([P, TILES, NG])
            dve.wait_ge(s["consts"], 17)
            for n in range(TOPG):
                chosen = gif[:, :, n:n + 1].broadcast_to([P, TILES, NG])
                link(nc.vector.tensor_tensor((gt if n else gm)[:, :, :], groups, chosen, ALU.is_equal))
                if n:
                    link(nc.vector.tensor_tensor(gm[:, :, :], gm[:, :, :], gt[:, :, :], ALU.add))
            link(nc.vector.tensor_tensor(flat(tmp).rearrange("p (c n) -> p c n", n=E // NG),
                                         flat(sc).rearrange("p (c n) -> p c n", n=E // NG),
                                         flat(gm).rearrange("p (c a) -> p c a", a=1).broadcast_to([P, TILES * NG, E // NG]),
                                         ALU.mult))
            for j in range(TILES):
                ins = nc.vector.max(v8[:, j, :], tmp[:, j, :])
            link(ins)
            for j in range(TILES):
                ins = nc.vector.max_index(i8[:, j, :], v8[:, j, :], tmp[:, j, :])
            link(ins)
            link(nc.vector.tensor_copy(i8f[:, :, :], i8[:, :, :]))
            experts = iota_e[:, :].rearrange("p (a n) -> p a n", a=1).broadcast_to(wide)
            for n in range(TOPK):
                chosen = i8f[:, :, n:n + 1].broadcast_to(wide)
                if n == 0:
                    link(nc.vector.tensor_tensor(rank1[:, :, :], experts, chosen, ALU.is_equal))
                    continue
                link(nc.vector.tensor_tensor(oh[:, :, :], experts, chosen, ALU.is_equal))
                link(nc.vector.scalar_tensor_tensor(out=rank1[:, :, :], in0=oh[:, :, :], scalar=float(n + 1),
                                                    in1=rank1[:, :, :], op0=ALU.mult, op1=ALU.add))
            nc.vector.tensor_scalar(mask_b[:, :, :], rank1[:, :, :], 0.0, None, ALU.is_gt).then_inc(s["mask_ready"], 1)
            link(nc.vector.tensor_scalar(mask[:, :, :], rank1[:, :, :], 0.0, None, ALU.is_gt))
            link(nc.vector.tensor_tensor(w_te[:, :, :], tmp[:, :, :], mask[:, :, :], ALU.mult))
            nc.vector.tensor_copy(vals[:, :, 0:E, 2], rank1[:, :, :])
            link(nc.vector.tensor_copy(vals[:, :, 0:E, 3], w_te[:, :, :]))
            link(nc.vector.tensor_tensor(ra[:, :, :], w_te[:, :, :], vals[:, :, 0:E, 3], ALU.subtract))
            link(nc.vector.tensor_copy(vals[:, :, 0:E, 4], ra[:, :, :]))
            link(nc.vector.tensor_tensor(ra[:, :, :], ra[:, :, :], vals[:, :, 0:E, 4], ALU.subtract))
            nc.vector.tensor_copy(vals[:, :, 0:E, 5], ra[:, :, :]).then_inc(s["vals_ready"], 1)
            dve.wait_ge(s["pos_made"], 1)
            link(nc.vector.tensor_scalar(cnt1[:, :], ps[:, 6, 0:E], -1.0, None, ALU.add))
            link(nc.vector.tensor_copy(flat(pos), ps[:, 5, :]))
            last_one = cnt1[:, :].rearrange("p (a n) -> p a n", a=1).broadcast_to(wide)
            link(nc.vector.tensor_tensor(ra[:, :, :], pos[:, :, :], last_one, ALU.is_equal))
            link(nc.vector.scalar_tensor_tensor(out=rb[:, :, :], in0=pos[:, :, :], scalar=float(CAP - 1), in1=ra[:, :, :],
                                                op0=ALU.is_lt, op1=ALU.max))
            link(nc.vector.tensor_tensor(rb[:, :, :], rb[:, :, :], mask[:, :, :], ALU.mult))
            link(nc.vector.tensor_scalar(ra[:, :, :], pos[:, :, :], float(CAP - 1), 1.0, ALU.min, ALU.add))
            link(nc.vector.tensor_tensor(ra[:, :, :], ra[:, :, :], rb[:, :, :], ALU.mult))
            link(nc.vector.tensor_scalar(slot_of[:, :, 0:E], ra[:, :, :], -1.0, None, ALU.add))
            nc.vector.scalar_tensor_tensor(out=w_over[:, :, :], in0=pos[:, :, :], scalar=float(CAP - 1),
                                           in1=w_te[:, :, :], op0=ALU.is_ge, op1=ALU.mult).then_inc(s["over_ready"], 1)

            def one_hot(e, i):
                at_least(dve, s["tab_made"], e - RING // 2 + 1)
                own = (vals[:, :, e:e + 1, :] if isinstance(e, int) else vals[:, :, bass.ds(e, 1), :])
                nc.vector.tensor_copy(vals_now[:, i % (RING // 2), :, 0:VALS], own.rearrange("p j a n -> p j (a n)"))
                slots = (slot_of[:, :, e:e + 1] if isinstance(e, int) else slot_of[:, :, bass.ds(e, 1)])
                nc.vector.tensor_tensor(ohs[:, i % RING, :, :], slots.broadcast_to([P, TILES, CAP]),
                                        iota_c[:, :].rearrange("p (a n) -> p a n", a=1).broadcast_to([P, TILES, CAP]),
                                        ALU.is_equal).then_inc(s["oh_ready"], 1)

            def tables(e, i):
                dve.wait_ge(s["tab_made"], e + 2)
                two = slice(e, e + 2) if isinstance(e, int) else bass.ds(e, 2)
                link(nc.vector.tensor_copy(tab[:, :, :], ps[0:CAP, TAB[i // 2 % 2], 0:2 * CAP].rearrange(
                    "p (a n) -> p a n", a=2)[:, :, 0:VALS]))
                link(nc.vector.tensor_tensor(src_now[:, i:i + 2], tab[:, :, 0], tab[:, :, 1], ALU.add))
                link(nc.vector.tensor_reduce(w_sum[:, :], tab[:, :, 3:6], AX.X, ALU.add))
                nc.vector.tensor_scalar(w_slot[:, two], w_sum[:, :], slot_is_own[:, 0:1], slot_is_last[:, 0:1],
                                        ALU.mult, ALU.add)
                link(nc.vector.scalar_tensor_tensor(out=row_of[:, :], in0=src_now[:, i:i + 2], scalar=float(TOPK),
                                                    in1=tab[:, :, 2], op0=ALU.mult, op1=ALU.add))
                nc.vector.scalar_tensor_tensor(out=dst_f[:, two], in0=row_of[:, :], scalar=slot_is_own[:, 0:1],
                                               in1=dst_base[:, two], op0=ALU.mult, op1=ALU.add).then_inc(s["tab_moved"], 1)

            def move_xeT(e, i, wait_used=False):
                dve.wait_ge(s["xeT_made"], e + 1)
                if wait_used:
                    at_least(dve, s["gu_made"], e - 1)
                nc.vector.tensor_copy(xeT[:, i % 2, :, :].rearrange("p k n -> p (k n)"),
                                      ps[:, 2, 0:KT * CAP]).then_inc(s["xeT_moved"], 1)

            def mult(e, i):
                dve.wait_ge(s["silu_done"], e + 1)
                at_least(dve, s["heT_made"], e - 1)
                nc.vector.tensor_tensor(he[:, i % 2, :, 0:MH], he_a[:, i % 2, :].rearrange("p (k n) -> p k n", k=2),
                                        ps[0:CAP, i % 2, M:2 * M].rearrange("p (k n) -> p k n", k=2),
                                        ALU.mult).then_inc(s["he_ready"], 1)

            dve.wait_ge(s["dve_step"], chain.n)

            def next_tables(first, end):
                for e in range(first, end, 2):
                    one_hot(e + 1, e + 1)
                    one_hot(e + 2, e + 2)
                    tables(e, e)
            for e in range(RING // 2):
                one_hot(e, e)
            tables(0, 0)
            one_hot(RING // 2, RING // 2)
            tables(2, 2)
            move_xeT(0, 0)
            move_xeT(1, 1)
            mult(0, 0)
            next_tables(RING // 2, RING // 2 + 2)
            move_xeT(2, 0, True)
            mult(1, 1)
            next_tables(RING // 2 + 2, RING)

            def turn(r, last=False):
                for i in range(RING):
                    e = r * RING + i
                    if not last or i < RING - 3:
                        move_xeT(e + 3, i + 3)
                    if not last or i < RING - 2:
                        mult(e + 2, i)
                    if not last:
                        if i % 2 == 1:
                            tables(e + RING - 1, i - 1)
                        one_hot(e + RING + 1, i + 1)
            before = chain.n
            turn(0)
            with dve.Fori(1, TURNS - 1) as r:
                chain.enter(r, 1, chain.n - before)
                turn(r)
            chain.leave(TURNS - 2)
            turn(TURNS - 1, True)

            dve.wait_ge(s["sh_added"], TILES)
            for j in range(TILES):
                if j % 2 == 0:
                    dve.wait_ge(s["over_made"], j // 2 + 1)
                    xs = x_s[:, j:j + 2, :].rearrange("p a n -> p (a n)")
                    link(nc.vector.tensor_tensor(xs, xs, ps[:, j // 2, :], ALU.add))
                dve.wait_ge(y_loaded[j % YRING], 16 * (j // YRING + 1))
                link(nc.vector.tensor_reduce(ysum[:, j % 2, :], y_t[j % YRING][:, :].rearrange("p (k n) -> p n k", k=TOPK),
                                             AX.X, ALU.add))
                nc.vector.tensor_tensor(x_s[:, j, :], x_s[:, j, :], ysum[:, j % 2, :], ALU.add).then_inc(s["out_ready"], 1)

        @block.tensor
        def _(pe):
            def transpose_rows(rows, ready):
                for c in rows:
                    pe.wait_ge(s["xn_ready"], ready + 2 * c + 2)
                    for i in range(2):
                        for k in range(KT):
                            q = i * KT + k
                            ins = pe.transpose(ps[:, XT + c, q * P:(q + 1) * P], xn_s[:, 2 * c + i, k * P:(k + 1) * P], ident[:, :])
                    ins.then_inc(s["xT_made"], 1)

            pe.wait_ge(s["consts"], 5)
            pe.wait_ge(s["bo_loaded"], 16)
            pe.matmul(ps[:, KV + 1, 0:D], ones_row[:, :], bo_row[:, :], start=True, stop=True).then_inc(s["bo_spread"], 1)
            transpose_rows(range(TILES // 4), 0)
            pe.wait_ge(s["xT_lo_ready"], TILES // 4)

            def exact(bank, pairs):
                n = 0
                for (l_hi, l_lo), (r_hi, r_lo) in pairs:
                    for lhsT, rhs in ((l_hi, r_hi), (l_hi, r_lo), (l_lo, r_hi)):
                        ins = pe.matmul(bank, lhsT, rhs, start=(n == 0), stop=(n == 3 * len(pairs) - 1))
                        n += 1
                return ins

            def parts(hi, lo, *at):
                return hi[at], lo[at]

            def project(g, n):
                what, b, t = PROJ[n]
                at_least(pe, s["proj_moved"], g * NPROJ + n - 1)
                for part, at in ((WQ, 0), (WK, NQ), (WV, NQ + TB)):
                    if n == at:
                        pe.wait_ge(s["w_lo_ready"], w_split(g, part))
                pairs = []
                for k in range(KT):
                    if what == "q":
                        lhsT = parts(w_hi, w_lo, ALL, WQ, slice(k * GROUP + t * P, k * GROUP + (t + 1) * P))
                        rhs = parts(xT_hi, xT_lo, ALL, k, slice(b * GROUP, (b + 1) * GROUP))
                    else:
                        lhsT = parts(xT_hi, xT_lo, ALL, k, slice((TB * b + t) * P, (TB * b + t + 1) * P))
                        rhs = parts(w_hi, w_lo, ALL, WK if what == "k" else WV, slice(k * GROUP, (k + 1) * GROUP))
                    pairs.append((lhsT, rhs))
                exact(ps[:, PJ[n % 2], :], pairs).then_inc(s["projected"], 1)

            def keys_values(g, b):
                pe.wait_ge(s["proj_moved"], g * NPROJ + NQ + (b + 1) * 2 * TB)
                at_least(pe, s["kv_laid"], g * B + b)
                for p in range(PAIRS):
                    for t in range(TB):
                        ins = pe.matmul(ps[:, KV + p // 2, (p % 2) * D:(p % 2) * D + 2 * (HEAD + 1)],
                                        k_s[:, t, p * P:(p + 1) * P], v_s[:, t, 2 * p:2 * p + 2, :].rearrange("p a n -> p (a n)"),
                                        start=(t == 0), stop=(t == TB - 1))
                ins.then_inc(s["kv_made"], 1)

            def heads(N, b, t):
                if t == 0:
                    pe.wait_ge(s["kv_laid"], N + 1)
                at_least(pe, s["heads_normed"], N * TB + t)
                for p in range(PAIRS):
                    w = 2 * (HEAD + 1)
                    ins = pe.matmul(ps[:, HO + p // 2, (p % 2) * w:(p % 2 + 1) * w], qT[:, p, (b * TB + t) * P:(b * TB + t + 1) * P],
                                    kv_s[:, p, :, :].rearrange("p a n -> p (a n)"), start=True, stop=True)
                ins.then_inc(s["heads_made"], 1)

            def transpose_heads(N, t):
                pe.wait_ge(s["heads_normed"], N * TB + t + 1)
                at_least(pe, s["aT_lo_ready"], N * TB + t)
                for p in range(PAIRS):
                    ins = pe.transpose(ps[:, AT, p * P:(p + 1) * P], a_s[:, t, 2 * p:2 * p + 2, :].rearrange("p a n -> p (a n)"),
                                       ident[:, :])
                ins.then_inc(s["aT_made"], 1)

            def attention_out(g, N, b, t):
                pe.wait_ge(s["aT_lo_ready"], N * TB + t + 1)
                if t == 0:
                    at_least(pe, s["attn_added"], N)
                    if b == 0:
                        pe.wait_ge(s["w_lo_ready"], w_split(g, WO))
                exact(ps[:, AO, t * D:(t + 1) * D],
                      [(parts(aT_hi, aT_lo, ALL, p, slice(t * P, (t + 1) * P)),
                        parts(w_hi, w_lo, ALL, WO, slice(p * D, (p + 1) * D))) for p in range(PAIRS)]).then_inc(s["attn_made"], 1)

            def attend(g, first=False):
                N, b = g * B - 1, B - 1
                for n in range(NQ):
                    if first and n == 2:
                        transpose_rows(range(TILES // 4, TILES // 2), 0)
                    if first and n == PAIRS:
                        pe.wait_ge(s["xT_lo_ready"], TILES // 2)
                    project(g, n)
                    if not first:
                        if n < TB:
                            heads(N, b, n)
                        elif n < 2 * TB:
                            transpose_heads(N, n - TB)
                        elif n < 3 * TB:
                            attention_out(g, N, b, n - 2 * TB)
                for n in range(NQ, NQ + 2 * TB):
                    project(g, n)
                if first:
                    pe.wait_ge(s["bo_added"], 1)
                keys_values(g, 0)
                for b in range(B - 1):
                    N = g * B + b
                    at = NQ + (b + 1) * 2 * TB
                    for t in range(TB):
                        project(g, at + t)
                        heads(N, b, t)
                    for t in range(TB):
                        project(g, at + TB + t)
                        transpose_heads(N, t)
                    attention_out(g, N, b, 0)
                    keys_values(g, b + 1)
                    attention_out(g, N, b, 1)
            attend(0, first=True)
            with pe.Fori(1, GROUPS) as g:
                attend(g)
            for t in range(TB):
                heads(GROUPS * B - 1, B - 1, t)
            for t in range(TB):
                transpose_heads(GROUPS * B - 1, t)
            for t in range(TB):
                attention_out(GROUPS - 1, GROUPS * B - 1, B - 1, t)
            pe.wait_ge(s["attn_added"], GROUPS * B)
            pe.wait_ge(s["proj_moved"], GROUPS * NPROJ)

            def values(b):
                pe.wait_ge(s["ctx_loaded"], b * 16 + 16)
                at_least(pe, s["vT_moved"], b)
                for n in range(2):
                    for k in range(KT):
                        q = n * KT + k
                        ins = pe.transpose(ps[:, VT, q * P:(q + 1) * P], ctx_b[:, k, n * P:(n + 1) * P], ident[:, :])
                ins.then_inc(s["vT_made"], 1)

            def scores(b, n, h):
                half, j = h // 4, h % 4
                if j % 2 == 0:
                    pe.wait_ge(s["k_lo_ready"], (b * 2 + half) * 2 + j // 2 + 1)
                    pe.wait_ge(s["q_lo_ready"], (b * 2 + half) * 2 + j // 2 + 1)
                at_least(pe, s["exp_done"], n - 3)
                for m in range(2):
                    ins = pe.matmul(ps[:, SB[j], m * D:(m + 1) * D], q_st[:, half, j, m * P:(m + 1) * P],
                                    k_st[:, half, j, :], start=True, stop=True)
                ins.then_inc(s["s_made"], 1)

            def transpose_probs(n, h):
                pe.wait_ge(s["p_normed"], n + 1)
                at_least(pe, s["pT_moved"], n)
                for k in range(2):
                    for m in range(2):
                        q = k * 2 + m
                        ins = pe.transpose(ps[:, PT, q * P:(q + 1) * P], p_s[:, h % PRING, m, k * P:(k + 1) * P], ident[:, :])
                ins.then_inc(s["t_made"], 1)

            def weigh_values(b, n, h, carried=False):
                pe.wait_ge(s["pT_moved"], n + 1)
                if h == 0:
                    pe.wait_ge(s["vT_moved"], b + 1)
                if h % 4 == 0 and not carried:
                    at_least(pe, s["av_added"], b * 2 + h // 4 - 1)
                r = slice(h % 4 * QUAD, h % 4 * QUAD + QUAD)
                for k in range(2):
                    ins = pe.matmul(ps[r, AV[h // 4], 0:D], vT_s[:, k, h * XD:(h + 1) * XD], pT_s[:, h % 2, k, :],
                                    start=(k == 0), stop=(k == 1))
                ins.then_inc(s["av_made"], 1)

            def cross(b, first=False):
                values(b)
                for h in range(XH):
                    n = b * XH + h
                    scores(b, n, h)
                    if h >= LAG or not first:
                        transpose_probs(n - LAG, (h - LAG) % XH)
                    if h >= LAG + 1 or not first:
                        weigh_values(b if h >= LAG + 1 else b - 1, n - LAG - 1, (h - LAG - 1) % XH, h < LAG + 1)
            cross(0, first=True)
            with pe.Fori(1, B) as b:
                cross(b)
            for h in range(XH - LAG, XH + 1):
                if h < XH:
                    transpose_probs((B - 1) * XH + h, h)
                weigh_values(B - 1, (B - 1) * XH + h - 1, h - 1)
            pe.wait_ge(s["av_added"], 2 * B)

            transpose_rows(range(TILES // 2), 2 * TILES)
            pe.wait_ge(s["xT_moved"], TILES)
            pe.wait_ge(s["gate_loaded"], 16)
            for j in range(TILES):
                for k in range(KT):
                    ins = pe.matmul(ps[:, 4, j * E:(j + 1) * E], xnT[:, k, j * P:(j + 1) * P], gate_s[:, k, :],
                                    start=(k == 0), stop=(k == KT - 1))
            ins.then_inc(s["logits_made"], 1)

            def shared_gate_up(j, i):
                pe.wait_ge(s["hT_staged"], j + 1)
                at_least(pe, s["sh_silu"], j)
                for half in range(2):
                    for k in range(KT):
                        ins = pe.matmul(ps[:, half, 0:MS], hT_j[:, i, k, :], sgu_s[:, k, half * MS:(half + 1) * MS],
                                        start=(k == 0), stop=(k == KT - 1))
                ins.then_inc(s["sh_gu_made"], 1)

            def shared_hidden(j, i):
                pe.wait_ge(s["sh_mult"], j + 1)
                at_least(pe, s["shT_moved"], j)
                for k in range(MSP):
                    ins = pe.transpose(ps[0:MHP, 2, k * P:(k + 1) * P], sh_h[:, i, k, :], ident[:, :])
                ins.then_inc(s["shT_made"], 1)

            def shared_down(j, i):
                pe.wait_ge(s["shT_moved"], j + 1)
                for k in range(MSP):
                    ins = pe.matmul(ps[:, 3, 0:D], sh_T[:, i, k, :], sd_s[:, k, :], start=(k == 0), stop=(k == MSP - 1))
                ins.then_inc(s["sh_made"], 1)

            def shared_pair(pair, first=False):
                for i in range(2):
                    j = pair * 2 + i
                    shared_gate_up(j, i)
                    if i == 1 or not first:
                        shared_hidden(j - 1, (i + 1) % 2)
                    if not first:
                        shared_down(j - 2, i)
            pe.wait_ge(s["sgu_loaded"], 16)
            pe.wait_ge(s["sd_loaded"], 16)
            shared_pair(0, first=True)
            with pe.Fori(1, TILES // 2 - 1) as pair:
                shared_pair(pair)

            pe.wait_ge(s["mask_ready"], 1)
            pe.wait_ge(s["consts"], 17)
            for j in range(TILES):
                for i in range(j + 1):
                    pe.matmul(ps[:, 5, j * E:(j + 1) * E], (before_b if i == j else ones_b)[:, :], mask_b[:, i, :],
                              start=(i == 0), stop=(i == j))
            for i in range(TILES):
                ins = pe.matmul(ps[:, 6, 0:E], ones_b[:, :], mask_b[:, i, :], start=(i == 0), stop=(i == TILES - 1))
            ins.then_inc(s["pos_made"], 1)

            shared_pair(TILES // 2 - 1)
            pe.wait_ge(s["over_ready"], 1)
            for j in range(TILES):
                ins = pe.transpose(ps[0:E, 6 + j // 4, (j % 4) * P:(j % 4 + 1) * P], w_over[:, j, :], ident[:, :])
            ins.then_inc(s["overT_made"], 1)

            def table(e, i):
                pe.wait_ge(s["oh_ready"], e + 1)
                for j in range(TILES):
                    q = i % 2 * CAP
                    ins = pe.matmul(ps[0:CAP, TAB[i // 2 % 2], q:q + CAP], ohs[:, i % RING, j, :],
                                    vals_now[:, i % (RING // 2), j, :], start=(j == 0), stop=(j == TILES - 1))
                ins.then_inc(s["tab_made"], 1)

            def transpose_tokens(e, turn, i, first=False):
                pe.wait_ge(gathered[i % RING], turn * 16 + 16)
                if first:
                    at_least(pe, s["xeT_moved"], e)
                for k in range(KT):
                    ins = pe.transpose(ps[:, 2, k * CAP:(k + 1) * CAP], xe[:, i % RING, k * P:(k + 1) * P], ident[0:CAP, 0:CAP])
                    if k == KT - 1:
                        ins.then_inc(s["xeT_made"], 1)

            def gate_up(e, turn, i):
                pe.wait_ge(wgu_loaded[i % RING], turn * 16 + 16)
                pe.wait_ge(s["xeT_moved"], e + 1)
                for k in range(KT):
                    ins = pe.matmul(ps[0:CAP, i % 2, 0:2 * M], xeT[:, i % 2, k, :], wgu_s[:, i % RING, k * 2 * M:(k + 1) * 2 * M],
                                    start=(k == 0), stop=(k == KT - 1))
                    if k == KT - 1:
                        ins.then_inc(s["gu_made"], 1)

            def transpose_hidden(e, i):
                pe.wait_ge(s["he_ready"], e + 1)
                at_least(pe, s["heT_moved"], e)
                for k in range(2):
                    ins = pe.transpose(ps[0:MHP, 3, k * CAP:(k + 1) * CAP], he[:, i % 2, k, :], ident[0:CAP, 0:CAP])
                    if k == 1:
                        ins.then_inc(s["heT_made"], 1)

            def down(e, turn, i, last=False):
                pe.wait_ge(wd_loaded[i % RING], turn * 16 + 16)
                if last:
                    pe.wait_ge(s["heT_moved"], e + 1)
                at_least(pe, s["oe_moved"], e - 1)
                for k in range(2):
                    ins = pe.matmul(ps[0:CAP, 4 + i % 2, 0:D], heT[:, i % 2, k, :], wd_s[:, i % RING, k * D:(k + 1) * D],
                                    start=(k == 0), stop=(k == 1))
                    if k == 1:
                        ins.then_inc(s["oe_made"], 1)

            shared_down(TILES - 2, 0)
            pe.wait_ge(s["overT_moved"], 1)
            for e in range(RING // 2):
                table(e, e)
            shared_hidden(TILES - 1, 1)
            shared_down(TILES - 1, 1)
            pe.wait_ge(s["sh_moved"], TILES)
            transpose_tokens(0, 0, 0)
            transpose_tokens(1, 0, 1, True)
            gate_up(0, 0, 0)
            for e in range(RING // 2, RING // 2 + 2):
                table(e, e)
            transpose_tokens(2, 0, 2, True)
            gate_up(1, 0, 1)
            transpose_hidden(0, 0)
            for e in range(RING // 2 + 2, RING):
                table(e, e)

            def turn(r, last=False):
                for i in range(RING):
                    e = r * RING + i
                    if not last or i < RING - 2:
                        gate_up(e + 2, r + (i + 2) // RING, i + 2)
                    if not last or i < RING - 3:
                        transpose_tokens(e + 3, r + (i + 3) // RING, i + 3)
                    if not last or i < RING - 1:
                        transpose_hidden(e + 1, i + 1)
                    down(e, r, i, last and i == RING - 1)
                    if not last:
                        table(e + RING, i)
            turn(0)
            with pe.Fori(1, TURNS - 1) as r:
                turn(r)
            turn(TURNS - 1, True)

            pe.wait_ge(s["over_loaded"], 16)
            pe.wait_ge(s["oe_moved"], E)
            for c in range(TILES // 2):
                for i in range(2):
                    j = 2 * c + i
                    ins = pe.matmul(ps[:, c, i * D:(i + 1) * D], w_overT[:, j * P:(j + 1) * P], over_s[:, :], start=True, stop=True)
                ins.then_inc(s["over_made"], 1)


def kernel(x, ctx_2048, L0_attn_Wq, L0_attn_Wk, L0_attn_Wv, L0_attn_Wo, L0_attn_bo, L0_ffn_gate_weight,
           L0_ffn_Wg, L0_ffn_Wu, L0_ffn_Wd, L0_ffn_Sg, L0_ffn_Su, L0_ffn_Sd):
    import numpy as np
    import concourse.bacc as bacc
    from concourse.bass_utils import run_bass_kernel_spmd

    def by_rows(w):
        return np.ascontiguousarray(np.asarray(w).T.reshape(KT, P, -1).transpose(1, 0, 2))

    gu = np.concatenate([np.asarray(L0_ffn_Wg), np.asarray(L0_ffn_Wu)], axis=1)
    arrays = {
        "x": np.asarray(x).reshape(T, D),
        "ctx": np.asarray(ctx_2048),
        "wq": np.asarray(L0_attn_Wq),
        "wk": np.asarray(L0_attn_Wk),
        "wv": np.asarray(L0_attn_Wv),
        "wo": np.asarray(L0_attn_Wo),
        "bo": np.asarray(L0_attn_bo).reshape(1, D),
        "gate": by_rows(L0_ffn_gate_weight),
        "wgu": gu.reshape(E, 2 * M, KT, P).transpose(0, 3, 2, 1).reshape(E, P, KT * 2 * M),
        "wd": np.asarray(L0_ffn_Wd).transpose(0, 2, 1).reshape(E, 2, MH, D).transpose(0, 2, 1, 3).reshape(E, MH, 2 * D),
        "sgu": np.concatenate([by_rows(L0_ffn_Sg), by_rows(L0_ffn_Su)], axis=2),
        "sd": np.asarray(L0_ffn_Sd).T.reshape(MSP, MH, D).transpose(1, 0, 2),
    }
    arrays = {f"in_{k}": np.ascontiguousarray(v) for k, v in arrays.items()}
    nc = bacc.Bacc("TRN2", target_bir_lowering=False, num_devices=1)
    args = [nc.dram_tensor(k, v.shape, mybir.dt.from_np(v.dtype), kind="ExternalInput").ap() for k, v in arrays.items()]
    args.append(nc.dram_tensor("out", (T, D), F32, kind="ExternalOutput").ap())
    decoder_layer(nc, *args)
    r = run_bass_kernel_spmd(nc, [arrays], core_ids=[0])
    return r.results[0]["out"].reshape(B, S, D)
```
